# Optimizing a Trainium2 kernel written in Bass

```python
import numpy as np
import jax
import jax.numpy as jnp

def _softmax(x, axis=-1):
    return jax.nn.softmax(x, axis=axis)

def _gelu(x):
    return jax.nn.gelu(x, approximate=True)

def _silu(x):
    return jax.nn.silu(x)

def _sigmoid(x):
    return jax.nn.sigmoid(x)

def _layernorm(x, axis=-1, eps=1e-05):
    m = jnp.mean(x, axis=axis, keepdims=True)
    v = jnp.var(x, axis=axis, keepdims=True)
    return (x - m) / jnp.sqrt(v + eps)

def _scatter_add(tgt, idx, src, axis=0):
    return tgt.at[idx].add(src)

def _segment_sum(src, seg, n):
    return jax.ops.segment_sum(src, seg, n)
kernel_name = 'mk_xattn_ffn_d1_seqx_r4_47affe'

def setup_inputs(seed: int=0):
    np.random.seed(seed)
    _w = jnp.asarray

    def _rec_inputs():
        import jax
        import jax.numpy as jnp
        _rk = jax.random.key(seed)
        x = 0.0001212 + 1 * jax.random.normal(jax.random.fold_in(_rk, 1), (16, 128, 512), jnp.float32)
        _lenS = 128 - jax.random.randint(jax.random.fold_in(_rk, 7), (16,), 0, max(1, 128 // 4) + 1, jnp.int32)
        _lenS2 = 128 - jax.random.randint(jax.random.fold_in(_rk, 8), (16,), 0, max(1, 128 // 4) + 1, jnp.int32)
        _ctx_2048P = jax.random.normal(jax.random.fold_in(_rk, 11), (16, 16, 512), jnp.float32)
        _ctx_2048c = jax.random.dirichlet(jax.random.fold_in(_rk, 511), 0.3 * jnp.ones((16,), jnp.float32), (16, 128))
        _ctx_2048t = jnp.einsum('bsk,bkd->bsd', _ctx_2048c, _ctx_2048P)
        _ctx_2048t = _ctx_2048t * jax.lax.rsqrt(jnp.mean(jnp.square(_ctx_2048t)) + 1e-12) * 0.953939
        ctx_2048 = 0.000173663 + 1.0001 * (_ctx_2048t + 0.3 * jax.random.normal(jax.random.fold_in(_rk, 611), (16, 128, 512), jnp.float32))
        return (x, ctx_2048)
    x, ctx_2048 = _rec_inputs()

    def _L0_xattn_setup():
        import jax, jax.numpy as jnp
        import numpy as np
        B_DIM, T_DIM, C_DIM = (16, 256, 512)

        def _wkv(w, u, k, v):
            Bn, Tn, Cn = k.shape
            NEG_INF = jnp.float32(-1e+38)

            def step(carry, kv_t):
                p, q, o = carry
                kt, vt = kv_t
                no = jnp.maximum(o, u + kt)
                A = jnp.exp(o - no)
                E = jnp.exp(u + kt - no)
                y = (A * p + E * vt) / (A * q + E)
                no2 = jnp.maximum(w + o, kt)
                A2 = jnp.exp(w + o - no2)
                E2 = jnp.exp(kt - no2)
                return ((A2 * p + E2 * vt, A2 * q + E2, no2), y)
            init = (jnp.zeros((Bn, Cn), k.dtype), jnp.zeros((Bn, Cn), k.dtype), jnp.full((Bn, Cn), NEG_INF, k.dtype))
            kT = jnp.moveaxis(k, 1, 0)
            vT = jnp.moveaxis(v, 1, 0)
            _, yT = jax.lax.scan(step, init, (kT, vT))
            return jnp.moveaxis(yT, 0, 1)
        key = jax.random.key(seed)
        k1, k2, k3, k4 = jax.random.split(key, 4)
        w = -jnp.exp(jax.random.normal(k1, (C_DIM,), jnp.float32))
        u = jax.random.normal(k2, (C_DIM,), jnp.float32)
        k = jax.random.normal(k3, (B_DIM, T_DIM, C_DIM), jnp.float32)
        v = jax.random.normal(k4, (B_DIM, T_DIM, C_DIM), jnp.float32)
        return {'B': B_DIM, 'T': T_DIM, 'C': C_DIM, 'w': w, 'u': u, 'k': k, 'v': v}
    _L0_xattn_all = _L0_xattn_setup()
    _L0_xattn_in = {k: v for k, v in _L0_xattn_all.items() if k in ('w', 'u')}
    del _L0_xattn_all

    def _L0_ffn_setup():
        import jax, jax.numpy as jnp
        import numpy as np
        D = 512
        E = 16
        TOP_K = 2
        S_EXP = 2
        H_R = D // E * 4
        H_S = D * 4
        B, S = (4, 512)
        key = jax.random.key(seed)
        ks = jax.random.split(key, 12)
        sc = 0.02
        return {'x': jax.random.normal(ks[0], (B, S, D), jnp.float32), 'gate_w': jax.random.normal(ks[1], (D, E), jnp.float32) * sc, 'gate_b': jnp.zeros((E,), jnp.float32), 'ew1': jax.random.normal(ks[2], (E, D, H_R), jnp.float32) * sc, 'eb1': jnp.zeros((E, H_R), jnp.float32), 'ew2': jax.random.normal(ks[3], (E, H_R, D), jnp.float32) * sc, 'eb2': jnp.zeros((E, D), jnp.float32), 'sw1': jax.random.normal(ks[4], (S_EXP, D, H_S), jnp.float32) * sc, 'sb1': jnp.zeros((S_EXP, H_S), jnp.float32), 'sw2': jax.random.normal(ks[5], (S_EXP, H_S, D), jnp.float32) * sc, 'sb2': jnp.zeros((S_EXP, D), jnp.float32)}
    _L0_ffn_all = _L0_ffn_setup()
    _L0_ffn_in = {k: v for k, v in _L0_ffn_all.items() if k in ('gate_w', 'gate_b', 'ew1', 'eb1', 'ew2', 'eb2', 'sw1', 'sb1', 'sw2', 'sb2')}
    del _L0_ffn_all
    return {'x': x, 'ctx_2048': ctx_2048, 'L0_xattn_w': _L0_xattn_in['w'], 'L0_xattn_u': _L0_xattn_in['u'], 'L0_ffn_gate_w': _L0_ffn_in['gate_w'], 'L0_ffn_gate_b': _L0_ffn_in['gate_b'], 'L0_ffn_ew1': _L0_ffn_in['ew1'], 'L0_ffn_eb1': _L0_ffn_in['eb1'], 'L0_ffn_ew2': _L0_ffn_in['ew2'], 'L0_ffn_eb2': _L0_ffn_in['eb2'], 'L0_ffn_sw1': _L0_ffn_in['sw1'], 'L0_ffn_sb1': _L0_ffn_in['sb1'], 'L0_ffn_sw2': _L0_ffn_in['sw2'], 'L0_ffn_sb2': _L0_ffn_in['sb2']}

def reference(x, ctx_2048, L0_xattn_w, L0_xattn_u, L0_ffn_gate_w, L0_ffn_gate_b, L0_ffn_ew1, L0_ffn_eb1, L0_ffn_ew2, L0_ffn_eb2, L0_ffn_sw1, L0_ffn_sb1, L0_ffn_sw2, L0_ffn_sb2):
    import jax
    import jax.numpy as jnp

    def _L0_xattn_ref(B, T, C, w, u, k, v):
        import jax, jax.numpy as jnp
        import numpy as np
        B_DIM, T_DIM, C_DIM = (16, 256, 512)

        def _wkv(w, u, k, v):
            Bn, Tn, Cn = k.shape
            NEG_INF = jnp.float32(-1e+38)

            def step(carry, kv_t):
                p, q, o = carry
                kt, vt = kv_t
                no = jnp.maximum(o, u + kt)
                A = jnp.exp(o - no)
                E = jnp.exp(u + kt - no)
                y = (A * p + E * vt) / (A * q + E)
                no2 = jnp.maximum(w + o, kt)
                A2 = jnp.exp(w + o - no2)
                E2 = jnp.exp(kt - no2)
                return ((A2 * p + E2 * vt, A2 * q + E2, no2), y)
            init = (jnp.zeros((Bn, Cn), k.dtype), jnp.zeros((Bn, Cn), k.dtype), jnp.full((Bn, Cn), NEG_INF, k.dtype))
            kT = jnp.moveaxis(k, 1, 0)
            vT = jnp.moveaxis(v, 1, 0)
            _, yT = jax.lax.scan(step, init, (kT, vT))
            return jnp.moveaxis(yT, 0, 1)
        return _wkv(w, u, k, v)

    def _L0_ffn_ref(x, gate_w, gate_b, ew1, eb1, ew2, eb2, sw1, sb1, sw2, sb2):
        import jax, jax.numpy as jnp
        import numpy as np
        D = 512
        E = 16
        TOP_K = 2
        S_EXP = 2
        H_R = D // E * 4
        H_S = D * 4
        B, S = (4, 512)
        b, s, d = x.shape
        xf = x.reshape(-1, d)
        gates = jax.nn.softmax(xf @ gate_w + gate_b, axis=-1)
        topv, topi = jax.lax.top_k(gates, TOP_K)
        combine = jnp.sum(jax.nn.one_hot(topi, E, dtype=xf.dtype) * topv[..., None], axis=1)
        h = jax.nn.gelu(jnp.einsum('nd,edh->neh', xf, ew1) + eb1, approximate=False)
        eo = jnp.einsum('neh,ehd->ned', h, ew2) + eb2
        routed = jnp.einsum('ned,ne->nd', eo, combine)
        hs = jax.nn.gelu(jnp.einsum('nd,sdh->snh', xf, sw1) + sb1[:, None, :], approximate=False)
        shared = jnp.einsum('snh,shd->nd', hs, sw2) + jnp.sum(sb2, axis=0)
        return (shared + routed).reshape(b, s, d)
    x = x + _L0_xattn_ref(16, 128, 512, L0_xattn_w, L0_xattn_u, _layernorm(x, axis=-1), ctx_2048)
    x = x + _L0_ffn_ref(_layernorm(x, axis=-1), L0_ffn_gate_w, L0_ffn_gate_b, L0_ffn_ew1, L0_ffn_eb1, L0_ffn_ew2, L0_ffn_eb2, L0_ffn_sw1, L0_ffn_sb1, L0_ffn_sw2, L0_ffn_sb2)
    return x

_drawn_inputs = setup_inputs


def setup_inputs(seed=0):
    import zlib

    import numpy as np

    out = dict(_drawn_inputs(seed))
    spreads = {'L0_ffn_gate_b': (0.0, 0.8),
     'L0_ffn_eb1': (0.0, 0.8),
     'L0_ffn_eb2': (0.0, 0.612),
     'L0_ffn_sb1': (0.0, 0.271),
     'L0_ffn_sb2': (0.0, 0.1)}
    factors = {'L0_ffn_gate_w': 4.021, 'L0_ffn_ew1': 7.731, 'L0_ffn_ew2': 7.253}
    for name, (base, spread) in spreads.items():
        noise = np.random.default_rng([zlib.crc32(name.encode()), seed]).standard_normal(out[name].shape)
        drawn = base * np.exp(spread * noise) if base else spread * noise
        out[name] = jnp.asarray(drawn.astype(out[name].dtype))
    for name, factor in factors.items():
        out[name] = (out[name] * factor).astype(out[name].dtype)
    return out
```

```python
import concourse.bass as bass
from concourse import mybir
from contextlib import ExitStack



class Steps:

    def __init__(self, sem, names):
        self.sem, self.names = sem, names.split()

    def at(self, round_, name=None):
        n = len(self.names) if name is None else self.names.index(name) + 1
        return round_ * len(self.names) + n


def mixed_layer(nc, x, ctx_in, decay, bonus, gate_w, gate_b, ew1, eb1, ew2, eb2, sw1, sb1, sw2, sb2, out):
    f32, f32r, bf16 = mybir.dt.float32, mybir.dt.float32r, mybir.dt.bfloat16
    i32, u32 = mybir.dt.int32, mybir.dt.uint32
    ALU, ACT, AX = mybir.AluOpType, mybir.ActivationFunctionType, mybir.AxisListType

    P = 128
    B, T, D = x.shape
    E, _, HR = ew1.shape
    S_EXP, _, HS = sw1.shape
    GB = 4
    NQ = B // GB
    TT = 32
    TB = T // TT
    NT = NQ * TB
    QT = GB * T
    NTOK = B * T
    KC = D // P
    CB = D // 32
    HC = CB // 2
    CPS = HS // P
    CH = S_EXP * CPS
    NCH = NQ * CH
    RING = 3
    BR = 96
    TPE = NTOK // P
    SLOT_TILES = 2 * NTOK // P + E
    TROWS = E * TPE + SLOT_TILES
    EPS = 1e-5
    NEG = -1e38

    xq = x.rearrange("(q g) (tb t) c -> q g t tb c", g=GB, t=TT)
    vq = ctx_in.rearrange("(q g) (tb t) c -> q g t tb c", g=GB, t=TT)
    outq = out.rearrange("(q g) (tb t) c -> q g t tb c", g=GB, t=TT)
    sw1_c = sw1.rearrange("s (k p) (n h) -> s n p k h", p=P, h=P)
    sw2_c = sw2.rearrange("s (n h) d -> s n h d", h=P)
    ew1_c = ew1.rearrange("e (k p) h -> e p k h", p=P)

    xn_dram = nc.dram_tensor("xn_rows", (NTOK, D), f32, kind="Internal").ap()
    table_dram = nc.dram_tensor("slot_table", (TROWS * P, 1), i32, kind="Internal").ap()
    y_dram = nc.dram_tensor("expert_rows", (SLOT_TILES * P, D), f32, kind="Internal").ap()
    xn_tiles = xn_dram.rearrange("(n p) d -> n p d", p=P)
    table_rows = table_dram.rearrange("(r p) o -> r (p o)", p=P)
    y_tiles = y_dram.rearrange("(n p) d -> n p d", p=P)

    top = ExitStack()
    with top:
        def sb(name, shape, dt=f32, where=top):
            return where.enter_context(nc.sbuf_tensor(name, shape, dt))

        def sem(name):
            return top.enter_context(nc.semaphore(name))

        X2 = sb("X2", [P, NQ, TB, D])
        xhi = sb("xhi", [P, 2, KC, QT], f32r)
        xlo = sb("xlo", [P, 2, KC, QT], f32r)
        ident = sb("ident", [P, P])
        tri = sb("tri", [P, P], bf16)
        ones_bf = sb("ones_bf", [P, P], bf16)
        ones16 = sb("ones16", [P, E])
        neg_half = sb("neg_half", [P, TB])
        iota_e = sb("iota_e", [P, E])
        ebase = sb("ebase", [P, E])
        thr = sb("thr", [P, TPE])
        iota_p = sb("iota_p", [P, 1])
        tokid = sb("tokid", [P, NT], i32)
        tok_stage = sb("tok_stage", [P, 1], i32)
        u_col = sb("u_col", [P, CB])
        w_col = sb("w_col", [P, CB])
        gw_f = sb("gw_f", [P, KC, E])
        gw2 = sb("gw2", [P, KC, P], f32r)
        sel = sb("sel", [64, E])
        gb_b = sb("gb_b", [P, E])
        b1_rows = sb("b1_rows", [CH, P])
        b1_col = sb("b1_col", [P, CH])
        eb1_at = sb("eb1_at", [64, P])
        bias_f = sb("bias_f", [BR, D])
        bias_r = sb("bias_r", [BR, D], f32r)
        lgT = bias_f[0:64]
        st6 = sb("st6", [P, TB, 6])
        mv = sb("mv", [P, TB, 2])
        veps = sb("veps", [P, TB])
        rstd = sb("rstd", [P, TB])
        st6b = sb("st6b", [P, 6])
        mvb = sb("mvb", [P, 2])
        vepsb = sb("vepsb", [P, 1])
        rstdb = sb("rstdb", [P, 1])
        xn = sb("xn", [P, D])
        logits = sb("logits", [P, TB, E])
        gates = sb("gates", [P, TB, E])
        gmax = sb("gmax", [P, TB])
        gsum = sb("gsum", [P, TB])
        grec = sb("grec", [P, TB])
        gt = sb("gt", [P, E])
        top8 = sb("top8", [P, 8])
        idx8 = sb("idx8", [P, 8], u32)
        idxf = sb("idxf", [P, 2])
        oh = sb("oh", [P, 2, E])
        member = sb("member", [P, E], bf16)
        msum = sb("msum", [P, E], bf16)
        comb = sb("comb", [P, E])
        comb2 = sb("comb2", [P, E])
        cb96 = sb("cb96", [P, BR])
        chi = sb("chi", [P, E], f32r)
        cbT = sb("cbT", [BR, TB, P], f32r)
        rb = sb("rb", [P, E])
        rsel = sb("rsel", [P, 2, E])
        posf = sb("posf", [P, 2])
        pos_stage = sb("pos_stage", [P, 2], i32)
        pos_all = sb("pos_all", [P, NT, 2])
        e_all = sb("e_all", [P, NT, 2])
        row_all = sb("row_all", [P, NT, 2], i32)
        c_all = sb("c_all", [P, NT, 2])
        cnt = sb("cnt", [P, E])
        nt = sb("nt", [P, E])
        tend = sb("tend", [P, E])
        move = sb("move", [P, E])
        fin_e = sb("fin_e", [P, E])
        fin_n = sb("fin_n", [P, E])
        e_s = sb("e_s", [P, 1])
        trow = sb("trow", [P, 1])
        ts = sb("ts", [P, 1])
        trow_i = sb("trow_i", [P, 1], i32)
        zero_i = sb("zero_i", [P, (TROWS * P) // P], i32)

        shared_mem = ExitStack()
        w1_raw = sb("w1_raw", [P, RING, KC, P], where=shared_mem)
        w2_raw = sb("w2_raw", [P, RING, D], where=shared_mem)
        w1hi = sb("w1hi", [P, RING, KC, P], f32r, shared_mem)
        w1lo = sb("w1lo", [P, RING, KC, P], f32r, shared_mem)
        w2hi = sb("w2hi", [P, RING, D], f32r, shared_mem)
        w2lo = sb("w2lo", [P, RING, D], f32r, shared_mem)
        hf = sb("hf", [P, RING, QT], where=shared_mem)
        hhi = sb("hhi", [P, RING, QT], f32r, shared_mem)
        hlo = sb("hlo", [P, RING, QT], f32r, shared_mem)
        shared_mem.close()
        routed_mem = ExitStack()
        xg = sb("xg", [P, 4, D], where=routed_mem)
        xghi = sb("xghi", [P, 2, KC, P], f32r, routed_mem)
        xglo = sb("xglo", [P, 2, KC, P], f32r, routed_mem)
        e1hi = sb("e1hi", [P, 2, KC, P], f32r, routed_mem)
        e1lo = sb("e1lo", [P, 2, KC, P], f32r, routed_mem)
        e2hi = sb("e2hi", [P, 2, D], f32r, routed_mem)
        e2lo = sb("e2lo", [P, 2, D], f32r, routed_mem)
        rf = sb("rf", [P, 2, P], where=routed_mem)
        rhi = sb("rhi", [P, 2, P], f32r, routed_mem)
        rlo = sb("rlo", [P, 2, P], f32r, routed_mem)
        ysb = sb("ysb", [P, 4, D], where=routed_mem)
        idc = sb("idc", [P, 4], i32, routed_mem)
        routed_mem.close()
        combine_mem = ExitStack()
        yg = sb("yg", [P, 2, TB, D], where=combine_mem)
        idy = sb("idy", [P, 2, TB], i32, combine_mem)
        combine_mem.close()
        sb("rings", [P, 13824])

        wkv_mem = ExitStack()
        TS = T + 1
        wp = sb("wp", [P, CB, TS], where=wkv_mem)
        kp = sb("kp", [P, CB, TS], where=wkv_mem)
        kn = sb("kn", [P, TB, D], where=wkv_mem)
        vin = sb("vin", [P, TB, D], where=wkv_mem)
        vp = sb("vp", [P, CB, T], where=wkv_mem)
        mx = sb("mx", [P, HC, TS], where=wkv_mem)
        ea = sb("ea", [P, HC, TS], where=wkv_mem)
        eb = sb("eb", [P, HC, TS], where=wkv_mem)
        eu = sb("eu", [P, HC, T], where=wkv_mem)
        en = sb("en", [P, HC, T], where=wkv_mem)
        bv = sb("bv", [P, HC, TS], where=wkv_mem)
        pp = sb("pp", [P, HC, TS], where=wkv_mem)
        qq = sb("qq", [P, HC, TS], where=wkv_mem)
        wkv_mem.close()
        ew1_sb = sb("ew1_sb", [P, E, KC, P])
        ew2_sb = sb("ew2_sb", [P, E, D])
        cmp = sb("cmp", [P, E, TPE])
        rv = sb("rv", [P, P])
        rvT = sb("rvT", [1, P], i32)
        pick = sb("pick", [P, NT * 2, E])
        moved = sb("moved", [P, NT * 2])
        ohT = sb("ohT", [64, P])
        ids_i = sb("ids_i", [P, P], i32)
        ids_f = sb("ids_f", [P, P])
        ids = sb("ids", [P, P], i32)
        bslot = sb("bslot", [P, P])
        yc = kn[:, :, :].rearrange("p a c -> p (a c)").rearrange("p (c t) -> p c t", t=T)
        yT = vin

        acc = [top.enter_context(nc.psum_tensor(f"acc{i}", [P, D], f32)) for i in range(TB)]
        up = [top.enter_context(nc.psum_tensor(f"up{i}", [P, QT], f32)) for i in range(RING)]
        misc = top.enter_context(nc.psum_tensor("misc", [P, 512], f32))
        CBT0, RANK0 = 128, 256
        t_bank = [misc, up[0]]
        r_bank = [up[1], up[2]]
        y_bank = [acc[0], acc[1]]

        x_in = [sem(f"x_in{q}") for q in range(NQ)]
        v_in, uw_in, c_in = sem("v_in"), sem("uw_in"), sem("c_in")
        w1_in = [sem(f"w1_in{i}") for i in range(RING)]
        w2_in = [sem(f"w2_in{i}") for i in range(RING)]
        ew_in, xn_out, tz, y_out, out_done = sem("ew_in"), sem("xn_out"), sem("tz"), sem("y_out"), sem("out_done")
        scat, tab_in = sem("scat"), sem("tab_in")
        g_in = [sem(f"g_in{i}") for i in range(4)]
        yg_in = [sem(f"yg_in{i}") for i in range(TB)]
        w1_hi, w2_hi, h_hi, h_full = sem("w1_hi"), sem("w2_hi"), sem("h_hi"), sem("h_full")
        w1_lo, w2_lo, h_lo = sem("w1_lo"), sem("w2_lo"), sem("h_lo")
        up_done, down_done, acc_ready = sem("up_done"), sem("down_done"), sem("acc_ready")
        acc_free = sem("acc_free")
        rstd1, rstd2 = sem("rstd1"), sem("rstd2")
        gexp, xhi_ok, cbt_ok = sem("gexp"), sem("xhi_ok"), sem("cbt_ok")
        xT_ps, gate_ps, lg_ps, rank_ps = sem("xT_ps"), sem("gate_ps"), sem("lg_ps"), sem("rank_ps")
        b1_ps, cnt_ps, rv_ps, ids_ps, bs_ps = sem("b1_ps"), sem("cnt_ps"), sem("rv_ps"), sem("ids_ps"), sem("bs_ps")
        b1_ok = sem("b1_ok")
        ln1 = Steps(sem("ln1"), "s0 s1 s2 s3 a0 a1 a2 a3 veps n0 n1 n2 n3 tk tv")
        wkv = Steps(sem("wkv"), "smax aw aexp kexp uk umax eexp nexp bmul sp sq ap aq ev num den nt nr y")
        wexp = Steps(sem("wexp"), "a b u n ln rec")
        ty = sem("ty")
        ln2 = Steps(sem("ln2"), "x2 s a veps norm xlo")
        gsm = Steps(sem("gsm"), "parts lg max sub sum rec gates")
        rt = Steps(sem("rt"), "gt max idx idxf c e o1 o2 mem wc comb hi h0 h1 lo rank m1 m2 pos pint pall msum")
        con = Steps(sem("con"), "k0 w0 ea eb bv ms ones o16 half cb0 cb1 cb2 bias0 gz wcol ghi glo bhi1 bhi2 blo bhi3")
        pcon = Steps(sem("pcon"), "id0 tri0 sel0 id tri sela selb ie eb thr ip tok stage z")
        cph = Steps(sem("cph"), "cnt cmp nt tend fin etile ebase es ctiles ts trow0 rve move trow oh tri mul shift row")
        tvec = Steps(sem("tvec"), "rvT ohT idf idi bs")
        pst, cz = sem("pst"), sem("cz")

        rx, rT, rup, ry = sem("rx"), sem("rT"), sem("rup"), sem("ry")
        r1hi, r2hi, rhh, rff, rxh = sem("r1hi"), sem("r2hi"), sem("rhh"), sem("rff"), sem("rxh")
        r1lo, r2lo, rhl, rxl, rye = sem("r1lo"), sem("r2lo"), sem("rhl"), sem("rxl"), sem("rye")
        idc_ok = sem("idc_ok")
        yst = [sem(f"yst{i}") for i in range(4)]
        idy_ok, comb1, comb2s = sem("idy_ok"), sem("comb1"), sem("comb2s")

        block = top.enter_context(nc.Block())

        def need(eng, s, value):
            if not isinstance(value, int) or value > 0:
                eng.wait_ge(s, value)

        def apart(eng):
            eng.nop(nofuse=True)

        def schedule(q, step, head, half, mid, tile, late=None):
            eng = step.engine
            c0 = CH * q
            for j in range(2):
                step(c0 + j)
                head(j)
            at = c0 + 2
            if q < NQ - 1:
                if q == 0:
                    for s in range(2):
                        for j in range(9):
                            step(at + 9 * s + j)
                            half(s, j)
                else:
                    with eng.Fori(0, 2) as s:
                        for j in range(9):
                            step(at + 9 * s + j, at + j)
                            half(s, j)
                at += 18
                mid()
            if q == 0:
                for j in range(3):
                    step(at + j)
                    tile(0, j)
            with eng.Fori(1 if q == 0 else 0, TB - 1) as tb:
                for j in range(3):
                    step(at + 3 * tb + j, at + j)
                    tile(tb, j)
            at += 3 * (TB - 1)
            for j in range(3):
                step(at + j)
                tile(TB - 1, j)
            at += 3
            if q == NQ - 1:
                for j in range(3):
                    step(at + j)
                    late(j)
                at += 3
                rest = (c0 + CH - at) // 3
                with eng.Fori(0, rest - 1) as i:
                    for j in range(3):
                        step(at + 3 * i + j, at + j)
                at += 3 * (rest - 1)
                for j in range(3):
                    step(at + j)
                at += 3
            assert at == c0 + CH

        def uses(c, static):
            return (c - static) // 3 + static // 3 + 1 if not isinstance(c, int) else c // 3 + 1

        @block.sync
        def _(sp):
            def load_quad(q):
                for g in range(GB):
                    sp.dma_start(X2[32 * g:32 * g + 32, q], xq[q, g]).then_inc(x_in[q], 16)
                need(sp, ln2.sem, ln2.at(TB * q - 1, "x2") if q else 0)
                for g in range(GB):
                    sp.dma_start(vin[32 * g:32 * g + 32], vq[q, g]).then_inc(v_in, 16)

            def load_w1(c, static, n):
                need(sp, w1_hi, c - 2)
                need(sp, w1_lo, c - 2)
                sp.dma_start(w1_raw[:, static % RING], sw1_c[n // CPS, n % CPS]).then_inc(w1_in[static % RING], 16)

            def load_w2(c, static, n):
                need(sp, w2_hi, c - 2)
                need(sp, w2_lo, c - 2)
                sp.dma_start(w2_raw[:, static % RING], sw2_c[n // CPS, n % CPS]).then_inc(w2_in[static % RING], 16)

            load_quad(0)
            for k, v in ((u_col, bonus), (w_col, decay)):
                for g in range(GB):
                    sp.dma_start(k[32 * g:32 * g + 32], v.rearrange("(b p) -> p b", p=32)).then_inc(uw_in, 16)
            for c in range(RING):
                load_w1(c, c, c)
            sp.dma_start(gw_f[:], gate_w.rearrange("(k p) e -> p k e", p=P)).then_inc(c_in, 16)
            sp.dma_start(gb_b[:], gate_b.rearrange("(o e) -> o e", o=1).broadcast_to([P, E])).then_inc(c_in, 16)
            sp.dma_start(b1_rows[:], sb1.rearrange("s (n h) -> (s n) h", h=P)).then_inc(c_in, 16)
            sp.dma_start(eb1_at[32:32 + E], eb1).then_inc(c_in, 16)
            sp.wait_ge(con.sem, con.at(0, "bias0"))
            for r in range(3):
                sp.dma_start(bias_f[32 * r:32 * r + E], eb2).then_inc(c_in, 16)
                sp.dma_start(bias_f[32 * r + E:32 * r + E + S_EXP], sb2).then_inc(c_in, 16)

            for q in range(NQ):
                if q < NQ - 1:
                    load_quad(q + 1)
                last = q == NQ - 1
                n3 = 9
                c0 = CH * q
                if last:
                    sp.wait_ge(ln2.sem, ln2.at(NT - 1, "x2"))
                for n in range(3):
                    load_w2(c0 + n, c0 + n, n)
                    load_w1(c0 + n + 3, c0 + n + 3, n + 3)
                with sp.Fori(1, n3) as i:
                    for j in range(3):
                        n = 3 * i + j
                        load_w2(c0 + n, c0 + j, n)
                        load_w1(c0 + n + 3, c0 + j, n + 3)
                    if last:
                        sp.dma_start(ew1_sb[:, i], ew1_c[i]).then_inc(ew_in, 16)
                        sp.dma_start(ew2_sb[:, i], ew2[i]).then_inc(ew_in, 16)
                for n in range(3 * n3, CH):
                    load_w2(c0 + n, c0 + n, n)
                    if c0 + n + 3 < NCH:
                        load_w1(c0 + n + 3, c0 + n + 3, (n + 3) % CH)
                if last:
                    for i in [0, *range(n3, E)]:
                        sp.dma_start(ew1_sb[:, i], ew1_c[i]).then_inc(ew_in, 16)
                        sp.dma_start(ew2_sb[:, i], ew2[i]).then_inc(ew_in, 16)

            def store_y(s, static):
                sp.wait_ge(rye, s + 1)
                sp.dma_start(y_tiles[s], ysb[:, static % 4]).then_inc(yst[static % 4], 16)

            with sp.Fori(0, SLOT_TILES // 4) as i:
                for j in range(4):
                    store_y(4 * i + j, j)
            with sp.Fori(0, NQ) as q:
                sp.wait_ge(comb2s, TB * (q + 1))
                for g in range(GB):
                    sp.dma_start(outq[q, g], X2[32 * g:32 * g + 32, q]).then_inc(out_done, 16)
            sp.wait_ge(out_done, 16 * GB * NQ)

        @block.tensor
        def _(pe):
            def splits(o, lhs, rhs, start, stop):
                nc.tensor.matmul(o, lhs[0], rhs[0], start=start, stop=False)
                nc.tensor.matmul(o, lhs[0], rhs[1], start=False, stop=False)
                return nc.tensor.matmul(o, lhs[1], rhs[0], start=False, stop=stop)

            def up_product(c, static, q):
                slot, par = static % RING, q % 2
                need(pe, w1_hi, c + 1)
                need(pe, w1_lo, c + 1)
                need(pe, h_hi, c - 2)
                need(pe, h_full, c - 2)
                for k in range(KC):
                    last = splits(up[slot][:], (w1hi[:, slot, k], w1lo[:, slot, k]),
                                  (xhi[:, par, k], xlo[:, par, k]), k == 0, k == KC - 1)
                last.then_inc(up_done, 1)

            def block_ready(q):
                pe.wait_ge(xhi_ok, TB * (q + 1))
                pe.wait_ge(ln2.sem, ln2.at(TB * (q + 1) - 1, "xlo"))

            class step:
                engine = pe

                def __new__(cls, c, static=None):
                    static = c if static is None else static
                    q, n = static // CH, static % CH
                    slot = static % RING
                    ahead = static + 2
                    if isinstance(c, int) and ahead % CH == 0 and ahead < NCH:
                        block_ready(ahead // CH)
                    if not isinstance(c, int) or ahead < NCH:
                        up_product(c + 2, ahead, ahead // CH)
                    need(pe, w2_hi, c + 1)
                    need(pe, w2_lo, c + 1)
                    need(pe, h_hi, c + 1)
                    first = isinstance(c, int) and n == 0
                    for t in range(TB):
                        hh = hhi[:, slot, P * t:P * t + P]
                        if first and q:
                            pe.wait_ge(acc_free, TB * (q - 1) + t + 1)
                        nc.tensor.matmul(acc[t][:], hh, w2hi[:, slot], start=first, stop=False)
                        nc.tensor.matmul(acc[t][:], hh, w2lo[:, slot], start=False, stop=False)
                    need(pe, h_lo, c + 1)
                    for t in range(TB):
                        last = nc.tensor.matmul(acc[t][:], hlo[:, slot, P * t:P * t + P], w2hi[:, slot],
                                                start=False, stop=False)
                    last.then_inc(down_done, 1)
                    if isinstance(c, int) and n == CH - 1:
                        pe.wait_ge(cbt_ok, TB * (q + 1))
                        for t in range(TB):
                            last = nc.tensor.matmul(acc[t][:], cbT[:, t], bias_r[:], start=False, stop=True)
                        last.then_inc(acc_ready, 1)

            def transpose_x(t):
                pe.wait_ge(ln2.sem, ln2.at(t, "norm"))
                for k in range(KC):
                    last = nc.tensor.transpose(misc[:, P * k:P * k + P], xn[:, P * k:P * k + P], ident[:])
                last.then_inc(xT_ps, 1)

            def gate_product(q):
                block_ready(q)
                for k in range(KC):
                    nc.tensor.matmul(misc[:], gw2[:, k], xhi[:, q % 2, k], start=k == 0, stop=False)
                    last = nc.tensor.matmul(misc[:], gw2[:, k], xlo[:, q % 2, k], start=False, stop=k == KC - 1)
                last.then_inc(gate_ps, 1)

            def gate_transpose(q):
                pe.wait_ge(gsm.sem, gsm.at(q, "parts"))
                for tb in range(TB):
                    last = nc.tensor.matmul(misc[:, E * tb:E * tb + E], lgT[:, P * tb:P * tb + P], sel[:],
                                            start=True, stop=True)
                last.then_inc(lg_ps, 1)

            def routing_products(t):
                pe.wait_ge(rt.sem, rt.at(t, "lo"))
                nc.tensor.transpose(misc[0:BR, CBT0:CBT0 + P], cb96[:], ident[:])
                nc.tensor.matmul(misc[:, RANK0:RANK0 + E], tri[:], member[:], start=True, stop=False)
                nc.tensor.matmul(misc[:, RANK0:RANK0 + E], ones_bf[:], msum[:], start=False, stop=True)\
                    .then_inc(rank_ps, 1)

            pe.wait_ge(pcon.sem, pcon.at(0, "tri"))
            pe.wait_ge(c_in, 16 * 10)
            nc.tensor.transpose(misc[:, 0:CH], b1_rows[:], ident[0:CH, 0:CH]).then_inc(b1_ps, 1)
            pe.wait_ge(b1_ok, 1)
            pe.wait_ge(con.sem, con.at(0))
            transpose_x(0)
            with pe.Fori(1, TB) as tb:
                pe.wait_ge(xhi_ok, tb)
                pe.wait_ge(ln2.sem, ln2.at(tb - 1, "xlo"))
                transpose_x(tb)
            gate_product(0)
            up_product(0, 0, 0)
            up_product(1, 1, 0)
            for q in range(NQ):
                def head(j, q=q):
                    if j == 0:
                        gate_transpose(q)

                def tile(tb, j, q=q):
                    t = TB * q + tb
                    if j == 0 and q < NQ - 1:
                        pe.wait_ge(gsm.sem, gsm.at(q, "lg"))
                        pe.wait_ge(cbt_ok, t)
                        pe.wait_ge(rt.sem, t * len(rt.names))
                        transpose_x(t + TB)
                    if j == 1:
                        if q < NQ - 1:
                            pe.wait_ge(xhi_ok, t + TB + 1)
                            pe.wait_ge(ln2.sem, ln2.at(t + TB, "xlo"))
                        else:
                            pe.wait_ge(gsm.sem, gsm.at(q, "lg"))
                            pe.wait_ge(cbt_ok, t)
                            pe.wait_ge(rt.sem, t * len(rt.names))
                        routing_products(t)

                def late(j):
                    if j == 0:
                        pe.wait_ge(rt.sem, rt.at(NT - 1))
                        pe.wait_ge(cbt_ok, NT)
                        nc.tensor.matmul(misc[:, 0:E], ones_bf[:], msum[:], start=True, stop=True)\
                            .then_inc(cnt_ps, 1)

                schedule(q, step, head, lambda s, j: None, lambda: None, tile, late)
                if q < NQ - 1:
                    pe.wait_ge(rt.sem, rt.at(TB * (q + 1) - 1, "rank"))
                    gate_product(q + 1)

            pe.wait_ge(cph.sem, cph.at(0))
            nc.tensor.transpose(misc[:, 0:P], rv[:], ident[:]).then_inc(rv_ps, 1)
            pe.wait_ge(tvec.sem, tvec.at(0, "idf"))
            nc.tensor.transpose(misc[:, P:2 * P], ids_f[:], ident[:]).then_inc(ids_ps, 1)
            nc.tensor.matmul(misc[:, 2 * P:3 * P], eb1_at[32:32 + E], ohT[32:32 + E], start=True, stop=True)\
                .then_inc(bs_ps, 1)
            pe.wait_ge(tvec.sem, tvec.at(0))

            def routed_T(s, static):
                i = static % 2
                pe.wait_ge(g_in[static % 4], 16 * ((s - static) // 4 + static // 4 + 1))
                need(pe, rxh, s - 1)
                need(pe, rxl, s - 1)
                for k in range(KC):
                    last = nc.tensor.transpose(t_bank[i][:, P * k:P * k + P], xg[:, static % 4, P * k:P * k + P],
                                               ident[:])
                last.then_inc(rT, 1)

            def routed_up(s, static):
                i = static % 2
                pe.wait_ge(rxh, s + 1)
                pe.wait_ge(rxl, s + 1)
                pe.wait_ge(r1hi, s + 1)
                pe.wait_ge(r1lo, s + 1)
                need(pe, rhh, s - 1)
                need(pe, rff, s - 1)
                for k in range(KC):
                    last = splits(r_bank[i][:, 0:P], (e1hi[:, i, k], e1lo[:, i, k]), (xghi[:, i, k], xglo[:, i, k]),
                                  k == 0, k == KC - 1)
                last.then_inc(rup, 1)

            def routed_down(s, static):
                i = static % 2
                pe.wait_ge(r2hi, s + 1)
                pe.wait_ge(r2lo, s + 1)
                pe.wait_ge(rhh, s + 1)
                pe.wait_ge(rhl, s + 1)
                need(pe, rye, s - 1)
                splits(y_bank[i][:], (rhi[:, i], rlo[:, i]), (e2hi[:, i], e2lo[:, i]), True, True).then_inc(ry, 1)

            pe.wait_ge(acc_free, TB * NQ)
            routed_T(0, 0)
            routed_T(1, 1)
            routed_up(0, 0)
            NL = SLOT_TILES // 4 - 1
            for s in range(4):
                routed_T(s + 2, s + 2)
                routed_up(s + 1, s + 1)
                routed_down(s, s)
            with pe.Fori(1, NL) as it:
                for j in range(4):
                    s = 4 * it + j
                    routed_T(s + 2, j + 2)
                    routed_up(s + 1, j + 1)
                    routed_down(s, j)
            for s in range(4 * NL, SLOT_TILES):
                if s + 2 < SLOT_TILES:
                    routed_T(s + 2, s + 2)
                if s + 1 < SLOT_TILES:
                    routed_up(s + 1, s + 1)
                routed_down(s, s)

        @block.scalar
        def _(act):
            def split_w1(c, static):
                slot = static % RING
                act.wait_ge(w1_in[slot], 16 * uses(c, static))
                need(act, up_done, c - 2)
                nc.scalar.copy(w1hi[:, slot], w1_raw[:, slot]).then_inc(w1_hi, 1)

            class step:
                engine = act

                def __new__(cls, c, static=None):
                    static = c if static is None else static
                    slot, n = static % RING, static % CH
                    cc = c % CH if isinstance(c, int) else c - CH * (static // CH)
                    bias = b1_col[:, bass.ds(cc, 1)]
                    act.wait_ge(b1_ok, 1)
                    act.wait_ge(up_done, c + 1)
                    need(act, down_done, c - 2)
                    nc.scalar.activation(hhi[:, slot], up[slot][:], ACT.Gelu, bias=bias).then_inc(h_hi, 1)
                    act.wait_ge(b1_ok, 1)
                    need(act, h_lo, c - 2)
                    nc.scalar.activation(hf[:, slot], up[slot][:], ACT.Gelu, bias=bias).then_inc(h_full, 1)
                    act.wait_ge(w2_in[slot], 16 * uses(c, static))
                    nc.scalar.copy(w2hi[:, slot], w2_raw[:, slot]).then_inc(w2_hi, 1)
                    if not isinstance(c, int) or c + 3 < NCH:
                        split_w1(c + 3, static + 3)

            def wkv_exps(r):
                nc.scalar.preload_act_table_set("natural_log_exp_and_others")
                for name, arg, buf in (("a", "aexp", ea[:, :, 1:]), ("b", "kexp", eb[:, :, 1:]),
                                       ("u", "eexp", eu[:]), ("n", "nexp", en[:])):
                    act.wait_ge(wkv.sem, wkv.at(r, arg))
                    nc.scalar.activation(buf, buf, ACT.Exp).then_inc(wexp.sem, 1)

            def wkv_reciprocal(r):
                nc.scalar.preload_act_table_set("natural_log_exp_and_others")
                act.wait_ge(wkv.sem, wkv.at(r, "den"))
                nc.scalar.activation(en[:], ea[:, :, 1:], ACT.Ln).then_inc(wexp.sem, 1)
                act.wait_ge(wexp.sem, wexp.at(r, "ln"))
                nc.scalar.activation(eu[:], en[:], ACT.Exp, scale=-1.0).then_inc(wexp.sem, 1)

            def gate_exp(q):
                act.wait_ge(gsm.sem, gsm.at(q, "sub"))
                nc.scalar.activation(gates[:], gates[:], ACT.Exp).then_inc(gexp, 1)

            def x_hi(t, par, tb):
                act.wait_ge(xT_ps, t + 1)
                nc.scalar.copy(xhi[:, par, :, bass.ds(P * tb, P)],
                               misc[:].rearrange("p (k n) -> p k n", k=KC)).then_inc(xhi_ok, 1)

            def combine_T(t, tb, q):
                act.wait_ge(rank_ps, t + 1)
                need(act, acc_ready, q)
                nc.scalar.copy(cbT[:, tb], misc[0:BR, CBT0:CBT0 + P]).then_inc(cbt_ok, 1)

            for c in range(RING):
                split_w1(c, c)
            act.wait_ge(b1_ps, 1)
            nc.scalar.copy(b1_col[:], misc[:, 0:CH]).then_inc(b1_ok, 1)
            act.wait_ge(b1_ok, 1)
            for s in range(2):
                wkv_exps(s)
                wkv_reciprocal(s)
            with act.Fori(0, TB) as tb:
                x_hi(tb, 0, tb)

            for q in range(NQ):
                def head(j, q=q):
                    if j == 1:
                        gate_exp(q)

                def half(s, j, q=q):
                    if j == 3:
                        wkv_exps(2 * (q + 1) + s)
                    if j == 7:
                        wkv_reciprocal(2 * (q + 1) + s)

                def tile(tb, j, q=q):
                    if j == 1 and q < NQ - 1:
                        if q:
                            act.wait_ge(up_done, CH * q)
                        x_hi(TB * (q + 1) + tb, (q + 1) % 2, tb)
                    if j == 2:
                        combine_T(TB * q + tb, tb, q)

                schedule(q, step, head, half, lambda: None, tile, lambda j: None)

            act.wait_ge(tvec.sem, tvec.at(0))
            act.wait_ge(ew_in, 32 * E)
            act.wait_ge(down_done, NCH)
            act.wait_ge(h_lo, NCH)
            act.wait_ge(w1_lo, NCH)
            act.wait_ge(w2_lo, NCH)
            act.wait_ge(w2_hi, NCH)
            act.wait_ge(h_full, NCH)

            def routed_w(s, static):
                i = static % 2
                e = act.value_load(rvT[0:1, bass.ds(s, 1)], min_val=0, max_val=E - 1)
                need(act, rup, s - 1)
                nc.scalar.copy(e1hi[:, i], ew1_sb[:, e]).then_inc(r1hi, 1)
                need(act, ry, s - 1)
                nc.scalar.copy(e2hi[:, i], ew2_sb[:, e]).then_inc(r2hi, 1)

            def routed_x(s, static):
                i = static % 2
                act.wait_ge(rT, s + 1)
                need(act, rup, s - 1)
                nc.scalar.copy(xghi[:, i], t_bank[i][:].rearrange("p (k n) -> p k n", k=KC)).then_inc(rxh, 1)

            def routed_h(s, static):
                i = static % 2
                b = bslot[:, bass.ds(s, 1)]
                act.wait_ge(tvec.sem, tvec.at(0))
                act.wait_ge(rup, s + 1)
                need(act, ry, s - 1)
                nc.scalar.activation(rhi[:, i], r_bank[i][:, 0:P], ACT.Gelu, bias=b).then_inc(rhh, 1)
                act.wait_ge(tvec.sem, tvec.at(0))
                need(act, rhl, s - 1)
                nc.scalar.activation(rf[:, i], r_bank[i][:, 0:P], ACT.Gelu, bias=b).then_inc(rff, 1)

            routed_w(0, 0)
            routed_x(0, 0)
            routed_x(1, 1)
            routed_h(0, 0)
            for s in range(4):
                routed_w(s + 1, s + 1)
                routed_x(s + 2, s + 2)
                routed_h(s + 1, s + 1)
            NL = SLOT_TILES // 4 - 1
            with act.Fori(1, NL) as it:
                for j in range(4):
                    s = 4 * it + j
                    routed_w(s + 1, j + 1)
                    routed_x(s + 2, j + 2)
                    routed_h(s + 1, j + 1)
            for s in range(4 * NL, SLOT_TILES - 1):
                routed_w(s + 1, s + 1)
                if s + 2 < SLOT_TILES:
                    routed_x(s + 2, s + 2)
                routed_h(s + 1, s + 1)

        @block.vector
        def _(dve):
            V = nc.vector

            def f(ap):
                return ap.bitcast(f32)

            def split_w1(c, static):
                slot = static % RING
                dve.wait_ge(w1_hi, c + 1)
                dve.wait_ge(w1_in[slot], 16 * uses(c, static))
                need(dve, up_done, c - 2)
                V.tensor_tensor(w1lo[:, slot], w1_raw[:, slot], f(w1hi[:, slot]), ALU.subtract).then_inc(w1_lo, 1)

            class step:
                engine = dve

                def __new__(cls, c, static=None):
                    static = c if static is None else static
                    slot = static % RING
                    dve.wait_ge(h_hi, c + 1)
                    dve.wait_ge(h_full, c + 1)
                    need(dve, down_done, c - 2)
                    V.tensor_tensor(hlo[:, slot], hf[:, slot], f(hhi[:, slot]), ALU.subtract).then_inc(h_lo, 1)
                    dve.wait_ge(w2_hi, c + 1)
                    dve.wait_ge(w2_in[slot], 16 * uses(c, static))
                    V.tensor_tensor(w2lo[:, slot], w2_raw[:, slot], f(w2hi[:, slot]), ALU.subtract).then_inc(w2_lo, 1)
                    if not isinstance(c, int) or c + 3 < NCH:
                        split_w1(c + 3, static + 3)

            def const(ins):
                ins.then_inc(con.sem, 1)

            def after(steps, r, name):
                dve.wait_ge(steps.sem, steps.at(r, name))

            const(V.memset(kp[:, :, 0:1], NEG))
            const(V.memset(wp[:, :, 0:1], NEG))
            const(V.memset(ea[:, :, 0:1], 0.0))
            const(V.memset(eb[:, :, 0:1], 0.0))
            const(V.memset(bv[:, :, 0:1], 0.0))
            const(V.memset(msum[:], 0.0))
            const(V.memset(ones_bf[:], 1.0))
            const(V.memset(ones16[:], 1.0))
            const(V.memset(neg_half[:], -0.5))
            const(V.memset(cb96[:], 0.0))
            after(con, 0, "cb0")
            const(V.memset(cb96[:, E:E + S_EXP], 1.0))
            const(V.memset(cb96[:, 32 + E:32 + E + S_EXP], 1.0))
            const(V.memset(bias_f[:], 0.0))
            const(V.memset(f(gw2[:]), 0.0))
            dve.wait_ge(uw_in, 16 * 2 * GB)
            const(V.tensor_copy(wp[:, :, 1:], w_col[:].unsqueeze(2).broadcast_to([P, CB, T])))
            for c in range(RING):
                split_w1(c, c)
            dve.wait_ge(c_in, 16 * 10)
            after(con, 0, "gz")
            const(V.tensor_copy(gw2[:, :, 0:E], gw_f[:]))
            after(con, 0, "ghi")
            const(V.tensor_tensor(gw2[:, :, 32:32 + E], gw_f[:], f(gw2[:, :, 0:E]), ALU.subtract))
            const(V.tensor_copy(bias_r[0:32], bias_f[0:32]))
            const(V.tensor_copy(bias_r[64:96], bias_f[64:96]))
            const(V.tensor_copy(bias_r[32:64], bias_f[32:64]))
            after(con, 0, "blo")
            const(V.tensor_tensor(bias_r[32:64], bias_f[32:64], f(bias_r[32:64]), ALU.subtract))

            def ln1_stats(q):
                dve.wait_ge(x_in[q], 16 * GB)
                for tb in range(TB):
                    V.bn_stats(st6[:, tb], X2[:, q, tb]).then_inc(ln1.sem, 1)
                for tb in range(TB):
                    after(ln1, q, f"s{tb}")
                    V.bn_aggr(mv[:, tb], st6[:, tb]).then_inc(ln1.sem, 1)
                after(ln1, q, "a3")
                V.tensor_scalar(veps[:], mv[:, :, 1], EPS, None, ALU.add).then_inc(ln1.sem, 1)

            def ln1_apply(q):
                dve.wait_ge(rstd1, q + 1)
                if q:
                    dve.wait_ge(ty, q)
                for tb in range(TB):
                    V.tensor_scalar(kn[:, tb], X2[:, q, tb], mv[:, tb, 0:1], rstd[:, tb:tb + 1],
                                    ALU.subtract, ALU.mult).then_inc(ln1.sem, 1)
                after(ln1, q, "n3")
                V.transpose(kp[:, :, 1:].rearrange("p c (tb t) -> p c tb t", t=TT),
                            kn[:].rearrange("p tb (c k) -> p c tb k", k=32)).then_inc(ln1.sem, 1)
                dve.wait_ge(v_in, 16 * GB * (q + 1))
                V.transpose(vp[:].rearrange("p c (tb t) -> p c tb t", t=TT),
                            vin[:].rearrange("p tb (c k) -> p c tb k", k=32)).then_inc(ln1.sem, 1)

            def wkv_part(q, s, part):
                r = 2 * q + s
                cs = bass.ds(HC * s, HC)
                k_h, v_h, w_h = kp[:, cs, 1:], vp[:, cs, :], wp[:, cs, 1:]
                m_prev, m_now = mx[:, :, 0:T], mx[:, :, 1:]
                p_prev, q_prev = pp[:, :, 0:T], qq[:, :, 0:T]
                flat = lambda a: a.rearrange("p c t -> p (c t)")

                def do(ins):
                    ins.then_inc(wkv.sem, 1)

                if part == 0:
                    after(ln1, q, "tv")
                    do(V.tensor_tensor_scan(flat(mx[:]), flat(wp[:, cs, :]), flat(kp[:, cs, :]), 0.0,
                                            ALU.add, ALU.max))
                    after(wkv, r, "smax")
                    do(V.tensor_tensor(ea[:, :, 1:], w_h, m_prev, ALU.add))
                elif part == 1:
                    after(wkv, r, "aw")
                    do(V.tensor_tensor(ea[:, :, 1:], ea[:, :, 1:], m_now, ALU.subtract))
                    do(V.tensor_tensor(eb[:, :, 1:], k_h, m_now, ALU.subtract))
                    do(V.tensor_tensor(eu[:], k_h, u_col[:, cs].unsqueeze(2).broadcast_to([P, HC, T]), ALU.add))
                elif part == 2:
                    after(wkv, r, "uk")
                    do(V.tensor_tensor(en[:], m_prev, eu[:], ALU.max))
                    after(wkv, r, "umax")
                    do(V.tensor_tensor(eu[:], eu[:], en[:], ALU.subtract))
                    after(wkv, r, "eexp")
                    do(V.tensor_tensor(en[:], m_prev, en[:], ALU.subtract))
                elif part == 4:
                    dve.wait_ge(wexp.sem, wexp.at(r, "n"))
                    do(V.tensor_tensor(bv[:, :, 1:], eb[:, :, 1:], v_h, ALU.mult))
                    after(wkv, r, "bmul")
                    do(V.tensor_tensor_scan(flat(pp[:]), flat(ea[:]), flat(bv[:]), 0.0, ALU.mult, ALU.add))
                    do(V.tensor_tensor_scan(flat(qq[:]), flat(ea[:]), flat(eb[:]), 0.0, ALU.mult, ALU.add))
                elif part == 5:
                    after(wkv, r, "sq")
                    do(V.tensor_tensor(bv[:, :, 1:], en[:], p_prev, ALU.mult))
                    do(V.tensor_tensor(ea[:, :, 1:], en[:], q_prev, ALU.mult))
                    do(V.tensor_tensor(eb[:, :, 1:], eu[:], v_h, ALU.mult))
                elif part == 6:
                    after(wkv, r, "ev")
                    do(V.tensor_tensor(bv[:, :, 1:], bv[:, :, 1:], eb[:, :, 1:], ALU.add))
                    do(V.tensor_tensor(ea[:, :, 1:], ea[:, :, 1:], eu[:], ALU.add))
                elif part == 8:
                    dve.wait_ge(wexp.sem, wexp.at(r, "rec"))
                    do(V.tensor_tensor(eb[:, :, 1:], ea[:, :, 1:], eu[:], ALU.mult))
                    after(wkv, r, "nt")
                    do(V.scalar_tensor_tensor(out=en[:], in0=eb[:, :, 1:], scalar=-2.0, in1=eu[:],
                                              op0=ALU.add, op1=ALU.mult))
                    after(wkv, r, "nr")
                    do(V.scalar_tensor_tensor(out=yc[:, cs, :], in0=en[:], scalar=-1.0, in1=bv[:, :, 1:],
                                              op0=ALU.mult, op1=ALU.mult))

            def wkv_back(q):
                after(wkv, 2 * q + 1, "y")
                V.transpose(yT[:].rearrange("p tb (c k) -> p tb c k", k=32),
                            yc.rearrange("p c (tb t) -> p tb c t", t=TT)).then_inc(ty, 1)

            def ln2_stats(q, tb, t):
                dve.wait_ge(ty, q + 1)
                V.tensor_tensor(X2[:, q, tb], X2[:, q, tb], yT[:, tb], ALU.add).then_inc(ln2.sem, 1)
                after(ln2, t, "x2")
                apart(dve)
                V.bn_stats(st6b[:], X2[:, q, tb]).then_inc(ln2.sem, 1)
                after(ln2, t, "s")
                apart(dve)
                V.bn_aggr(mvb[:], st6b[:]).then_inc(ln2.sem, 1)
                after(ln2, t, "a")
                V.tensor_scalar(vepsb[:], mvb[:, 1:2], EPS, None, ALU.add).then_inc(ln2.sem, 1)

            def ln2_apply(q, tb, t):
                dve.wait_ge(rstd2, t + 1)
                need(dve, xn_out, 16 * t)
                need(dve, xT_ps, t)
                V.tensor_scalar(xn[:], X2[:, q, tb], mvb[:, 0:1], rstdb[:], ALU.subtract, ALU.mult)\
                    .then_inc(ln2.sem, 1)

            def x_lo(tb, par, t):
                dve.wait_ge(xhi_ok, t + 1)
                tok = bass.ds(P * tb, P)
                V.tensor_tensor(xlo[:, par, :, tok], misc[:].rearrange("p (k n) -> p k n", k=KC),
                                f(xhi[:, par, :, tok]), ALU.subtract).then_inc(ln2.sem, 1)

            def spread(col):
                return col.unsqueeze(2).broadcast_to([P, TB, E])

            def gate_parts(q):
                dve.wait_ge(gate_ps, q + 1)
                V.tensor_copy(lgT[:], misc[0:64]).then_inc(gsm.sem, 1)

            def gates_max(q):
                dve.wait_ge(lg_ps, q + 1)
                V.tensor_tensor(logits[:], misc[:, 0:TB * E].rearrange("p (t e) -> p t e", e=E),
                                gb_b[:].unsqueeze(1).broadcast_to([P, TB, E]), ALU.add).then_inc(gsm.sem, 1)
                after(gsm, q, "lg")
                V.tensor_reduce(gmax[:], logits[:], AX.X, ALU.max).then_inc(gsm.sem, 1)
                after(gsm, q, "max")
                V.tensor_tensor(gates[:], logits[:], spread(gmax[:]), ALU.subtract).then_inc(gsm.sem, 1)

            def gates_norm(q):
                dve.wait_ge(gexp, q + 1)
                V.tensor_reduce(gsum[:], gates[:], AX.X, ALU.add).then_inc(gsm.sem, 1)
                after(gsm, q, "sum")
                V.reciprocal(grec[:], gsum[:]).then_inc(gsm.sem, 1)
                after(gsm, q, "rec")
                V.tensor_tensor(gates[:], gates[:], spread(grec[:]), ALU.mult).then_inc(gsm.sem, 1)

            def rdo(ins):
                ins.then_inc(rt.sem, 1)

            def route_pick(q, tb, t):
                after(gsm, q, "gates")
                if not isinstance(t, int) or t:
                    dve.wait_ge(rank_ps, t)
                rdo(V.tensor_copy(gt[:], gates[:, tb]))
                after(rt, t, "gt")
                apart(dve)
                rdo(V.max(top8[:], gt[:]))
                after(rt, t, "max")
                apart(dve)
                rdo(V.max_index(idx8[:], top8[:], gt[:]))
                after(rt, t, "idx")
                rdo(V.tensor_copy(idxf[:], idx8[:, 0:2]))
                rdo(V.tensor_copy(c_all[:, t] if isinstance(t, int) else c_all[:, t, :], top8[:, 0:2]))
                after(rt, t, "idxf")
                rdo(V.tensor_copy(e_all[:, t] if isinstance(t, int) else e_all[:, t, :], idxf[:]))
                for j in range(2):
                    rdo(V.tensor_scalar(oh[:, j], iota_e[:], idxf[:, j:j + 1], None, ALU.is_equal))
                after(rt, t, "o2")
                rdo(V.tensor_tensor(member[:], oh[:, 0], oh[:, 1], ALU.add))
                rdo(V.tensor_scalar(comb2[:], oh[:, 0], top8[:, 0:1], None, ALU.mult))

            def route_combine(t):
                after(rt, t, "wc")
                rdo(V.scalar_tensor_tensor(out=comb[:], in0=oh[:, 1], scalar=top8[:, 1:2], in1=comb2[:],
                                           op0=ALU.mult, op1=ALU.add))
                after(rt, t, "comb")
                rdo(V.tensor_copy(chi[:], comb[:]))
                after(rt, t, "hi")
                rdo(V.tensor_copy(cb96[:, 0:E], f(chi[:])))
                rdo(V.tensor_copy(cb96[:, 32:32 + E], f(chi[:])))
                rdo(V.tensor_tensor(cb96[:, 64:64 + E], comb[:], f(chi[:]), ALU.subtract))

            def route_place(t):
                dve.wait_ge(rank_ps, t + 1)
                dve.wait_ge(cbt_ok, t + 1)
                rdo(V.tensor_tensor(rb[:], misc[:, RANK0:RANK0 + E], ebase[:], ALU.add))
                after(rt, t, "rank")
                for j in range(2):
                    rdo(V.tensor_tensor(rsel[:, j], oh[:, j], rb[:], ALU.mult))
                after(rt, t, "m2")
                rdo(V.tensor_reduce(posf[:], rsel[:], AX.X, ALU.add))
                after(rt, t, "pos")
                need(dve, scat, 32 * t)
                rdo(V.tensor_copy(pos_stage[:], posf[:]))
                rdo(V.tensor_copy(pos_all[:, t] if isinstance(t, int) else pos_all[:, t, :], posf[:]))
                rdo(V.tensor_tensor(msum[:], msum[:], member[:], ALU.add))

            def take_block(q):
                dve.wait_ge(acc_ready, q + 1)
                for t in range(TB):
                    V.tensor_tensor(X2[:, q, t], X2[:, q, t], acc[t][:], ALU.add).then_inc(acc_free, 1)

            after(con, 0, None)
            dve.wait_ge(pcon.sem, pcon.at(0))
            ln1_stats(0)
            ln1_apply(0)
            for s in range(2):
                for part in range(9):
                    wkv_part(0, s, part)
            wkv_back(0)
            ln2_stats(0, 0, 0)
            ln2_apply(0, 0, 0)
            x_lo(0, 0, 0)
            with dve.Fori(1, TB) as tb:
                ln2_stats(0, tb, tb)
                ln2_apply(0, tb, tb)
                x_lo(tb, 0, tb)

            for q in range(NQ):
                def head(j, q=q):
                    if j == 0:
                        gate_parts(q)
                        if q:
                            take_block(q - 1)
                        if q < NQ - 1:
                            ln1_stats(q + 1)
                    else:
                        gates_max(q)
                        if q < NQ - 1:
                            ln1_apply(q + 1)
                        else:
                            gates_norm(q)

                def mid(q=q):
                    gates_norm(q)
                    wkv_back(q + 1)

                def half(s, j, q=q):
                    wkv_part(q + 1, s, j)

                def tile(tb, j, q=q):
                    t = TB * q + tb
                    if j == 0:
                        if q < NQ - 1:
                            ln2_stats(q + 1, tb, t + TB)
                        route_pick(q, tb, t)
                    if j == 1:
                        if q < NQ - 1:
                            ln2_apply(q + 1, tb, t + TB)
                        route_combine(t)
                        if q < NQ - 1:
                            if q:
                                dve.wait_ge(up_done, CH * q)
                            x_lo(tb, (q + 1) % 2, t + TB)
                    if j == 2:
                        route_place(t)

                def late(j):
                    if j == 1:
                        slots()

                def cdo(ins):
                    ins.then_inc(cph.sem, 1)

                def slots():
                    dve.wait_ge(cnt_ps, 1)
                    dve.wait_ge(cz, 2)
                    cdo(V.tensor_copy(cnt[:], misc[:, 0:E]))
                    after(cph, 0, "cnt")
                    cdo(V.tensor_tensor(cmp[:], cnt[:].unsqueeze(2).broadcast_to([P, E, TPE]),
                                        thr[:].unsqueeze(1).broadcast_to([P, E, TPE]), ALU.is_gt))
                    after(cph, 0, "cmp")
                    cdo(V.tensor_reduce(nt[:], cmp[:], AX.X, ALU.add))
                    after(cph, 0, "nt")
                    cdo(V.tensor_tensor_scan(tend[:], ones16[:], nt[:], 0.0, ALU.mult, ALU.add))
                    after(cph, 0, "tend")
                    cdo(V.tensor_scalar(fin_e[:], tend[:], iota_p[:], None, ALU.is_le))
                    cdo(V.tensor_tensor(move[:], tend[:], nt[:], ALU.subtract))
                    after(cph, 0, "etile")
                    cdo(V.scalar_tensor_tensor(out=move[:], in0=move[:], scalar=float(P), in1=ebase[:],
                                               op0=ALU.mult, op1=ALU.subtract))
                    cdo(V.tensor_reduce(e_s[:], fin_e[:], AX.X, ALU.add))
                    cdo(V.tensor_tensor(fin_n[:], fin_e[:], nt[:], ALU.mult))
                    after(cph, 0, "ctiles")
                    cdo(V.tensor_reduce(ts[:], fin_n[:], AX.X, ALU.add))
                    cdo(V.scalar_tensor_tensor(out=trow[:], in0=e_s[:], scalar=float(TPE), in1=iota_p[:],
                                               op0=ALU.mult, op1=ALU.add))
                    cdo(V.tensor_scalar(rv[:, 0:1], e_s[:], float(E - 1), None, ALU.min))
                    after(rt, NT - 1, None)
                    cdo(V.tensor_tensor(pick[:], e_all[:].rearrange("p n j -> p (n j)").unsqueeze(2)
                                        .broadcast_to([P, NT * 2, E]),
                                        iota_e[:].unsqueeze(1).broadcast_to([P, NT * 2, E]), ALU.is_equal))
                    after(cph, 0, "move")
                    cdo(V.tensor_tensor(trow[:], trow[:], ts[:], ALU.subtract))
                    cdo(V.tensor_scalar(rv[:, 32:32 + E], iota_e[:], rv[:, 0:1], None, ALU.is_equal))
                    after(cph, 0, "trow")
                    cdo(V.tensor_copy(trow_i[:], trow[:]))
                    cdo(V.tensor_tensor(pick[:], pick[:], move[:].unsqueeze(1).broadcast_to([P, NT * 2, E]),
                                        ALU.mult))
                    after(cph, 0, "mul")
                    cdo(V.tensor_reduce(moved[:], pick[:], AX.X, ALU.add))
                    after(cph, 0, "shift")
                    cdo(V.tensor_tensor(row_all[:], pos_all[:], moved[:].rearrange("p (n j) -> p n j", j=2),
                                        ALU.add))

                schedule(q, step, head, half, mid, tile, late)

            take_block(NQ - 1)
            dve.wait_ge(rv_ps, 1)
            V.tensor_copy(rvT[:], misc[0:1, 0:P]).then_inc(tvec.sem, 1)
            V.tensor_copy(ohT[32:32 + E], misc[32:32 + E, 0:P]).then_inc(tvec.sem, 1)
            dve.wait_ge(tab_in, 16)
            V.tensor_copy(ids_f[0:SLOT_TILES], ids_i[0:SLOT_TILES]).then_inc(tvec.sem, 1)
            dve.wait_ge(ids_ps, 1)
            dve.wait_ge(bs_ps, 1)
            V.tensor_copy(ids[:], misc[:, P:2 * P]).then_inc(tvec.sem, 1)
            V.tensor_copy(bslot[:], misc[:, 2 * P:3 * P]).then_inc(tvec.sem, 1)
            after(tvec, 0, None)
            dve.wait_ge(ew_in, 32 * E)
            dve.wait_ge(down_done, NCH)
            dve.wait_ge(w1_lo, NCH)
            dve.wait_ge(w2_lo, NCH)
            dve.wait_ge(h_lo, NCH)

            def routed_w(s, static):
                i = static % 2
                e = dve.value_load(rvT[0:1, bass.ds(s, 1)], min_val=0, max_val=E - 1)
                dve.wait_ge(r1hi, s + 1)
                need(dve, rup, s - 1)
                V.tensor_tensor(e1lo[:, i], ew1_sb[:, e], f(e1hi[:, i]), ALU.subtract).then_inc(r1lo, 1)
                dve.wait_ge(r2hi, s + 1)
                need(dve, ry, s - 1)
                V.tensor_tensor(e2lo[:, i], ew2_sb[:, e], f(e2hi[:, i]), ALU.subtract).then_inc(r2lo, 1)

            def routed_x(s, static):
                i = static % 2
                dve.wait_ge(rxh, s + 1)
                need(dve, rup, s - 1)
                V.tensor_tensor(xglo[:, i], t_bank[i][:].rearrange("p (k n) -> p k n", k=KC), f(xghi[:, i]),
                                ALU.subtract).then_inc(rxl, 1)

            def routed_h(s, static):
                i = static % 2
                dve.wait_ge(rhh, s + 1)
                dve.wait_ge(rff, s + 1)
                need(dve, ry, s - 1)
                V.tensor_tensor(rlo[:, i], rf[:, i], f(rhi[:, i]), ALU.subtract).then_inc(rhl, 1)

            def routed_y(s, static):
                dve.wait_ge(ry, s + 1)
                n = static % 4
                need(dve, yst[n], 16 * ((s - static) // 4 + static // 4))
                V.tensor_copy(ysb[:, n], y_bank[static % 2][:]).then_inc(rye, 1)

            routed_w(0, 0)
            routed_x(0, 0)
            routed_x(1, 1)
            routed_h(0, 0)
            for s in range(4):
                routed_w(s + 1, s + 1)
                routed_x(s + 2, s + 2)
                routed_h(s + 1, s + 1)
                routed_y(s, s)
            NL = SLOT_TILES // 4 - 1
            with dve.Fori(1, NL) as it:
                for j in range(4):
                    s = 4 * it + j
                    routed_w(s + 1, j + 1)
                    routed_x(s + 2, j + 2)
                    routed_h(s + 1, j + 1)
                    routed_y(s, j)
            for s in range(4 * NL, SLOT_TILES):
                if s + 1 < SLOT_TILES:
                    routed_w(s + 1, s + 1)
                    if s + 2 < SLOT_TILES:
                        routed_x(s + 2, s + 2)
                    routed_h(s + 1, s + 1)
                routed_y(s, s)

            with dve.Fori(0, NQ) as q:
                for tb in range(TB):
                    dve.wait_ge(yg_in[tb], 32 * (q + 1))
                    V.scalar_tensor_tensor(out=X2[:, q, tb], in0=yg[:, 0, tb], scalar=c_all[:, TB * q + tb, 0:1],
                                           in1=X2[:, q, tb], op0=ALU.mult, op1=ALU.add).then_inc(comb1, 1)
                    dve.wait_ge(comb1, TB * q + tb + 1)
                    V.scalar_tensor_tensor(out=X2[:, q, tb], in0=yg[:, 1, tb], scalar=c_all[:, TB * q + tb, 1:2],
                                           in1=X2[:, q, tb], op0=ALU.mult, op1=ALU.add).then_inc(comb2s, 1)

        @block.gpsimd
        def _(pool):
            G = nc.gpsimd

            def const(ins):
                ins.then_inc(pcon.sem, 1)

            const(G.memset(ident[:], 0.0))
            const(G.memset(tri[:], 1.0))
            const(G.memset(sel[:], 0.0))
            pool.wait_ge(pcon.sem, pcon.at(0, "sel0"))
            const(G.affine_select(out=ident[:], in_=ident[:], compare_op=ALU.not_equal, fill=1.0, base=0,
                                  pattern=[[-1, P]], channel_multiplier=1))
            const(G.affine_select(out=tri[:], in_=tri[:], compare_op=ALU.is_gt, fill=0.0, base=0,
                                  pattern=[[1, P]], channel_multiplier=-1))
            const(G.affine_select(out=sel[:], in_=sel[:], compare_op=ALU.not_equal, fill=1.0, base=0,
                                  pattern=[[-1, E]], channel_multiplier=1))
            pool.wait_ge(pcon.sem, pcon.at(0, "sela"))
            const(G.affine_select(out=sel[:], in_=sel[:], compare_op=ALU.not_equal, fill=1.0, base=-32,
                                  pattern=[[-1, E]], channel_multiplier=1))
            const(G.iota(iota_e[:], [[1, E]], base=0, channel_multiplier=0, allow_small_or_imprecise_dtypes=True))
            const(G.iota(ebase[:], [[NTOK, E]], base=0, channel_multiplier=0, allow_small_or_imprecise_dtypes=True))
            const(G.iota(thr[:], [[P, TPE]], base=0, channel_multiplier=0, allow_small_or_imprecise_dtypes=True))
            const(G.iota(iota_p[:], [[0, 1]], base=0, channel_multiplier=1, allow_small_or_imprecise_dtypes=True))
            const(G.iota(tokid[:], [[P, NT]], base=0, channel_multiplier=1))
            const(G.memset(tok_stage[:], 0))
            const(G.memset(zero_i[:], 0))
            pool.wait_ge(pcon.sem, pcon.at(0))
            pool.dma_start(table_dram.rearrange("(p n) o -> p (n o)", p=P), zero_i[:]).then_inc(tz, 16)

            def rstd_quad(q):
                pool.wait_ge(ln1.sem, ln1.at(q, "veps"))
                G.tensor_tensor(rstd[:], veps[:], neg_half[:], ALU.pow).then_inc(rstd1, 1)

            def rstd_tile(t):
                pool.wait_ge(ln2.sem, ln2.at(t, "veps"))
                G.tensor_tensor(rstdb[:], vepsb[:], neg_half[:, 0:1], ALU.pow).then_inc(rstd2, 1)

            def store_rows(t):
                pool.wait_ge(ln2.sem, ln2.at(t, "norm"))
                pool.dma_start(xn_tiles[t], xn[:]).then_inc(xn_out, 16)

            def scatter(t):
                need(pool, scat, 32 * t)
                G.tensor_copy(tok_stage[:], tokid[:, bass.ds(t, 1)]).then_inc(pst, 1)
                pool.wait_ge(pst, t + 1)
                pool.wait_ge(rt.sem, rt.at(t, "pint"))
                apart(pool)
                pool.indirect_dma_start(out=table_dram[:, :], out_offset=bass.IndirectOffsetOnAxis(
                    ap=pos_stage[:, 0:1], axis=0), in_=tok_stage[:], in_offset=None).then_inc(scat, 16)
                pool.wait_ge(scat, 32 * t + 16)
                apart(pool)
                pool.indirect_dma_start(out=table_dram[:, :], out_offset=bass.IndirectOffsetOnAxis(
                    ap=pos_stage[:, 1:2], axis=0), in_=tok_stage[:], in_offset=None).then_inc(scat, 16)

            pool.wait_ge(con.sem, con.at(0, "half"))
            rstd_quad(0)
            with pool.Fori(0, TB) as tb:
                rstd_tile(tb)
                store_rows(tb)
            pool.wait_ge(tz, 16)
            for q in range(NQ):
                if q < NQ - 1:
                    rstd_quad(q + 1)
                else:
                    pool.wait_ge(ln2.sem, ln2.at(NT - 1, "x2"))
                    G.memset(rv[:], 0.0).then_inc(cz, 1)
                    G.memset(ids_f[:], 0.0).then_inc(cz, 1)

                def tile(tb):
                    if q < NQ - 1:
                        rstd_tile(TB * (q + 1) + tb)
                        store_rows(TB * (q + 1) + tb)
                    scatter(TB * q + tb)

                if q == 0:
                    tile(0)
                with pool.Fori(1 if q == 0 else 0, TB) as tb:
                    tile(tb)

            pool.wait_ge(cph.sem, cph.at(0))
            pool.wait_ge(scat, 32 * NT)
            pool.indirect_dma_start(out=ids_i[0:SLOT_TILES, :], out_offset=None, in_=table_rows[:, :],
                                    in_offset=bass.IndirectOffsetOnAxis(ap=trow_i[0:SLOT_TILES, 0:1], axis=0))\
                .then_inc(tab_in, 16)
            pool.wait_ge(tvec.sem, tvec.at(0, "idi"))
            pool.wait_ge(xn_out, 16 * NT)
            pool.wait_ge(down_done, NCH)
            pool.wait_ge(h_lo, NCH)
            pool.wait_ge(w2_lo, NCH)
            pool.wait_ge(w1_lo, NCH)

            def gather(s, static):
                n = static % 4
                need(pool, rT, s - 3)
                G.tensor_copy(idc[:, n:n + 1], ids[:, bass.ds(s, 1)]).then_inc(idc_ok, 1)
                pool.wait_ge(idc_ok, s + 1)
                apart(pool)
                pool.indirect_dma_start(out=xg[:, n], out_offset=None, in_=xn_dram[:, :],
                                        in_offset=bass.IndirectOffsetOnAxis(ap=idc[:, n:n + 1], axis=0))\
                    .then_inc(g_in[n], 16)

            for s in range(4):
                gather(s, s)
            with pool.Fori(1, SLOT_TILES // 4) as i:
                for j in range(4):
                    gather(4 * i + j, j)

            for n in range(4):
                pool.wait_ge(yst[n], 16 * (SLOT_TILES // 4))
            pool.wait_ge(rye, SLOT_TILES)
            with pool.Fori(0, NQ) as q:
                for tb in range(TB):
                    t = TB * q + tb
                    for j in range(2):
                        G.tensor_copy(idy[:, j, tb:tb + 1], row_all[:, bass.ds(t, 1), j]).then_inc(idy_ok, 1)
                        pool.wait_ge(idy_ok, 2 * t + j + 1)
                        apart(pool)
                        pool.indirect_dma_start(out=yg[:, j, tb], out_offset=None, in_=y_dram[:, :],
                                                in_offset=bass.IndirectOffsetOnAxis(ap=idy[:, j, tb:tb + 1], axis=0))\
                            .then_inc(yg_in[tb], 16)
                pool.wait_ge(comb2s, TB * (q + 1))


_INS = ["x", "ctx_2048", "L0_xattn_w", "L0_xattn_u", "L0_ffn_gate_w", "L0_ffn_gate_b", "L0_ffn_ew1", "L0_ffn_eb1",
        "L0_ffn_ew2", "L0_ffn_eb2", "L0_ffn_sw1", "L0_ffn_sb1", "L0_ffn_sw2", "L0_ffn_sb2"]


def kernel(**inputs):
    import numpy as np
    import concourse.bacc as bacc
    from concourse import mybir as mb
    from concourse.bass_utils import run_bass_kernel_spmd

    nc = bacc.Bacc("TRN2", target_bir_lowering=False, num_devices=1)
    arrays, args = {}, []
    for name in _INS:
        a = np.ascontiguousarray(inputs[name])
        arrays[f"in_{name}"] = a
        args.append(nc.dram_tensor(f"in_{name}", a.shape, mb.dt.from_np(a.dtype), kind="ExternalInput").ap())
    shape = arrays["in_x"].shape
    args.append(nc.dram_tensor("out_0", shape, mb.dt.float32, kind="ExternalOutput").ap())
    with nc.allow_non_contiguous_dma(reason="small per-channel vectors go to columns"):
        mixed_layer(nc, *args)
    r = run_bass_kernel_spmd(nc, [arrays], core_ids=[0])
    return r.results[0]["out_0"]
```

```python
import concourse.bass as bass
from concourse import mybir
from contextlib import ExitStack



class Steps:

    def __init__(self, sem, names):
        self.sem, self.names = sem, names.split()

    def at(self, round_, name=None):
        n = len(self.names) if name is None else self.names.index(name) + 1
        return round_ * len(self.names) + n


def mixed_layer(nc, x, ctx_in, decay, bonus, gate_w, gate_b, ew1, eb1, ew2, eb2, sw1, sb1, sw2, sb2, out):
    f32, f32r, bf16 = mybir.dt.float32, mybir.dt.float32r, mybir.dt.bfloat16
    i32, u32 = mybir.dt.int32, mybir.dt.uint32
    ALU, ACT, AX = mybir.AluOpType, mybir.ActivationFunctionType, mybir.AxisListType

    P = 128
    B, T, D = x.shape
    E, _, HR = ew1.shape
    S_EXP, _, HS = sw1.shape
    GB = 4
    NQ = B // GB
    TT = 32
    TB = T // TT
    NT = NQ * TB
    QT = GB * T
    NTOK = B * T
    KC = D // P
    CB = D // 32
    HC = CB // 2
    CPS = HS // P
    CH = S_EXP * CPS
    NCH = NQ * CH
    RING = 3
    BR = 96
    TPE = NTOK // P
    SLOT_TILES = 2 * NTOK // P + E
    TROWS = E * TPE + SLOT_TILES
    EPS = 1e-5
    NEG = -1e38

    xq = x.rearrange("(q g) (tb t) c -> q g t tb c", g=GB, t=TT)
    vq = ctx_in.rearrange("(q g) (tb t) c -> q g t tb c", g=GB, t=TT)
    outq = out.rearrange("(q g) (tb t) c -> q g t tb c", g=GB, t=TT)
    sw1_c = sw1.rearrange("s (k p) (n h) -> s n p k h", p=P, h=P)
    sw2_c = sw2.rearrange("s (n h) d -> s n h d", h=P)
    ew1_c = ew1.rearrange("e (k p) h -> e p k h", p=P)

    xn_dram = nc.dram_tensor("xn_rows", (NTOK, D), f32, kind="Internal").ap()
    table_dram = nc.dram_tensor("slot_table", (TROWS * P, 1), i32, kind="Internal").ap()
    y_dram = nc.dram_tensor("expert_rows", (SLOT_TILES * P, D), f32, kind="Internal").ap()
    xn_tiles = xn_dram.rearrange("(n p) d -> n p d", p=P)
    table_rows = table_dram.rearrange("(r p) o -> r (p o)", p=P)
    y_tiles = y_dram.rearrange("(n p) d -> n p d", p=P)

    top = ExitStack()
    with top:
        def sb(name, shape, dt=f32, where=top):
            return where.enter_context(nc.sbuf_tensor(name, shape, dt))

        def sem(name):
            return top.enter_context(nc.semaphore(name))

        X2 = sb("X2", [P, NQ, TB, D])
        xhi = sb("xhi", [P, 2, KC, QT], f32r)
        xlo = sb("xlo", [P, 2, KC, QT], f32r)
        ident = sb("ident", [P, P])
        tri = sb("tri", [P, P], bf16)
        ones_bf = sb("ones_bf", [P, P], bf16)
        ones16 = sb("ones16", [P, E])
        neg_half = sb("neg_half", [P, TB])
        iota_e = sb("iota_e", [P, E])
        ebase = sb("ebase", [P, E])
        thr = sb("thr", [P, TPE])
        iota_p = sb("iota_p", [P, 1])
        tokid = sb("tokid", [P, NT], i32)
        tok_stage = sb("tok_stage", [P, 1], i32)
        u_col = sb("u_col", [P, CB])
        w_col = sb("w_col", [P, CB])
        gw_f = sb("gw_f", [P, KC, E])
        gw2 = sb("gw2", [P, KC, P], f32r)
        sel = sb("sel", [64, E])
        gb_b = sb("gb_b", [P, E])
        b1_rows = sb("b1_rows", [CH, P])
        b1_col = sb("b1_col", [P, CH])
        eb1_at = sb("eb1_at", [64, P])
        bias_f = sb("bias_f", [BR, D])
        bias_r = sb("bias_r", [BR, D], f32r)
        lgT = bias_f[0:64]
        st6 = sb("st6", [P, TB, 6])
        mv = sb("mv", [P, TB, 2])
        veps = sb("veps", [P, TB])
        rstd = sb("rstd", [P, TB])
        logits = sb("logits", [P, TB, E])
        gates = sb("gates", [P, TB, E])
        gmax = sb("gmax", [P, TB])
        gsum = sb("gsum", [P, TB])
        grec = sb("grec", [P, TB])
        gt = sb("gt", [P, E])
        top8 = sb("top8", [P, 8])
        idx8 = sb("idx8", [P, 8], u32)
        idxf = sb("idxf", [P, 2])
        oh = sb("oh", [P, 2, E])
        member = sb("member", [P, E], bf16)
        msum = sb("msum", [P, E], bf16)
        comb = sb("comb", [P, E])
        comb2 = sb("comb2", [P, E])
        cb96 = sb("cb96", [P, BR])
        chi = sb("chi", [P, E], f32r)
        cbT = sb("cbT", [BR, TB, P], f32r)
        rb = sb("rb", [P, E])
        rsel = sb("rsel", [P, 2, E])
        posf = sb("posf", [P, 2])
        pos_stage = sb("pos_stage", [P, 2], i32)
        pos_all = sb("pos_all", [P, NT, 2])
        e_all = sb("e_all", [P, NT, 2])
        row_all = sb("row_all", [P, NT, 2], i32)
        c_all = sb("c_all", [P, NT, 2])
        cnt = sb("cnt", [P, E])
        nt = sb("nt", [P, E])
        tend = sb("tend", [P, E])
        move = sb("move", [P, E])
        fin_e = sb("fin_e", [P, E])
        fin_n = sb("fin_n", [P, E])
        e_s = sb("e_s", [P, 1])
        trow = sb("trow", [P, 1])
        ts = sb("ts", [P, 1])
        trow_i = sb("trow_i", [P, 1], i32)
        zero_i = sb("zero_i", [P, (TROWS * P) // P], i32)

        shared_mem = ExitStack()
        w1_raw = sb("w1_raw", [P, RING, KC, P], where=shared_mem)
        w2_raw = sb("w2_raw", [P, RING, D], where=shared_mem)
        w1hi = sb("w1hi", [P, RING, KC, P], f32r, shared_mem)
        w1lo = sb("w1lo", [P, RING, KC, P], f32r, shared_mem)
        w2hi = sb("w2hi", [P, RING, D], f32r, shared_mem)
        w2lo = sb("w2lo", [P, RING, D], f32r, shared_mem)
        hf = sb("hf", [P, RING, QT], where=shared_mem)
        hhi = sb("hhi", [P, RING, QT], f32r, shared_mem)
        hlo = sb("hlo", [P, RING, QT], f32r, shared_mem)
        shared_mem.close()
        routed_mem = ExitStack()
        xg = sb("xg", [P, 4, D], where=routed_mem)
        xghi = sb("xghi", [P, 2, KC, P], f32r, routed_mem)
        xglo = sb("xglo", [P, 2, KC, P], f32r, routed_mem)
        e1hi = sb("e1hi", [P, 2, KC, P], f32r, routed_mem)
        e1lo = sb("e1lo", [P, 2, KC, P], f32r, routed_mem)
        e2hi = sb("e2hi", [P, 2, D], f32r, routed_mem)
        e2lo = sb("e2lo", [P, 2, D], f32r, routed_mem)
        rf = sb("rf", [P, 2, P], where=routed_mem)
        rhi = sb("rhi", [P, 2, P], f32r, routed_mem)
        rlo = sb("rlo", [P, 2, P], f32r, routed_mem)
        ysb = sb("ysb", [P, 4, D], where=routed_mem)
        idc = sb("idc", [P, 4], i32, routed_mem)
        routed_mem.close()
        combine_mem = ExitStack()
        yg = sb("yg", [P, 2, TB, D], where=combine_mem)
        idy = sb("idy", [P, 2, TB], i32, combine_mem)
        combine_mem.close()
        sb("rings", [P, 13824])

        wkv_mem = ExitStack()
        TS = T + 1
        wp = sb("wp", [P, CB, TS], where=wkv_mem)
        kp = sb("kp", [P, CB, TS], where=wkv_mem)
        kn = sb("kn", [P, TB, D], where=wkv_mem)
        vin = sb("vin", [P, TB, D], where=wkv_mem)
        vp = sb("vp", [P, CB, T], where=wkv_mem)
        mx = sb("mx", [P, HC, TS], where=wkv_mem)
        ea = sb("ea", [P, HC, TS], where=wkv_mem)
        eb = sb("eb", [P, HC, TS], where=wkv_mem)
        eu = sb("eu", [P, HC, T], where=wkv_mem)
        en = sb("en", [P, HC, T], where=wkv_mem)
        bv = sb("bv", [P, HC, TS], where=wkv_mem)
        pp = sb("pp", [P, HC, TS], where=wkv_mem)
        qq = sb("qq", [P, HC, TS], where=wkv_mem)
        wkv_mem.close()
        ew1_sb = sb("ew1_sb", [P, E, KC, P])
        ew2_sb = sb("ew2_sb", [P, E, D])
        cmp = sb("cmp", [P, E, TPE])
        rv = sb("rv", [P, P])
        rvT = sb("rvT", [1, P], i32)
        pick = sb("pick", [P, NT * 2, E])
        moved = sb("moved", [P, NT * 2])
        ohT = sb("ohT", [64, P])
        ids_i = sb("ids_i", [P, P], i32)
        ids_f = sb("ids_f", [P, P])
        ids = sb("ids", [P, P], i32)
        bslot = sb("bslot", [P, P])
        xn = kn
        xt = kn[:, 0]
        ku_sum = kn[:, :, :].rearrange("p a c -> p (a c)").rearrange("p (c t) -> p c t", t=T)
        yT = en[:].rearrange("p c t -> p (c t)").rearrange("p (tb c) -> p tb c", tb=TB)

        acc = [top.enter_context(nc.psum_tensor(f"acc{i}", [P, D], f32)) for i in range(TB)]
        up = [top.enter_context(nc.psum_tensor(f"up{i}", [P, QT], f32)) for i in range(RING)]
        misc = top.enter_context(nc.psum_tensor("misc", [P, 512], f32))
        CBT0, RANK0 = 128, 256
        t_bank = [misc, up[0]]
        r_bank = [up[1], up[2]]
        y_bank = [acc[0], acc[1]]

        x_in = [sem(f"x_in{q}") for q in range(NQ)]
        v_in, uw_in, c_in = sem("v_in"), sem("uw_in"), sem("c_in")
        w1_in = [sem(f"w1_in{i}") for i in range(RING)]
        w2_in = [sem(f"w2_in{i}") for i in range(RING)]
        ew_in, xn_out, tz, y_out, out_done = sem("ew_in"), sem("xn_out"), sem("tz"), sem("y_out"), sem("out_done")
        scat, tab_in = sem("scat"), sem("tab_in")
        g_in = [sem(f"g_in{i}") for i in range(4)]
        yg_in = [sem(f"yg_in{i}") for i in range(TB)]
        w1_hi, w2_hi, h_hi, h_full = sem("w1_hi"), sem("w2_hi"), sem("h_hi"), sem("h_full")
        w1_lo, w2_lo, h_lo = sem("w1_lo"), sem("w2_lo"), sem("h_lo")
        up_done, down_done, acc_ready = sem("up_done"), sem("down_done"), sem("acc_ready")
        acc_free = sem("acc_free")
        rstd1, rstd2 = sem("rstd1"), sem("rstd2")
        gexp, xhi_ok, cbt_ok = sem("gexp"), sem("xhi_ok"), sem("cbt_ok")
        xT_ps, gate_ps, lg_ps, rank_ps = sem("xT_ps"), sem("gate_ps"), sem("lg_ps"), sem("rank_ps")
        b1_ps, cnt_ps, rv_ps, ids_ps, bs_ps = sem("b1_ps"), sem("cnt_ps"), sem("rv_ps"), sem("ids_ps"), sem("bs_ps")
        b1_ok = sem("b1_ok")
        ln1 = Steps(sem("ln1"), "s0 s1 s2 s3 a0 a1 a2 a3 veps n0 n1 n2 n3 tk tv")
        wscan = sem("wscan")
        wz = Steps(sem("wz"), "wm z z2")
        wkv = Steps(sem("wkv"), "bmul sp sq aq ap den ev num nt nr y")
        wrelu = Steps(sem("wrelu"), "b a n u")
        wexp = Steps(sem("wexp"), "b a n u ln rec")
        ku = sem("ku")
        ty = sem("ty")
        ln2 = Steps(sem("ln2"), "s0 s1 s2 s3 a0 a1 a2 a3 veps")
        norm, xlo_ok, x2_ok = sem("norm"), sem("xlo_ok"), sem("x2_ok")
        gsm = Steps(sem("gsm"), "parts lg max sub sum rec gates")
        rt = Steps(sem("rt"), "gt max idx idxf c e o1 o2 mem wc comb hi h0 h1 lo rank m1 m2 pos pint pall msum")
        con = Steps(sem("con"), "k0 w0 ea eb bv half bias0 ms ones o16 cb0 cb1 cb2 gz wcol ghi glo bhi1 bhi2 blo bhi3")
        pcon = Steps(sem("pcon"), "id0 tri0 sel0 id tri sela selb ie eb thr ip tok stage z")
        cph = Steps(sem("cph"), "cnt cmp nt tend fin etile ebase es ctiles ts trow0 rve move trow oh tri mul shift row")
        tvec = Steps(sem("tvec"), "rvT ohT idf idi bs")
        pst, cz = sem("pst"), sem("cz")

        rx, rT, rup, ry = sem("rx"), sem("rT"), sem("rup"), sem("ry")
        r1hi, r2hi, rhh, rff, rxh = sem("r1hi"), sem("r2hi"), sem("rhh"), sem("rff"), sem("rxh")
        r1lo, r2lo, rhl, rxl = sem("r1lo"), sem("r2lo"), sem("rhl"), sem("rxl")
        rye = [sem("rye0"), sem("rye1")]
        idc_ok = sem("idc_ok")
        yst = [sem(f"yst{i}") for i in range(4)]
        idy_ok, comb1, comb2s = sem("idy_ok"), sem("comb1"), sem("comb2s")

        block = top.enter_context(nc.Block())

        def need(eng, s, value):
            if not isinstance(value, int) or value > 0:
                eng.wait_ge(s, value)

        def apart(eng):
            eng.nop(nofuse=True)

        def schedule(q, step, head, half, mid, tile, late=None):
            eng = step.engine
            c0 = CH * q
            for j in range(2):
                step(c0 + j)
                head(j)
            at = c0 + 2
            if q < NQ - 1:
                if q == 0:
                    for s in range(2):
                        for j in range(9):
                            step(at + 9 * s + j)
                            half(s, j)
                else:
                    with eng.Fori(0, 2) as s:
                        for j in range(9):
                            step(at + 9 * s + j, at + j)
                            half(s, j)
                at += 18
                mid()
            if q == 0:
                for j in range(3):
                    step(at + j)
                    tile(0, j)
            with eng.Fori(1 if q == 0 else 0, TB - 1) as tb:
                for j in range(3):
                    step(at + 3 * tb + j, at + j)
                    tile(tb, j)
            at += 3 * (TB - 1)
            for j in range(3):
                step(at + j)
                tile(TB - 1, j)
            at += 3
            if q == NQ - 1:
                for j in range(3):
                    step(at + j)
                    late(j)
                at += 3
                rest = (c0 + CH - at) // 3
                with eng.Fori(0, rest - 1) as i:
                    for j in range(3):
                        step(at + 3 * i + j, at + j)
                at += 3 * (rest - 1)
                for j in range(3):
                    step(at + j)
                at += 3
            assert at == c0 + CH

        def uses(c, static):
            return (c - static) // 3 + static // 3 + 1 if not isinstance(c, int) else c // 3 + 1

        def routed_rounds(eng, w1, x, w2, h, y, parity):
            def one(s, static):
                last = s if isinstance(s, int) else 0
                h(s, static)
                if last + 2 < SLOT_TILES:
                    w1(s + 2, static + 2)
                    x(s + 2, static + 2)
                if last + 1 < SLOT_TILES:
                    w2(s + 1, static + 1)
                if (not isinstance(s, int) or s) and (static - 1) % 2 == parity:
                    y(s - 1, static - 1)

            for s in range(2):
                w1(s, s)
                x(s, s)
            w2(0, 0)
            for s in range(5):
                one(s, s)
            rounds = (SLOT_TILES - 2 - 5) // 4
            with eng.Fori(0, rounds) as i:
                for j in range(5, 9):
                    one(4 * i + j, j)
            for s in range(5 + 4 * rounds, SLOT_TILES):
                one(s, s)
            if (SLOT_TILES - 1) % 2 == parity:
                y(SLOT_TILES - 1, SLOT_TILES - 1)

        def y_taken(s, static):
            return (s - static) // 2 + static // 2 + 1

        @block.sync
        def _(sp):
            def load_quad(q):
                for g in range(GB):
                    sp.dma_start(X2[32 * g:32 * g + 32, q], xq[q, g]).then_inc(x_in[q], 16)
                need(sp, ln1.sem, ln1.at(q - 1) if q else 0)
                for g in range(GB):
                    sp.dma_start(vin[32 * g:32 * g + 32], vq[q, g]).then_inc(v_in, 16)

            def load_w1(c, static, n):
                need(sp, w1_hi, c - 2)
                need(sp, w1_lo, c - 2)
                sp.dma_start(w1_raw[:, static % RING], sw1_c[n // CPS, n % CPS]).then_inc(w1_in[static % RING], 16)

            def load_w2(c, static, n):
                need(sp, w2_hi, c - 2)
                need(sp, w2_lo, c - 2)
                sp.dma_start(w2_raw[:, static % RING], sw2_c[n // CPS, n % CPS]).then_inc(w2_in[static % RING], 16)

            load_quad(0)
            for k, v in ((u_col, bonus), (w_col, decay)):
                for g in range(GB):
                    sp.dma_start(k[32 * g:32 * g + 32], v.rearrange("(b p) -> p b", p=32)).then_inc(uw_in, 16)
            for c in range(RING):
                load_w1(c, c, c)
            sp.dma_start(gw_f[:], gate_w.rearrange("(k p) e -> p k e", p=P)).then_inc(c_in, 16)
            sp.dma_start(gb_b[:], gate_b.rearrange("(o e) -> o e", o=1).broadcast_to([P, E])).then_inc(c_in, 16)
            sp.dma_start(b1_rows[:], sb1.rearrange("s (n h) -> (s n) h", h=P)).then_inc(c_in, 16)
            sp.dma_start(eb1_at[32:32 + E], eb1).then_inc(c_in, 16)
            sp.wait_ge(con.sem, con.at(0, "bias0"))
            for r in range(3):
                sp.dma_start(bias_f[32 * r:32 * r + E], eb2).then_inc(c_in, 16)
                sp.dma_start(bias_f[32 * r + E:32 * r + E + S_EXP], sb2).then_inc(c_in, 16)

            for q in range(NQ):
                if q < NQ - 1:
                    load_quad(q + 1)
                last = q == NQ - 1
                n3 = 9
                c0 = CH * q
                if last:
                    sp.wait_ge(xT_ps, NT)
                    sp.wait_ge(xn_out, 16 * NT)
                for n in range(3):
                    load_w2(c0 + n, c0 + n, n)
                    load_w1(c0 + n + 3, c0 + n + 3, n + 3)
                with sp.Fori(1, n3) as i:
                    for j in range(3):
                        n = 3 * i + j
                        load_w2(c0 + n, c0 + j, n)
                        load_w1(c0 + n + 3, c0 + j, n + 3)
                    if last:
                        sp.dma_start(ew1_sb[:, i], ew1_c[i]).then_inc(ew_in, 16)
                        sp.dma_start(ew2_sb[:, i], ew2[i]).then_inc(ew_in, 16)
                for n in range(3 * n3, CH):
                    load_w2(c0 + n, c0 + n, n)
                    if c0 + n + 3 < NCH:
                        load_w1(c0 + n + 3, c0 + n + 3, (n + 3) % CH)
                if last:
                    for i in [0, *range(n3, E)]:
                        sp.dma_start(ew1_sb[:, i], ew1_c[i]).then_inc(ew_in, 16)
                        sp.dma_start(ew2_sb[:, i], ew2[i]).then_inc(ew_in, 16)

            def store_y(s, static):
                sp.wait_ge(rye[static % 2], y_taken(s, static))
                sp.dma_start(y_tiles[s], ysb[:, static % 4]).then_inc(yst[static % 4], 16)

            with sp.Fori(0, SLOT_TILES // 4) as i:
                for j in range(4):
                    store_y(4 * i + j, j)
            with sp.Fori(0, NQ) as q:
                sp.wait_ge(comb2s, TB * (q + 1))
                for g in range(GB):
                    sp.dma_start(outq[q, g], X2[32 * g:32 * g + 32, q]).then_inc(out_done, 16)
            sp.wait_ge(out_done, 16 * GB * NQ)

        @block.tensor
        def _(pe):
            def splits(o, lhs, rhs, start, stop):
                nc.tensor.matmul(o, lhs[0], rhs[0], start=start, stop=False)
                nc.tensor.matmul(o, lhs[0], rhs[1], start=False, stop=False)
                return nc.tensor.matmul(o, lhs[1], rhs[0], start=False, stop=stop)

            def up_product(c, static, q):
                slot, par = static % RING, q % 2
                need(pe, w1_hi, c + 1)
                need(pe, w1_lo, c + 1)
                need(pe, h_hi, c - 2)
                need(pe, h_full, c - 2)
                for k in range(KC):
                    last = splits(up[slot][:], (w1hi[:, slot, k], w1lo[:, slot, k]),
                                  (xhi[:, par, k], xlo[:, par, k]), k == 0, k == KC - 1)
                last.then_inc(up_done, 1)

            def block_ready(q):
                pe.wait_ge(xhi_ok, TB * (q + 1))
                pe.wait_ge(xlo_ok, TB * (q + 1))

            class step:
                engine = pe

                def __new__(cls, c, static=None):
                    static = c if static is None else static
                    q, n = static // CH, static % CH
                    slot = static % RING
                    ahead = static + 2
                    if isinstance(c, int) and ahead % CH == 0 and ahead < NCH:
                        block_ready(ahead // CH)
                    if not isinstance(c, int) or ahead < NCH:
                        up_product(c + 2, ahead, ahead // CH)
                    need(pe, w2_hi, c + 1)
                    need(pe, w2_lo, c + 1)
                    need(pe, h_hi, c + 1)
                    first = isinstance(c, int) and n == 0
                    for t in range(TB):
                        hh = hhi[:, slot, P * t:P * t + P]
                        if first and q:
                            pe.wait_ge(acc_free, TB * (q - 1) + t + 1)
                        nc.tensor.matmul(acc[t][:], hh, w2hi[:, slot], start=first, stop=False)
                        nc.tensor.matmul(acc[t][:], hh, w2lo[:, slot], start=False, stop=False)
                    need(pe, h_lo, c + 1)
                    for t in range(TB):
                        last = nc.tensor.matmul(acc[t][:], hlo[:, slot, P * t:P * t + P], w2hi[:, slot],
                                                start=False, stop=False)
                    last.then_inc(down_done, 1)
                    if isinstance(c, int) and n == CH - 1:
                        pe.wait_ge(cbt_ok, TB * (q + 1))
                        for t in range(TB):
                            last = nc.tensor.matmul(acc[t][:], cbT[:, t], bias_r[:], start=False, stop=True)
                        last.then_inc(acc_ready, 1)

            def transpose_x(t, rows, bank):
                pe.wait_ge(norm, t + 1)
                for k in range(KC):
                    last = nc.tensor.transpose(bank[:, P * k:P * k + P], rows[:, P * k:P * k + P], ident[:])
                last.then_inc(xT_ps, 1)

            def gate_product(q):
                pe.wait_ge(con.sem, con.at(0))
                block_ready(q)
                for k in range(KC):
                    nc.tensor.matmul(misc[:], gw2[:, k], xhi[:, q % 2, k], start=k == 0, stop=False)
                    last = nc.tensor.matmul(misc[:], gw2[:, k], xlo[:, q % 2, k], start=False, stop=k == KC - 1)
                last.then_inc(gate_ps, 1)

            def gate_transpose(q):
                pe.wait_ge(gsm.sem, gsm.at(q, "parts"))
                for tb in range(TB):
                    last = nc.tensor.matmul(misc[:, E * tb:E * tb + E], lgT[:, P * tb:P * tb + P], sel[:],
                                            start=True, stop=True)
                last.then_inc(lg_ps, 1)

            def routing_products(t):
                pe.wait_ge(rt.sem, rt.at(t, "lo"))
                nc.tensor.transpose(misc[0:BR, CBT0:CBT0 + P], cb96[:], ident[:])
                nc.tensor.matmul(misc[:, RANK0:RANK0 + E], tri[:], member[:], start=True, stop=False)
                nc.tensor.matmul(misc[:, RANK0:RANK0 + E], ones_bf[:], msum[:], start=False, stop=True)\
                    .then_inc(rank_ps, 1)

            pe.wait_ge(pcon.sem, pcon.at(0, "tri"))
            pe.wait_ge(c_in, 16 * 10)
            nc.tensor.transpose(misc[:, 0:CH], b1_rows[:], ident[0:CH, 0:CH]).then_inc(b1_ps, 1)
            pe.wait_ge(b1_ok, 1)
            for tb in range(TB):
                transpose_x(tb, xn[:, tb], acc[tb])
            block_ready(0)
            up_product(0, 0, 0)
            up_product(1, 1, 0)
            gate_product(0)
            for q in range(NQ):
                def head(j, q=q):
                    if j == 0:
                        gate_transpose(q)

                def tile(tb, j, q=q):
                    t = TB * q + tb
                    if j == 0 and q < NQ - 1:
                        pe.wait_ge(gsm.sem, gsm.at(q, "lg"))
                        pe.wait_ge(cbt_ok, t)
                        pe.wait_ge(rt.sem, t * len(rt.names))
                        transpose_x(t + TB, xt, misc)
                    if j == 1:
                        if q < NQ - 1:
                            pe.wait_ge(xhi_ok, t + TB + 1)
                            pe.wait_ge(xlo_ok, t + TB + 1)
                        else:
                            pe.wait_ge(gsm.sem, gsm.at(q, "lg"))
                            pe.wait_ge(cbt_ok, t)
                            pe.wait_ge(rt.sem, t * len(rt.names))
                        routing_products(t)

                def late(j):
                    if j == 0:
                        pe.wait_ge(rt.sem, rt.at(NT - 1))
                        pe.wait_ge(cbt_ok, NT)
                        nc.tensor.matmul(misc[:, 0:E], ones_bf[:], msum[:], start=True, stop=True)\
                            .then_inc(cnt_ps, 1)

                schedule(q, step, head, lambda s, j: None, lambda: None, tile, late)
                if q < NQ - 1:
                    pe.wait_ge(rt.sem, rt.at(TB * (q + 1) - 1, "rank"))
                    gate_product(q + 1)

            pe.wait_ge(cph.sem, cph.at(0))
            nc.tensor.transpose(misc[:, 0:P], rv[:], ident[:]).then_inc(rv_ps, 1)
            pe.wait_ge(tvec.sem, tvec.at(0, "idf"))
            nc.tensor.transpose(misc[:, P:2 * P], ids_f[:], ident[:]).then_inc(ids_ps, 1)
            nc.tensor.matmul(misc[:, 2 * P:3 * P], eb1_at[32:32 + E], ohT[32:32 + E], start=True, stop=True)\
                .then_inc(bs_ps, 1)
            pe.wait_ge(tvec.sem, tvec.at(0))

            def routed_T(s, static):
                i = static % 2
                pe.wait_ge(g_in[static % 4], 16 * ((s - static) // 4 + static // 4 + 1))
                need(pe, rxh, s - 1)
                need(pe, rxl, s - 1)
                for k in range(KC):
                    last = nc.tensor.transpose(t_bank[i][:, P * k:P * k + P], xg[:, static % 4, P * k:P * k + P],
                                               ident[:])
                last.then_inc(rT, 1)

            def routed_up(s, static):
                i = static % 2
                pe.wait_ge(rxh, s + 1)
                pe.wait_ge(rxl, s + 1)
                pe.wait_ge(r1hi, s + 1)
                pe.wait_ge(r1lo, s + 1)
                need(pe, rhh, s - 1)
                need(pe, rff, s - 1)
                for k in range(KC):
                    last = splits(r_bank[i][:, 0:P], (e1hi[:, i, k], e1lo[:, i, k]), (xghi[:, i, k], xglo[:, i, k]),
                                  k == 0, k == KC - 1)
                last.then_inc(rup, 1)

            def routed_down(s, static):
                i = static % 2
                pe.wait_ge(r2hi, s + 1)
                pe.wait_ge(r2lo, s + 1)
                pe.wait_ge(rhh, s + 1)
                pe.wait_ge(rhl, s + 1)
                need(pe, rye[i], y_taken(s, static) - 1)
                splits(y_bank[i][:], (rhi[:, i], rlo[:, i]), (e2hi[:, i], e2lo[:, i]), True, True).then_inc(ry, 1)

            pe.wait_ge(acc_free, TB * NQ)
            routed_T(0, 0)
            routed_T(1, 1)
            routed_up(0, 0)
            NL = SLOT_TILES // 4 - 1
            for s in range(4):
                routed_T(s + 2, s + 2)
                routed_up(s + 1, s + 1)
                routed_down(s, s)
            with pe.Fori(1, NL) as it:
                for j in range(4):
                    s = 4 * it + j
                    routed_T(s + 2, j + 2)
                    routed_up(s + 1, j + 1)
                    routed_down(s, j)
            for s in range(4 * NL, SLOT_TILES):
                if s + 2 < SLOT_TILES:
                    routed_T(s + 2, s + 2)
                if s + 1 < SLOT_TILES:
                    routed_up(s + 1, s + 1)
                routed_down(s, s)

        @block.scalar
        def _(act):
            def split_w1(c, static):
                slot = static % RING
                act.wait_ge(w1_in[slot], 16 * uses(c, static))
                need(act, up_done, c - 2)
                nc.scalar.copy(w1hi[:, slot], w1_raw[:, slot]).then_inc(w1_hi, 1)

            class step:
                engine = act

                def __new__(cls, c, static=None):
                    static = c if static is None else static
                    slot, n = static % RING, static % CH
                    cc = c % CH if isinstance(c, int) else c - CH * (static // CH)
                    bias = b1_col[:, bass.ds(cc, 1)]
                    act.wait_ge(b1_ok, 1)
                    act.wait_ge(up_done, c + 1)
                    need(act, down_done, c - 2)
                    nc.scalar.activation(hhi[:, slot], up[slot][:], ACT.Gelu, bias=bias).then_inc(h_hi, 1)
                    act.wait_ge(b1_ok, 1)
                    need(act, h_lo, c - 2)
                    nc.scalar.activation(hf[:, slot], up[slot][:], ACT.Gelu, bias=bias).then_inc(h_full, 1)
                    act.wait_ge(w2_in[slot], 16 * uses(c, static))
                    nc.scalar.copy(w2hi[:, slot], w2_raw[:, slot]).then_inc(w2_hi, 1)
                    if not isinstance(c, int) or c + 3 < NCH:
                        split_w1(c + 3, static + 3)

            exps = {"b": (pp[:, :, 1:], eb[:, :, 1:], -1.0, "num"), "a": (pp[:, :, 1:], ea[:, :, 1:], 1.0, "nr"),
                    "n": (qq[:, :, 1:], en[:], 1.0, None), "u": (qq[:, :, 1:], eu[:], -1.0, None)}

            def wkv_relu(r, name):
                z, buf, sign, frees = exps[name]
                act.wait_ge(wz.sem, wz.at(r, "z" if name in "ba" else "z2"))
                if not isinstance(r, int) or r:
                    if name in "ba":
                        act.wait_ge(wkv.sem, wkv.at(r - 1, frees))
                    else:
                        act.wait_ge(x2_ok, r)
                nc.scalar.activation(buf, z, ACT.Relu, scale=sign).then_inc(wrelu.sem, 1)

            def wkv_exp(r, name):
                _, buf, _, _ = exps[name]
                act.wait_ge(wrelu.sem, wrelu.at(r, name))
                nc.scalar.activation(buf, buf, ACT.Exp, scale=-1.0).then_inc(wexp.sem, 1)

            def wkv_reciprocal(r):
                act.wait_ge(wkv.sem, wkv.at(r, "den"))
                nc.scalar.activation(en[:], ea[:, :, 1:], ACT.Ln).then_inc(wexp.sem, 1)
                act.wait_ge(wexp.sem, wexp.at(r, "ln"))
                nc.scalar.activation(en[:], en[:], ACT.Exp, scale=-1.0).then_inc(wexp.sem, 1)

            def gate_exp(q):
                act.wait_ge(gsm.sem, gsm.at(q, "sub"))
                nc.scalar.activation(gates[:], gates[:], ACT.Exp).then_inc(gexp, 1)

            def x_hi(t, par, tb, bank):
                act.wait_ge(xT_ps, t + 1)
                nc.scalar.copy(xhi[:, par, :, bass.ds(P * tb, P)],
                               bank[:].rearrange("p (k n) -> p k n", k=KC)).then_inc(xhi_ok, 1)

            def combine_T(t, tb, q):
                act.wait_ge(rank_ps, t + 1)
                need(act, acc_ready, q)
                nc.scalar.copy(cbT[:, tb], misc[0:BR, CBT0:CBT0 + P]).then_inc(cbt_ok, 1)

            nc.scalar.preload_act_table_set("natural_log_exp_and_others")
            for c in range(RING):
                split_w1(c, c)
            act.wait_ge(b1_ps, 1)
            nc.scalar.copy(b1_col[:], misc[:, 0:CH]).then_inc(b1_ok, 1)
            act.wait_ge(b1_ok, 1)
            for s in range(2):
                for name in "ba":
                    wkv_relu(s, name)
                    wkv_exp(s, name)
                for name in "nu":
                    wkv_relu(s, name)
                for name in "nu":
                    wkv_exp(s, name)
                wkv_reciprocal(s)
            for tb in range(TB):
                x_hi(tb, 0, tb, acc[tb])

            for q in range(NQ):
                def head(j, q=q):
                    if j == 1:
                        gate_exp(q)

                def half(s, j, q=q):
                    r = 2 * (q + 1) + s
                    if j == 1:
                        wkv_relu(r, "b")
                        wkv_relu(r, "a")
                    if j == 2:
                        wkv_relu(r, "n")
                        wkv_relu(r, "u")
                    if j == 3:
                        nc.scalar.preload_act_table_set("natural_log_exp_and_others")
                        for name in "banu":
                            wkv_exp(r, name)
                    if j == 6:
                        nc.scalar.preload_act_table_set("natural_log_exp_and_others")
                        wkv_reciprocal(r)

                def tile(tb, j, q=q):
                    if j == 1 and q < NQ - 1:
                        if q:
                            act.wait_ge(up_done, CH * q)
                        x_hi(TB * (q + 1) + tb, (q + 1) % 2, tb, misc)
                    if j == 2:
                        combine_T(TB * q + tb, tb, q)

                schedule(q, step, head, half, lambda: None, tile, lambda j: None)

            act.wait_ge(tvec.sem, tvec.at(0))
            act.wait_ge(ew_in, 32 * E)
            act.wait_ge(down_done, NCH)
            act.wait_ge(h_lo, NCH)
            act.wait_ge(w1_lo, NCH)
            act.wait_ge(w2_lo, NCH)
            act.wait_ge(w2_hi, NCH)
            act.wait_ge(h_full, NCH)

            def routed_w1(s, static):
                e = act.value_load(rvT[0:1, bass.ds(s, 1)], min_val=0, max_val=E - 1)
                need(act, rup, s - 1)
                nc.scalar.copy(e1hi[:, static % 2], ew1_sb[:, e]).then_inc(r1hi, 1)

            def routed_w2(s, static):
                e = act.value_load(rvT[0:1, bass.ds(s, 1)], min_val=0, max_val=E - 1)
                need(act, ry, s - 1)
                nc.scalar.copy(e2hi[:, static % 2], ew2_sb[:, e]).then_inc(r2hi, 1)

            def routed_x(s, static):
                i = static % 2
                act.wait_ge(rT, s + 1)
                need(act, rup, s - 1)
                nc.scalar.copy(xghi[:, i], t_bank[i][:].rearrange("p (k n) -> p k n", k=KC)).then_inc(rxh, 1)

            def routed_h(s, static):
                i = static % 2
                b = bslot[:, bass.ds(s, 1)]
                act.wait_ge(tvec.sem, tvec.at(0))
                act.wait_ge(rup, s + 1)
                need(act, ry, s - 1)
                nc.scalar.activation(rhi[:, i], r_bank[i][:, 0:P], ACT.Gelu, bias=b).then_inc(rhh, 1)
                act.wait_ge(tvec.sem, tvec.at(0))
                need(act, rhl, s - 1)
                nc.scalar.activation(rf[:, i], r_bank[i][:, 0:P], ACT.Gelu, bias=b).then_inc(rff, 1)

            def routed_y(s, static):
                n = static % 4
                act.wait_ge(ry, s + 1)
                need(act, yst[n], 16 * ((s - static) // 4 + static // 4))
                nc.scalar.copy(ysb[:, n], y_bank[1][:]).then_inc(rye[1], 1)

            routed_rounds(act, routed_w1, routed_x, routed_w2, routed_h, routed_y, 1)

        @block.vector
        def _(dve):
            V = nc.vector

            def f(ap):
                return ap.bitcast(f32)

            def split_w1(c, static):
                slot = static % RING
                dve.wait_ge(w1_hi, c + 1)
                dve.wait_ge(w1_in[slot], 16 * uses(c, static))
                need(dve, up_done, c - 2)
                V.tensor_tensor(w1lo[:, slot], w1_raw[:, slot], f(w1hi[:, slot]), ALU.subtract).then_inc(w1_lo, 1)

            class step:
                engine = dve

                def __new__(cls, c, static=None):
                    static = c if static is None else static
                    slot = static % RING
                    dve.wait_ge(h_hi, c + 1)
                    dve.wait_ge(h_full, c + 1)
                    need(dve, down_done, c - 2)
                    V.tensor_tensor(hlo[:, slot], hf[:, slot], f(hhi[:, slot]), ALU.subtract).then_inc(h_lo, 1)
                    dve.wait_ge(w2_hi, c + 1)
                    dve.wait_ge(w2_in[slot], 16 * uses(c, static))
                    V.tensor_tensor(w2lo[:, slot], w2_raw[:, slot], f(w2hi[:, slot]), ALU.subtract).then_inc(w2_lo, 1)
                    if not isinstance(c, int) or c + 3 < NCH:
                        split_w1(c + 3, static + 3)

            def const(ins):
                ins.then_inc(con.sem, 1)

            def after(steps, r, name):
                dve.wait_ge(steps.sem, steps.at(r, name))

            def ln1_stats(q):
                dve.wait_ge(x_in[q], 16 * GB)
                if q:
                    dve.wait_ge(norm, TB * q)
                for tb in range(TB):
                    V.bn_stats(st6[:, tb], X2[:, q, tb]).then_inc(ln1.sem, 1)
                for tb in range(TB):
                    after(ln1, q, f"s{tb}")
                    V.bn_aggr(mv[:, tb], st6[:, tb]).then_inc(ln1.sem, 1)
                after(ln1, q, "a3")
                V.tensor_scalar(veps[:], mv[:, :, 1], EPS, None, ALU.add).then_inc(ln1.sem, 1)

            def ln1_apply(q):
                dve.wait_ge(rstd1, q + 1)
                if q:
                    dve.wait_ge(xn_out, 16 * TB * q)
                    dve.wait_ge(xT_ps, TB * q)
                for tb in range(TB):
                    V.tensor_scalar(kn[:, tb], X2[:, q, tb], mv[:, tb, 0:1], rstd[:, tb:tb + 1],
                                    ALU.subtract, ALU.mult).then_inc(ln1.sem, 1)
                after(ln1, q, "n3")
                V.transpose(kp[:, :, 1:].rearrange("p c (tb t) -> p c tb t", t=TT),
                            kn[:].rearrange("p tb (c k) -> p c tb k", k=32)).then_inc(ln1.sem, 1)

            def v_transpose(q):
                dve.wait_ge(v_in, 16 * GB * (q + 1))
                V.transpose(vp[:].rearrange("p c (tb t) -> p c tb t", t=TT),
                            vin[:].rearrange("p tb (c k) -> p c tb k", k=32)).then_inc(ln1.sem, 1)

            def flat(a):
                return a.rearrange("p c t -> p (c t)")

            m_prev = mx[:, :, 0:T]

            def wkv_scan(q, s):
                cs, r = bass.ds(HC * s, HC), 2 * q + s
                after(ln1, q, "tk")
                if not isinstance(r, int) or r:
                    after(wz, r - 1, "z2")
                V.tensor_tensor_scan(flat(mx[:]), flat(wp[:, cs, :]), flat(kp[:, cs, :]), 0.0,
                                     ALU.add, ALU.max).then_inc(wscan, 1)

            def wkv_z(q, s):
                cs, r = bass.ds(HC * s, HC), 2 * q + s
                dve.wait_ge(wscan, r + 1)
                if not isinstance(r, int) or r:
                    after(wkv, r - 1, "ap")
                V.tensor_tensor(qq[:, :, 1:], wp[:, cs, 1:], m_prev, ALU.add).then_inc(wz.sem, 1)
                after(wz, r, "wm")
                V.tensor_tensor(pp[:, :, 1:], kp[:, cs, 1:], qq[:, :, 1:], ALU.subtract).then_inc(wz.sem, 1)

            def wkv_z2(q, s):
                cs, r = bass.ds(HC * s, HC), 2 * q + s
                dve.wait_ge(ku, r + 1)
                after(wz, r, "z")
                V.tensor_tensor(qq[:, :, 1:], ku_sum[:, cs, :], m_prev, ALU.subtract).then_inc(wz.sem, 1)

            def wkv_part(q, s, part):
                r = 2 * q + s
                cs = bass.ds(HC * s, HC)
                v_h = vp[:, cs, :]
                p_prev, q_prev = pp[:, :, 0:T], qq[:, :, 0:T]

                def do(ins):
                    ins.then_inc(wkv.sem, 1)

                if part == 0:
                    wkv_scan(q, s)
                    wkv_z(q, s)
                elif part == 1:
                    wkv_z2(q, s)
                elif part == 4:
                    after(ln1, q, "tv")
                    if not isinstance(r, int) or r:
                        after(wkv, r - 1, "y")
                    after(wexp, r, "b")
                    do(V.tensor_tensor(bv[:, :, 1:], eb[:, :, 1:], v_h, ALU.mult))
                    after(wexp, r, "a")
                    after(wkv, r, "bmul")
                    do(V.tensor_tensor_scan(flat(pp[:]), flat(ea[:]), flat(bv[:]), 0.0, ALU.mult, ALU.add))
                    after(wrelu, r, "u")
                    do(V.tensor_tensor_scan(flat(qq[:]), flat(ea[:]), flat(eb[:]), 0.0, ALU.mult, ALU.add))
                elif part == 5:
                    after(wkv, r, "sq")
                    after(wexp, r, "n")
                    do(V.tensor_tensor(ea[:, :, 1:], en[:], q_prev, ALU.mult))
                    do(V.tensor_tensor(bv[:, :, 1:], en[:], p_prev, ALU.mult))
                    after(wexp, r, "u")
                    after(wkv, r, "ap")
                    do(V.tensor_tensor(ea[:, :, 1:], ea[:, :, 1:], eu[:], ALU.add))
                elif part == 6:
                    do(V.tensor_tensor(eb[:, :, 1:], eu[:], v_h, ALU.mult))
                    after(wkv, r, "ev")
                    do(V.tensor_tensor(bv[:, :, 1:], bv[:, :, 1:], eb[:, :, 1:], ALU.add))
                elif part == 7:
                    after(wexp, r, "rec")
                    do(V.tensor_tensor(ea[:, :, 1:], ea[:, :, 1:], en[:], ALU.mult))
                    after(wkv, r, "nt")
                    do(V.scalar_tensor_tensor(out=en[:], in0=ea[:, :, 1:], scalar=-2.0, in1=en[:],
                                              op0=ALU.add, op1=ALU.mult))
                    after(wkv, r, "nr")
                    do(V.scalar_tensor_tensor(out=eu[:], in0=en[:], scalar=-1.0, in1=bv[:, :, 1:],
                                              op0=ALU.mult, op1=ALU.mult))
                elif part == 8:
                    wkv_back(q, s)

            def wkv_back(q, s):
                r = 2 * q + s
                after(wkv, r, "y")
                cols = bass.ds(32 * HC * s, 32 * HC)
                V.transpose(yT.rearrange("p tb (c k) -> p tb c k", k=32),
                            eu[:].rearrange("p c (tb t) -> p tb c t", t=TT)).then_inc(ty, 1)
                dve.wait_ge(ty, r + 1)
                V.tensor_tensor(X2[:, q, :, cols], X2[:, q, :, cols], yT, ALU.add)\
                    .then_inc(x2_ok, 1)

            def ln2_quad(q):
                dve.wait_ge(x2_ok, 2 * (q + 1))
                after(ln1, q, "n3")
                for tb in range(TB):
                    V.bn_stats(st6[:, tb], X2[:, q, tb]).then_inc(ln2.sem, 1)
                for tb in range(TB):
                    after(ln2, q, f"s{tb}")
                    V.bn_aggr(mv[:, tb], st6[:, tb]).then_inc(ln2.sem, 1)
                after(ln2, q, "a3")
                V.tensor_scalar(veps[:], mv[:, :, 1], EPS, None, ALU.add).then_inc(ln2.sem, 1)

            def ln2_apply(q, tb, t, rows):
                dve.wait_ge(rstd2, q + 1)
                if q:
                    dve.wait_ge(xn_out, 16 * t)
                    dve.wait_ge(xT_ps, t)
                V.tensor_scalar(rows, X2[:, q, tb], mv[:, tb, 0:1],
                                rstd[:, bass.ds(tb, 1)], ALU.subtract, ALU.mult).then_inc(norm, 1)

            def x_lo(tb, par, t, bank):
                dve.wait_ge(xhi_ok, t + 1)
                tok = bass.ds(P * tb, P)
                V.tensor_tensor(xlo[:, par, :, tok], bank[:].rearrange("p (k n) -> p k n", k=KC),
                                f(xhi[:, par, :, tok]), ALU.subtract).then_inc(xlo_ok, 1)

            def spread(col):
                return col.unsqueeze(2).broadcast_to([P, TB, E])

            def gate_parts(q):
                dve.wait_ge(gate_ps, q + 1)
                V.tensor_copy(lgT[:], misc[0:64]).then_inc(gsm.sem, 1)

            def gates_max(q):
                dve.wait_ge(lg_ps, q + 1)
                V.tensor_tensor(logits[:], misc[:, 0:TB * E].rearrange("p (t e) -> p t e", e=E),
                                gb_b[:].unsqueeze(1).broadcast_to([P, TB, E]), ALU.add).then_inc(gsm.sem, 1)
                after(gsm, q, "lg")
                V.tensor_reduce(gmax[:], logits[:], AX.X, ALU.max).then_inc(gsm.sem, 1)
                after(gsm, q, "max")
                V.tensor_tensor(gates[:], logits[:], spread(gmax[:]), ALU.subtract).then_inc(gsm.sem, 1)

            def gates_norm(q):
                dve.wait_ge(gexp, q + 1)
                V.tensor_reduce(gsum[:], gates[:], AX.X, ALU.add).then_inc(gsm.sem, 1)
                after(gsm, q, "sum")
                V.reciprocal(grec[:], gsum[:]).then_inc(gsm.sem, 1)
                after(gsm, q, "rec")
                V.tensor_tensor(gates[:], gates[:], spread(grec[:]), ALU.mult).then_inc(gsm.sem, 1)

            def rdo(ins):
                ins.then_inc(rt.sem, 1)

            def route_pick(q, tb, t):
                after(gsm, q, "gates")
                if not isinstance(t, int) or t:
                    dve.wait_ge(rank_ps, t)
                rdo(V.tensor_copy(gt[:], gates[:, tb]))
                after(rt, t, "gt")
                apart(dve)
                rdo(V.max(top8[:], gt[:]))
                after(rt, t, "max")
                apart(dve)
                rdo(V.max_index(idx8[:], top8[:], gt[:]))
                after(rt, t, "idx")
                rdo(V.tensor_copy(idxf[:], idx8[:, 0:2]))
                rdo(V.tensor_copy(c_all[:, t] if isinstance(t, int) else c_all[:, t, :], top8[:, 0:2]))
                after(rt, t, "idxf")
                rdo(V.tensor_copy(e_all[:, t] if isinstance(t, int) else e_all[:, t, :], idxf[:]))
                for j in range(2):
                    rdo(V.tensor_scalar(oh[:, j], iota_e[:], idxf[:, j:j + 1], None, ALU.is_equal))
                after(rt, t, "o2")
                rdo(V.tensor_tensor(member[:], oh[:, 0], oh[:, 1], ALU.add))
                rdo(V.tensor_scalar(comb2[:], oh[:, 0], top8[:, 0:1], None, ALU.mult))

            def route_combine(t):
                after(rt, t, "wc")
                rdo(V.scalar_tensor_tensor(out=comb[:], in0=oh[:, 1], scalar=top8[:, 1:2], in1=comb2[:],
                                           op0=ALU.mult, op1=ALU.add))
                after(rt, t, "comb")
                rdo(V.tensor_copy(chi[:], comb[:]))
                after(rt, t, "hi")
                rdo(V.tensor_copy(cb96[:, 0:E], f(chi[:])))
                rdo(V.tensor_copy(cb96[:, 32:32 + E], f(chi[:])))
                rdo(V.tensor_tensor(cb96[:, 64:64 + E], comb[:], f(chi[:]), ALU.subtract))

            def route_place(t):
                dve.wait_ge(rank_ps, t + 1)
                dve.wait_ge(cbt_ok, t + 1)
                rdo(V.tensor_tensor(rb[:], misc[:, RANK0:RANK0 + E], ebase[:], ALU.add))
                after(rt, t, "rank")
                for j in range(2):
                    rdo(V.tensor_tensor(rsel[:, j], oh[:, j], rb[:], ALU.mult))
                after(rt, t, "m2")
                rdo(V.tensor_reduce(posf[:], rsel[:], AX.X, ALU.add))
                after(rt, t, "pos")
                need(dve, scat, 32 * t)
                rdo(V.tensor_copy(pos_stage[:], posf[:]))
                rdo(V.tensor_copy(pos_all[:, t] if isinstance(t, int) else pos_all[:, t, :], posf[:]))
                rdo(V.tensor_tensor(msum[:], msum[:], member[:], ALU.add))

            def take_block(q):
                dve.wait_ge(acc_ready, q + 1)
                for t in range(TB):
                    V.tensor_tensor(X2[:, q, t], X2[:, q, t], acc[t][:], ALU.add).then_inc(acc_free, 1)

            const(V.memset(kp[:, :, 0:1], NEG))
            const(V.memset(wp[:, :, 0:1], NEG))
            const(V.memset(ea[:, :, 0:1], 0.0))
            const(V.memset(eb[:, :, 0:1], 0.0))
            const(V.memset(bv[:, :, 0:1], 0.0))
            const(V.memset(neg_half[:], -0.5))
            const(V.memset(bias_f[:], 0.0))
            const(V.memset(msum[:], 0.0))
            const(V.memset(ones_bf[:], 1.0))
            const(V.memset(ones16[:], 1.0))
            const(V.memset(cb96[:], 0.0))
            after(con, 0, "cb0")
            const(V.memset(cb96[:, E:E + S_EXP], 1.0))
            const(V.memset(cb96[:, 32 + E:32 + E + S_EXP], 1.0))
            const(V.memset(f(gw2[:]), 0.0))
            ln1_stats(0)
            ln1_apply(0)
            dve.wait_ge(uw_in, 16 * 2 * GB)
            const(V.tensor_copy(wp[:, :, 1:], w_col[:].unsqueeze(2).broadcast_to([P, CB, T])))
            dve.wait_ge(pcon.sem, pcon.at(0))
            after(con, 0, "wcol")
            wkv_scan(0, 0)
            wkv_z(0, 0)
            wkv_z2(0, 0)
            v_transpose(0)
            wkv_scan(0, 1)
            for part in (4, 5, 6):
                wkv_part(0, 0, part)
            for c in range(RING):
                split_w1(c, c)
            wkv_z(0, 1)
            wkv_z2(0, 1)
            wkv_part(0, 0, 7)
            wkv_back(0, 0)
            for part in (4, 5, 6):
                wkv_part(0, 1, part)
            dve.wait_ge(c_in, 16 * 10)
            after(con, 0, "gz")
            const(V.tensor_copy(gw2[:, :, 0:E], gw_f[:]))
            after(con, 0, "ghi")
            const(V.tensor_tensor(gw2[:, :, 32:32 + E], gw_f[:], f(gw2[:, :, 0:E]), ALU.subtract))
            wkv_part(0, 1, 7)
            wkv_back(0, 1)
            ln2_quad(0)
            for tb in range(TB):
                ln2_apply(0, tb, tb, xn[:, tb])
            for tb in range(TB):
                x_lo(tb, 0, tb, acc[tb])
            const(V.tensor_copy(bias_r[0:32], bias_f[0:32]))
            const(V.tensor_copy(bias_r[64:96], bias_f[64:96]))
            const(V.tensor_copy(bias_r[32:64], bias_f[32:64]))
            after(con, 0, "blo")
            const(V.tensor_tensor(bias_r[32:64], bias_f[32:64], f(bias_r[32:64]), ALU.subtract))
            after(con, 0, None)

            for q in range(NQ):
                def head(j, q=q):
                    if j == 0:
                        gate_parts(q)
                        if q:
                            take_block(q - 1)
                        if q < NQ - 1:
                            ln1_stats(q + 1)
                    else:
                        gates_max(q)
                        if q < NQ - 1:
                            ln1_apply(q + 1)
                            v_transpose(q + 1)
                        else:
                            gates_norm(q)

                def mid(q=q):
                    gates_norm(q)
                    ln2_quad(q + 1)

                def half(s, j, q=q):
                    wkv_part(q + 1, s, j)

                def tile(tb, j, q=q):
                    t = TB * q + tb
                    if j == 0:
                        if q < NQ - 1:
                            ln2_apply(q + 1, tb, t + TB, xt)
                        route_pick(q, tb, t)
                    if j == 1:
                        route_combine(t)
                        if q < NQ - 1:
                            if q:
                                dve.wait_ge(up_done, CH * q)
                            x_lo(tb, (q + 1) % 2, t + TB, misc)
                    if j == 2:
                        route_place(t)

                def late(j):
                    if j == 1:
                        slots()

                def cdo(ins):
                    ins.then_inc(cph.sem, 1)

                def slots():
                    dve.wait_ge(cnt_ps, 1)
                    dve.wait_ge(cz, 2)
                    cdo(V.tensor_copy(cnt[:], misc[:, 0:E]))
                    after(cph, 0, "cnt")
                    cdo(V.tensor_tensor(cmp[:], cnt[:].unsqueeze(2).broadcast_to([P, E, TPE]),
                                        thr[:].unsqueeze(1).broadcast_to([P, E, TPE]), ALU.is_gt))
                    after(cph, 0, "cmp")
                    cdo(V.tensor_reduce(nt[:], cmp[:], AX.X, ALU.add))
                    after(cph, 0, "nt")
                    cdo(V.tensor_tensor_scan(tend[:], ones16[:], nt[:], 0.0, ALU.mult, ALU.add))
                    after(cph, 0, "tend")
                    cdo(V.tensor_scalar(fin_e[:], tend[:], iota_p[:], None, ALU.is_le))
                    cdo(V.tensor_tensor(move[:], tend[:], nt[:], ALU.subtract))
                    after(cph, 0, "etile")
                    cdo(V.scalar_tensor_tensor(out=move[:], in0=move[:], scalar=float(P), in1=ebase[:],
                                               op0=ALU.mult, op1=ALU.subtract))
                    cdo(V.tensor_reduce(e_s[:], fin_e[:], AX.X, ALU.add))
                    cdo(V.tensor_tensor(fin_n[:], fin_e[:], nt[:], ALU.mult))
                    after(cph, 0, "ctiles")
                    cdo(V.tensor_reduce(ts[:], fin_n[:], AX.X, ALU.add))
                    cdo(V.scalar_tensor_tensor(out=trow[:], in0=e_s[:], scalar=float(TPE), in1=iota_p[:],
                                               op0=ALU.mult, op1=ALU.add))
                    cdo(V.tensor_scalar(rv[:, 0:1], e_s[:], float(E - 1), None, ALU.min))
                    after(rt, NT - 1, None)
                    cdo(V.tensor_tensor(pick[:], e_all[:].rearrange("p n j -> p (n j)").unsqueeze(2)
                                        .broadcast_to([P, NT * 2, E]),
                                        iota_e[:].unsqueeze(1).broadcast_to([P, NT * 2, E]), ALU.is_equal))
                    after(cph, 0, "move")
                    cdo(V.tensor_tensor(trow[:], trow[:], ts[:], ALU.subtract))
                    cdo(V.tensor_scalar(rv[:, 32:32 + E], iota_e[:], rv[:, 0:1], None, ALU.is_equal))
                    after(cph, 0, "trow")
                    cdo(V.tensor_copy(trow_i[:], trow[:]))
                    cdo(V.tensor_tensor(pick[:], pick[:], move[:].unsqueeze(1).broadcast_to([P, NT * 2, E]),
                                        ALU.mult))
                    after(cph, 0, "mul")
                    cdo(V.tensor_reduce(moved[:], pick[:], AX.X, ALU.add))
                    after(cph, 0, "shift")
                    cdo(V.tensor_tensor(row_all[:], pos_all[:], moved[:].rearrange("p (n j) -> p n j", j=2),
                                        ALU.add))

                schedule(q, step, head, half, mid, tile, late)

            take_block(NQ - 1)
            dve.wait_ge(rv_ps, 1)
            V.tensor_copy(rvT[:], misc[0:1, 0:P]).then_inc(tvec.sem, 1)
            V.tensor_copy(ohT[32:32 + E], misc[32:32 + E, 0:P]).then_inc(tvec.sem, 1)
            dve.wait_ge(tab_in, 16)
            V.tensor_copy(ids_f[0:SLOT_TILES], ids_i[0:SLOT_TILES]).then_inc(tvec.sem, 1)
            dve.wait_ge(ids_ps, 1)
            dve.wait_ge(bs_ps, 1)
            V.tensor_copy(ids[:], misc[:, P:2 * P]).then_inc(tvec.sem, 1)
            V.tensor_copy(bslot[:], misc[:, 2 * P:3 * P]).then_inc(tvec.sem, 1)
            after(tvec, 0, None)
            dve.wait_ge(ew_in, 32 * E)
            dve.wait_ge(down_done, NCH)
            dve.wait_ge(w1_lo, NCH)
            dve.wait_ge(w2_lo, NCH)
            dve.wait_ge(h_lo, NCH)

            def routed_w1(s, static):
                i = static % 2
                e = dve.value_load(rvT[0:1, bass.ds(s, 1)], min_val=0, max_val=E - 1)
                dve.wait_ge(r1hi, s + 1)
                need(dve, rup, s - 1)
                V.tensor_tensor(e1lo[:, i], ew1_sb[:, e], f(e1hi[:, i]), ALU.subtract).then_inc(r1lo, 1)

            def routed_w2(s, static):
                i = static % 2
                e = dve.value_load(rvT[0:1, bass.ds(s, 1)], min_val=0, max_val=E - 1)
                dve.wait_ge(r2hi, s + 1)
                need(dve, ry, s - 1)
                V.tensor_tensor(e2lo[:, i], ew2_sb[:, e], f(e2hi[:, i]), ALU.subtract).then_inc(r2lo, 1)

            def routed_x(s, static):
                i = static % 2
                dve.wait_ge(rxh, s + 1)
                need(dve, rup, s - 1)
                V.tensor_tensor(xglo[:, i], t_bank[i][:].rearrange("p (k n) -> p k n", k=KC), f(xghi[:, i]),
                                ALU.subtract).then_inc(rxl, 1)

            def routed_h(s, static):
                i = static % 2
                dve.wait_ge(rhh, s + 1)
                dve.wait_ge(rff, s + 1)
                need(dve, ry, s - 1)
                V.tensor_tensor(rlo[:, i], rf[:, i], f(rhi[:, i]), ALU.subtract).then_inc(rhl, 1)

            def routed_y(s, static):
                n = static % 4
                dve.wait_ge(ry, s + 1)
                need(dve, yst[n], 16 * ((s - static) // 4 + static // 4))
                V.tensor_copy(ysb[:, n], y_bank[0][:]).then_inc(rye[0], 1)

            routed_rounds(dve, routed_w1, routed_x, routed_w2, routed_h, routed_y, 0)

            with dve.Fori(0, NQ) as q:
                for tb in range(TB):
                    dve.wait_ge(yg_in[tb], 32 * (q + 1))
                    V.scalar_tensor_tensor(out=X2[:, q, tb], in0=yg[:, 0, tb], scalar=c_all[:, TB * q + tb, 0:1],
                                           in1=X2[:, q, tb], op0=ALU.mult, op1=ALU.add).then_inc(comb1, 1)
                    dve.wait_ge(comb1, TB * q + tb + 1)
                    V.scalar_tensor_tensor(out=X2[:, q, tb], in0=yg[:, 1, tb], scalar=c_all[:, TB * q + tb, 1:2],
                                           in1=X2[:, q, tb], op0=ALU.mult, op1=ALU.add).then_inc(comb2s, 1)

        @block.gpsimd
        def _(pool):
            G = nc.gpsimd

            def const(ins):
                ins.then_inc(pcon.sem, 1)

            const(G.memset(ident[:], 0.0))
            const(G.memset(tri[:], 1.0))
            const(G.memset(sel[:], 0.0))
            pool.wait_ge(pcon.sem, pcon.at(0, "sel0"))
            const(G.affine_select(out=ident[:], in_=ident[:], compare_op=ALU.not_equal, fill=1.0, base=0,
                                  pattern=[[-1, P]], channel_multiplier=1))
            const(G.affine_select(out=tri[:], in_=tri[:], compare_op=ALU.is_gt, fill=0.0, base=0,
                                  pattern=[[1, P]], channel_multiplier=-1))
            const(G.affine_select(out=sel[:], in_=sel[:], compare_op=ALU.not_equal, fill=1.0, base=0,
                                  pattern=[[-1, E]], channel_multiplier=1))
            pool.wait_ge(pcon.sem, pcon.at(0, "sela"))
            const(G.affine_select(out=sel[:], in_=sel[:], compare_op=ALU.not_equal, fill=1.0, base=-32,
                                  pattern=[[-1, E]], channel_multiplier=1))
            const(G.iota(iota_e[:], [[1, E]], base=0, channel_multiplier=0, allow_small_or_imprecise_dtypes=True))
            const(G.iota(ebase[:], [[NTOK, E]], base=0, channel_multiplier=0, allow_small_or_imprecise_dtypes=True))
            const(G.iota(thr[:], [[P, TPE]], base=0, channel_multiplier=0, allow_small_or_imprecise_dtypes=True))
            const(G.iota(iota_p[:], [[0, 1]], base=0, channel_multiplier=1, allow_small_or_imprecise_dtypes=True))
            const(G.iota(tokid[:], [[P, NT]], base=0, channel_multiplier=1))
            const(G.memset(tok_stage[:], 0))
            const(G.memset(zero_i[:], 0))
            pool.wait_ge(pcon.sem, pcon.at(0))
            pool.dma_start(table_dram.rearrange("(p n) o -> p (n o)", p=P), zero_i[:]).then_inc(tz, 16)

            def rstd_quad(q):
                pool.wait_ge(ln1.sem, ln1.at(q, "veps"))
                G.tensor_tensor(rstd[:], veps[:], neg_half[:], ALU.pow).then_inc(rstd1, 1)

            def rstd_quad2(q):
                pool.wait_ge(ln2.sem, ln2.at(q, "veps"))
                G.tensor_tensor(rstd[:], veps[:], neg_half[:], ALU.pow).then_inc(rstd2, 1)

            def key_plus_bonus(q):
                pool.wait_ge(uw_in, 16 * 2 * GB)
                pool.wait_ge(ln1.sem, ln1.at(q, "tk"))
                for s in range(2):
                    cs = bass.ds(HC * s, HC)
                    G.tensor_tensor(ku_sum[:, cs, :], kp[:, cs, 1:], u_col[:, cs].unsqueeze(2).broadcast_to([P, HC, T]),
                                    ALU.add).then_inc(ku, 1)

            def store_rows(t, rows):
                pool.wait_ge(norm, t + 1)
                pool.dma_start(xn_tiles[t], rows).then_inc(xn_out, 16)

            def scatter(t):
                need(pool, scat, 32 * t)
                G.tensor_copy(tok_stage[:], tokid[:, bass.ds(t, 1)]).then_inc(pst, 1)
                pool.wait_ge(pst, t + 1)
                pool.wait_ge(rt.sem, rt.at(t, "pint"))
                apart(pool)
                pool.indirect_dma_start(out=table_dram[:, :], out_offset=bass.IndirectOffsetOnAxis(
                    ap=pos_stage[:, 0:1], axis=0), in_=tok_stage[:], in_offset=None).then_inc(scat, 16)
                pool.wait_ge(scat, 32 * t + 16)
                apart(pool)
                pool.indirect_dma_start(out=table_dram[:, :], out_offset=bass.IndirectOffsetOnAxis(
                    ap=pos_stage[:, 1:2], axis=0), in_=tok_stage[:], in_offset=None).then_inc(scat, 16)

            pool.wait_ge(con.sem, con.at(0, "half"))
            rstd_quad(0)
            key_plus_bonus(0)
            rstd_quad2(0)
            for tb in range(TB):
                store_rows(tb, xn[:, tb])
            pool.wait_ge(tz, 16)
            for q in range(NQ):
                if q < NQ - 1:
                    rstd_quad(q + 1)
                    key_plus_bonus(q + 1)
                    rstd_quad2(q + 1)
                else:
                    pool.wait_ge(xT_ps, NT)
                    pool.wait_ge(xn_out, 16 * NT)
                    G.memset(rv[:], 0.0).then_inc(cz, 1)
                    G.memset(ids_f[:], 0.0).then_inc(cz, 1)

                def tile(tb):
                    if q < NQ - 1:
                        store_rows(TB * (q + 1) + tb, xt)
                    scatter(TB * q + tb)

                if q == 0:
                    tile(0)
                with pool.Fori(1 if q == 0 else 0, TB) as tb:
                    tile(tb)

            pool.wait_ge(cph.sem, cph.at(0))
            pool.wait_ge(scat, 32 * NT)
            pool.indirect_dma_start(out=ids_i[0:SLOT_TILES, :], out_offset=None, in_=table_rows[:, :],
                                    in_offset=bass.IndirectOffsetOnAxis(ap=trow_i[0:SLOT_TILES, 0:1], axis=0))\
                .then_inc(tab_in, 16)
            pool.wait_ge(tvec.sem, tvec.at(0, "idi"))
            pool.wait_ge(xn_out, 16 * NT)
            pool.wait_ge(down_done, NCH)
            pool.wait_ge(h_lo, NCH)
            pool.wait_ge(w2_lo, NCH)
            pool.wait_ge(w1_lo, NCH)

            def gather(s, static):
                n = static % 4
                need(pool, rT, s - 3)
                G.tensor_copy(idc[:, n:n + 1], ids[:, bass.ds(s, 1)]).then_inc(idc_ok, 1)
                pool.wait_ge(idc_ok, s + 1)
                apart(pool)
                pool.indirect_dma_start(out=xg[:, n], out_offset=None, in_=xn_dram[:, :],
                                        in_offset=bass.IndirectOffsetOnAxis(ap=idc[:, n:n + 1], axis=0))\
                    .then_inc(g_in[n], 16)

            for s in range(4):
                gather(s, s)
            with pool.Fori(1, SLOT_TILES // 4) as i:
                for j in range(4):
                    gather(4 * i + j, j)

            for n in range(4):
                pool.wait_ge(yst[n], 16 * (SLOT_TILES // 4))
            for i in range(2):
                pool.wait_ge(rye[i], SLOT_TILES // 2)
            with pool.Fori(0, NQ) as q:
                for tb in range(TB):
                    t = TB * q + tb
                    for j in range(2):
                        G.tensor_copy(idy[:, j, tb:tb + 1], row_all[:, bass.ds(t, 1), j]).then_inc(idy_ok, 1)
                        pool.wait_ge(idy_ok, 2 * t + j + 1)
                        apart(pool)
                        pool.indirect_dma_start(out=yg[:, j, tb], out_offset=None, in_=y_dram[:, :],
                                                in_offset=bass.IndirectOffsetOnAxis(ap=idy[:, j, tb:tb + 1], axis=0))\
                            .then_inc(yg_in[tb], 16)
                pool.wait_ge(comb2s, TB * (q + 1))


_INS = ["x", "ctx_2048", "L0_xattn_w", "L0_xattn_u", "L0_ffn_gate_w", "L0_ffn_gate_b", "L0_ffn_ew1", "L0_ffn_eb1",
        "L0_ffn_ew2", "L0_ffn_eb2", "L0_ffn_sw1", "L0_ffn_sb1", "L0_ffn_sw2", "L0_ffn_sb2"]


def kernel(**inputs):
    import numpy as np
    import concourse.bacc as bacc
    from concourse import mybir as mb
    from concourse.bass_utils import run_bass_kernel_spmd

    nc = bacc.Bacc("TRN2", target_bir_lowering=False, num_devices=1)
    arrays, args = {}, []
    for name in _INS:
        a = np.ascontiguousarray(inputs[name])
        arrays[f"in_{name}"] = a
        args.append(nc.dram_tensor(f"in_{name}", a.shape, mb.dt.from_np(a.dtype), kind="ExternalInput").ap())
    shape = arrays["in_x"].shape
    args.append(nc.dram_tensor("out_0", shape, mb.dt.float32, kind="ExternalOutput").ap())
    with nc.allow_non_contiguous_dma(reason="small per-channel vectors go to columns"):
        mixed_layer(nc, *args)
    r = run_bass_kernel_spmd(nc, [arrays], core_ids=[0])
    return r.results[0]["out_0"]
```

```python
import concourse.bass as bass
from concourse import mybir
from contextlib import ExitStack



class Steps:

    def __init__(self, sem, names):
        self.sem, self.names = sem, names.split()

    def at(self, round_, name=None):
        n = len(self.names) if name is None else self.names.index(name) + 1
        return round_ * len(self.names) + n


def mixed_layer(nc, x, ctx_in, decay, bonus, gate_w, gate_b, ew1, eb1, ew2, eb2, sw1, sb1, sw2, sb2, out):
    f32, f32r, bf16 = mybir.dt.float32, mybir.dt.float32r, mybir.dt.bfloat16
    i32, u32 = mybir.dt.int32, mybir.dt.uint32
    ALU, ACT, AX = mybir.AluOpType, mybir.ActivationFunctionType, mybir.AxisListType

    P = 128
    B, T, D = x.shape
    E, _, HR = ew1.shape
    S_EXP, _, HS = sw1.shape
    GB = 4
    NQ = B // GB
    TT = 32
    TB = T // TT
    NT = NQ * TB
    QT = GB * T
    NTOK = B * T
    KC = D // P
    CB = D // 32
    HC = CB // 2
    CPS = HS // P
    CH = S_EXP * CPS
    NCH = NQ * CH
    HOLD = NCH - 12
    RING = 3
    BR = 96
    TPE = NTOK // P
    SLOT_TILES = 2 * NTOK // P + E
    TROWS = E * TPE + SLOT_TILES
    EPS = 1e-5
    NEG = -1e38

    xq = x.rearrange("(q g) (tb t) c -> q g t tb c", g=GB, t=TT)
    vq = ctx_in.rearrange("(q g) (tb t) c -> q g t tb c", g=GB, t=TT)
    outq = out.rearrange("(q g) (tb t) c -> q g t tb c", g=GB, t=TT)
    sw1_c = sw1.rearrange("s (k p) (n h) -> s n p k h", p=P, h=P)
    sw2_c = sw2.rearrange("s (n h) d -> s n h d", h=P)
    ew1_c = ew1.rearrange("e (k p) h -> e p k h", p=P)

    xn_dram = nc.dram_tensor("xn_rows", (NTOK, D), f32, kind="Internal").ap()
    table_dram = nc.dram_tensor("slot_table", (TROWS * P, 1), i32, kind="Internal").ap()
    y_dram = nc.dram_tensor("expert_rows", (SLOT_TILES * P, D), f32, kind="Internal").ap()
    xn_tiles = xn_dram.rearrange("(n p) d -> n p d", p=P)
    table_rows = table_dram.rearrange("(r p) o -> r (p o)", p=P)
    y_tiles = y_dram.rearrange("(n p) d -> n p d", p=P)

    top = ExitStack()
    with top:
        def sb(name, shape, dt=f32, where=top):
            return where.enter_context(nc.sbuf_tensor(name, shape, dt))

        def sem(name):
            return top.enter_context(nc.semaphore(name))

        shared_mem = ExitStack()
        xs = sb("xs", [P, 2, 2, KC, QT], f32r, shared_mem)
        xhi, xlo = xs[:, :, 0], xs[:, :, 1]
        w1hi = sb("w1hi", [P, RING, KC, P], f32r, shared_mem)
        w1lo = sb("w1lo", [P, RING, KC, P], f32r, shared_mem)
        hf = sb("hf", [P, RING, QT], where=shared_mem)
        hhi = sb("hhi", [P, RING, QT], f32r, shared_mem)
        hlo = sb("hlo", [P, RING, QT], f32r, shared_mem)
        w2hi = sb("w2hi", [P, RING, D], f32r, shared_mem)
        w2lo = sb("w2lo", [P, RING, D], f32r, shared_mem)
        w2_raw = sb("w2_raw", [P, RING, D], where=shared_mem)
        w1_raw = sb("w1_raw", [P, RING, KC, P], where=shared_mem)
        shared_mem.close()
        EH = E // 2
        last_tokens = 2 * KC * QT
        raw_mem = ExitStack()
        sb("tokens_kept_raw", [P, last_tokens], where=raw_mem)
        e2raw = sb("e2raw", [P, E, D], where=raw_mem)
        raw_mem.close()
        routed_mem = ExitStack()
        sb("tokens_kept", [P, last_tokens], where=routed_mem)
        e2lo = sb("e2lo", [P, E, D], f32r, routed_mem)
        sb("hf_rest", [P, 3 * RING * D - EH * D], where=routed_mem)
        xghi = sb("xghi", [P, 2, KC, P], f32r, routed_mem)
        xglo = sb("xglo", [P, 2, KC, P], f32r, routed_mem)
        e1hi = sb("e1hi", [P, 2, KC, P], f32r, routed_mem)
        e1lo = sb("e1lo", [P, 2, KC, P], f32r, routed_mem)
        rf = sb("rf", [P, 2, P], where=routed_mem)
        rhi = sb("rhi", [P, 2, P], f32r, routed_mem)
        rlo = sb("rlo", [P, 2, P], f32r, routed_mem)
        ysb = sb("ysb", [P, 4, D], where=routed_mem)
        routed_mem.close()
        sb("tokens_and_rings", [P, 2 * last_tokens + 9 * RING * D])

        X2 = sb("X2", [P, NQ, TB, D])
        ident = sb("ident", [P, P])
        tri = sb("tri", [P, P], bf16)
        ones_bf = sb("ones_bf", [P, P], bf16)
        ones16 = sb("ones16", [P, E])
        neg_half = sb("neg_half", [P, TB])
        iota_e = sb("iota_e", [P, E])
        ebase = sb("ebase", [P, E])
        thr = sb("thr", [P, TPE])
        iota_p = sb("iota_p", [P, 1])
        tokid = sb("tokid", [P, NT], i32)
        tok_stage = sb("tok_stage", [P, 1], i32)
        u_col = sb("u_col", [P, CB])
        w_col = sb("w_col", [P, CB])
        gw_f = sb("gw_f", [P, KC, E])
        gw2 = sb("gw2", [P, KC, P], f32r)
        sel = sb("sel", [64, E])
        gb_b = sb("gb_b", [P, E])
        b1_rows = sb("b1_rows", [CH, P])
        b1_col = sb("b1_col", [P, CH])
        eb1_at = sb("eb1_at", [64, P])
        bias_f = sb("bias_f", [BR, D])
        bias_r = sb("bias_r", [BR, D], f32r)
        lgT = bias_f[0:64]
        st6 = sb("st6", [P, TB, 6])
        mv = sb("mv", [P, TB, 2])
        veps = sb("veps", [P, TB])
        rstd = sb("rstd", [P, TB])
        logits = sb("logits", [P, TB, E])
        gates = sb("gates", [P, TB, E])
        gmax = sb("gmax", [P, TB])
        gsum = sb("gsum", [P, TB])
        grec = sb("grec", [P, TB])
        gt = sb("gt", [P, E])
        top8 = sb("top8", [P, 8])
        idx8 = sb("idx8", [P, 8], u32)
        idxf = sb("idxf", [P, 2])
        oh = sb("oh", [P, 2, E])
        member = sb("member", [P, E], bf16)
        msum = sb("msum", [P, E], bf16)
        comb = sb("comb", [P, E])
        comb2 = sb("comb2", [P, E])
        cb96 = sb("cb96", [P, BR])
        chi = sb("chi", [P, E], f32r)
        cbT = sb("cbT", [BR, TB, P], f32r)
        rb = sb("rb", [P, E])
        rsel = sb("rsel", [P, 2, E])
        posf = sb("posf", [P, 2])
        pos_stage = sb("pos_stage", [P, 2], i32)
        pos_all = sb("pos_all", [P, NT, 2])
        e_all = sb("e_all", [P, NT, 2])
        row_all = sb("row_all", [P, NT, 2], i32)
        c_all = sb("c_all", [P, NT, 2])
        cnt = sb("cnt", [P, E])
        nt = sb("nt", [P, E])
        tend = sb("tend", [P, E])
        move = sb("move", [P, E])
        fin_e = sb("fin_e", [P, E])
        fin_n = sb("fin_n", [P, E])
        e_s = sb("e_s", [P, 1])
        trow = sb("trow", [P, 1])
        ts = sb("ts", [P, 1])
        trow_i = sb("trow_i", [P, 1], i32)
        zero_i = sb("zero_i", [P, (TROWS * P) // P], i32)

        wkv_mem = ExitStack()
        TS = T + 1
        wp = sb("wp", [P, CB, TS], where=wkv_mem)
        kp = sb("kp", [P, CB, TS], where=wkv_mem)
        kn = sb("kn", [P, TB, D], where=wkv_mem)
        vin = sb("vin", [P, TB, D], where=wkv_mem)
        vp = sb("vp", [P, CB, T], where=wkv_mem)
        mx = sb("mx", [P, HC, TS], where=wkv_mem)
        ea = sb("ea", [P, HC, TS], where=wkv_mem)
        eb = sb("eb", [P, HC, TS], where=wkv_mem)
        eu = sb("eu", [P, HC, T], where=wkv_mem)
        en = sb("en", [P, HC, T], where=wkv_mem)
        bv = sb("bv", [P, HC, TS], where=wkv_mem)
        pp = sb("pp", [P, HC, TS], where=wkv_mem)
        qq = sb("qq", [P, HC, TS], where=wkv_mem)
        wkv_mem.close()
        weights_mem = ExitStack()
        ew1_sb = sb("ew1_sb", [P, E, KC, P], where=weights_mem)
        e2hi = sb("e2hi", [P, E, D], f32r, weights_mem)
        weights_mem.close()
        yg = sb("yg", [P, NQ, 2, TB, D])
        rvT = sb("rvT", [1, P], i32)
        NS = SLOT_TILES + 8
        xrow = sb("xrow", [P, NS], i32)
        bslot = sb("bslot", [P, NS])
        idx = sb("idx", [P, 4], i32)
        slot_mem = ExitStack()
        cmp = sb("cmp", [P, E, TPE], where=slot_mem)
        rv = sb("rv", [P, P], where=slot_mem)
        ohT = sb("ohT", [64, P], where=slot_mem)
        ids_i = sb("ids_i", [P, P], i32, slot_mem)
        ids_f = sb("ids_f", [P, P], where=slot_mem)
        pick = sb("pick", [P, NT * 2, E], where=slot_mem)
        moved = sb("moved", [P, NT * 2], where=slot_mem)
        slot_mem.close()
        xg = sb("xg", [P, 4, D])
        xn = kn
        xt = kn[:, 0]
        ku_sum = kn[:, :, :].rearrange("p a c -> p (a c)").rearrange("p (c t) -> p c t", t=T)
        yT = en[:].rearrange("p c t -> p (c t)").rearrange("p (tb c) -> p tb c", tb=TB)

        acc = [top.enter_context(nc.psum_tensor(f"acc{i}", [P, D], f32)) for i in range(TB)]
        up = [top.enter_context(nc.psum_tensor(f"up{i}", [P, QT], f32)) for i in range(RING)]
        misc = top.enter_context(nc.psum_tensor("misc", [P, 512], f32))
        CBT0, RANK0 = 128, 256
        t_bank = [misc, up[0]]
        r_bank = [up[1], up[2]]
        y_bank = [acc[0], acc[1]]

        x_in = [sem(f"x_in{q}") for q in range(NQ)]
        v_in, uw_in, c_in = sem("v_in"), sem("uw_in"), sem("c_in")
        w1_in = [sem(f"w1_in{i}") for i in range(RING)]
        w2_in = [sem(f"w2_in{i}") for i in range(RING)]
        ew_in, e2_in, xn_out, tz, y_out, out_done = sem("ew_in"), [sem(f"e2_in{i}") for i in range(3)], sem("xn_out"), sem("tz"), sem("y_out"), sem("out_done")
        scat, tab_in = sem("scat"), sem("tab_in")
        g_in = [sem(f"g_in{i}") for i in range(4)]
        yg_in = [[sem(f"yg_in{q}{j}") for j in range(2)] for q in range(NQ)]
        w1_hi, w2_hi, h_hi, h_full = sem("w1_hi"), sem("w2_hi"), sem("h_hi"), sem("h_full")
        w1_lo, w2_lo, h_lo = sem("w1_lo"), sem("w2_lo"), sem("h_lo")
        up_done, down_done, acc_ready = sem("up_done"), sem("down_done"), sem("acc_ready")
        acc_free = sem("acc_free")
        rstd1, rstd2 = sem("rstd1"), sem("rstd2")
        gexp, xhi_ok, cbt_ok = sem("gexp"), sem("xhi_ok"), sem("cbt_ok")
        xT_ps, gate_ps, lg_ps, rank_ps = sem("xT_ps"), sem("gate_ps"), sem("lg_ps"), sem("rank_ps")
        b1_ps, cnt_ps, rv_ps, ids_ps, bs_ps = sem("b1_ps"), sem("cnt_ps"), sem("rv_ps"), sem("ids_ps"), sem("bs_ps")
        b1_ok = sem("b1_ok")
        ln1 = Steps(sem("ln1"), "s0 s1 s2 s3 a0 a1 a2 a3 veps n0 n1 n2 n3 tk")
        vT = sem("vT")
        wscan = sem("wscan")
        wz = Steps(sem("wz"), "wm z")
        z2_ok, ev_ok, w_ok = sem("z2_ok"), sem("ev_ok"), sem("w_ok")
        wkv = Steps(sem("wkv"), "bmul sp sq aq ap den num nt nr y")
        wrelu = Steps(sem("wrelu"), "b a n u")
        wexp = Steps(sem("wexp"), "b a n u ln rec")
        ku = sem("ku")
        ty = sem("ty")
        ln2 = Steps(sem("ln2"), "s0 s1 s2 s3 a0 a1 a2 a3 veps")
        norm, xlo_ok, x2_ok = sem("norm"), sem("xlo_ok"), sem("x2_ok")
        gsm = Steps(sem("gsm"), "parts lg max sub sum rec gates")
        rt = Steps(sem("rt"), "gt max idx idxf c e o1 o2 mem wc comb hi h0 h1 lo rank m1 m2 pos pint pall msum")
        con = Steps(sem("con"), "k0 w0 ea eb bv half bias0 ms ones o16 cb0 cb1 cb2 gz ghi glo bhi1 bhi2 blo bhi3")
        pcon = Steps(sem("pcon"), "id0 tri0 sel0 id tri sela selb ie eb thr ip tok stage z")
        cph = Steps(sem("cph"), "cnt cmp nt tend fin etile move es ctiles ts trow0 rve eq trow oh tri mul shift row")
        tvec = Steps(sem("tvec"), "rvT ohT idf xrow bs")
        pst, cz = sem("pst"), sem("cz")

        rx, rT, rup, ry = sem("rx"), sem("rT"), sem("rup"), sem("ry")
        r1hi, r2hi, rhh, rff, rxh = sem("r1hi"), sem("r2hi"), sem("rhh"), sem("rff"), sem("rxh")
        r1lo, r2lo, rhl, rxl = sem("r1lo"), sem("r2lo"), sem("rhl"), sem("rxl")
        rye = [sem("rye0"), sem("rye1")]
        idx_ok = sem("idx_ok")
        yst = [sem(f"yst{i}") for i in range(4)]
        comb1, comb2s = sem("comb1"), sem("comb2s")

        block = top.enter_context(nc.Block())

        def need(eng, s, value):
            if not isinstance(value, int) or value > 0:
                eng.wait_ge(s, value)

        def apart(eng):
            eng.nop(nofuse=True)

        def schedule(q, step, head, half, mid, tile, late=None, final=None):
            eng = step.engine
            c0 = CH * q
            for j in range(2):
                step(c0 + j)
                head(j)
            at = c0 + 2
            if q < NQ - 1:
                if q == 0:
                    for s in range(2):
                        for j in range(9):
                            step(at + 9 * s + j)
                            half(s, j)
                else:
                    with eng.Fori(0, 2) as s:
                        for j in range(9):
                            step(at + 9 * s + j, at + j)
                            half(s, j)
                at += 18
                mid()
            if q == 0:
                for j in range(3):
                    step(at + j)
                    tile(0, j)
            with eng.Fori(1 if q == 0 else 0, TB - 1) as tb:
                for j in range(3):
                    step(at + 3 * tb + j, at + j)
                    tile(tb, j)
            at += 3 * (TB - 1)
            for j in range(3):
                step(at + j)
                tile(TB - 1, j)
            at += 3
            if q == NQ - 1:
                for hook in (late, final):
                    for j in range(3):
                        step(at + j)
                        if hook:
                            hook(j)
                    at += 3
            assert at == (HOLD if q == NQ - 1 else c0 + CH)

        def last_chunks(step, tail=lambda k: None):
            for k in range(NCH - HOLD):
                step(HOLD + k)
                tail(k)

        def uses(c, static):
            return (c - static) // 3 + static // 3 + 1 if not isinstance(c, int) else c // 3 + 1

        def routed_rounds(eng, w1, x, h, y, parity, start=lambda: None):
            def one(s, static):
                last = s if isinstance(s, int) else 0
                h(s, static)
                if last + 2 < SLOT_TILES:
                    w1(s + 2, static + 2)
                    x(s + 2, static + 2)
                if (not isinstance(s, int) or s) and (static - 1) % 2 == parity:
                    y(s - 1, static - 1)

            for s in range(2):
                w1(s, s)
                x(s, s)
            start()
            for s in range(5):
                one(s, s)
            rounds = (SLOT_TILES - 2 - 5) // 4
            with eng.Fori(0, rounds) as i:
                for j in range(5, 9):
                    one(4 * i + j, j)
            for s in range(5 + 4 * rounds, SLOT_TILES):
                one(s, s)
            if (SLOT_TILES - 1) % 2 == parity:
                y(SLOT_TILES - 1, SLOT_TILES - 1)

        def y_taken(s, static):
            return (s - static) // 2 + static // 2 + 1

        @block.sync
        def _(sp):
            def load_quad(q):
                for g in range(GB):
                    sp.dma_start(X2[32 * g:32 * g + 32, q], xq[q, g]).then_inc(x_in[q], 16)
                need(sp, vT, q)
                for g in range(GB):
                    sp.dma_start(vin[32 * g:32 * g + 32], vq[q, g]).then_inc(v_in, 16)

            def load_w1(c, static, n):
                need(sp, w1_hi, c - 2)
                need(sp, w1_lo, c - 2)
                sp.dma_start(w1_raw[:, static % RING], sw1_c[n // CPS, n % CPS]).then_inc(w1_in[static % RING], 16)

            def load_w2(c, static, n):
                need(sp, w2_hi, c - 2)
                need(sp, w2_lo, c - 2)
                sp.dma_start(w2_raw[:, static % RING], sw2_c[n // CPS, n % CPS]).then_inc(w2_in[static % RING], 16)

            load_quad(0)
            for k, v in ((u_col, bonus), (w_col, decay)):
                for g in range(GB):
                    sp.dma_start(k[32 * g:32 * g + 32], v.rearrange("(b p) -> p b", p=32)).then_inc(uw_in, 16)
            for c in range(RING):
                load_w1(c, c, c)
            sp.dma_start(gw_f[:], gate_w.rearrange("(k p) e -> p k e", p=P)).then_inc(c_in, 16)
            sp.dma_start(gb_b[:], gate_b.rearrange("(o e) -> o e", o=1).broadcast_to([P, E])).then_inc(c_in, 16)
            sp.dma_start(b1_rows[:], sb1.rearrange("s (n h) -> (s n) h", h=P)).then_inc(c_in, 16)
            sp.dma_start(eb1_at[32:32 + E], eb1).then_inc(c_in, 16)
            sp.wait_ge(con.sem, con.at(0, "bias0"))
            for r in range(3):
                sp.dma_start(bias_f[32 * r:32 * r + E], eb2).then_inc(c_in, 16)
                sp.dma_start(bias_f[32 * r + E:32 * r + E + S_EXP], sb2).then_inc(c_in, 16)

            for q in range(NQ):
                if q == 0:
                    load_quad(1)
                last = q == NQ - 1
                c0 = CH * q
                chunks = HOLD - c0 if last else CH
                for n in range(3):
                    load_w2(c0 + n, c0 + n, n)
                    load_w1(c0 + n + 3, c0 + n + 3, n + 3)
                if last:
                    sp.wait_ge(xT_ps, NT)
                    sp.wait_ge(xn_out, 16 * NT)
                    sp.wait_ge(up_done, c0)
                    sp.wait_ge(gate_ps, NQ - 1)
                    for e in range(EH):
                        sp.dma_start(e2raw[:, e], ew2[e]).then_inc(e2_in[0], 16)
                rounds = (chunks - 3) // 3
                with sp.Fori(1, rounds) as i:
                    for j in range(3):
                        n = 3 * i + j
                        load_w2(c0 + n, c0 + j, n)
                        load_w1(c0 + n + 3, c0 + j, n + 3)
                    if last:
                        for j in range(4):
                            sp.dma_start(ew1_sb[:, 4 * i + (j - 4)], ew1_c[4 * i + (j - 4)]).then_inc(ew_in, 16)
                if q + 2 < NQ:
                    load_quad(q + 2)
                for n in range(3 * rounds, chunks):
                    load_w2(c0 + n, c0 + n, n)
                    if n + 3 < chunks or not last:
                        load_w1(c0 + n + 3, c0 + n + 3, (n + 3) % CH)

            sp.wait_ge(up_done, HOLD)
            sp.wait_ge(w1_hi, HOLD)
            sp.wait_ge(w1_lo, HOLD)
            in_w1 = 2 * RING
            for e in range(EH, EH + in_w1):
                sp.dma_start(e2raw[:, e], ew2[e]).then_inc(e2_in[2 * e // EH - 1], 16)
            sp.wait_ge(h_lo, HOLD)
            for e in range(EH + in_w1, E):
                sp.dma_start(e2raw[:, e], ew2[e]).then_inc(e2_in[2], 16)
            for c in range(HOLD, HOLD + RING):
                load_w1(c, c, c % CH)

            def store_y(s, static):
                sp.wait_ge(rye[static % 2], y_taken(s, static))
                sp.dma_start(y_tiles[s], ysb[:, static % 4]).then_inc(yst[static % 4], 16)

            with sp.Fori(0, SLOT_TILES // 4) as i:
                for j in range(4):
                    store_y(4 * i + j, j)

            for n in range(4):
                sp.wait_ge(yst[n], 16 * (SLOT_TILES // 4))
            for c in range(HOLD, NCH):
                load_w2(c, c, c % CH)
                if c + 3 < NCH:
                    load_w1(c + 3, c + 3, (c + 3) % CH)

            for q in range(NQ):
                if q < NQ - 1:
                    sp.wait_ge(comb2s, TB * (q + 1))
                else:
                    sp.wait_ge(acc_free, TB * (NQ + 1))
                for g in range(GB):
                    sp.dma_start(outq[q, g], X2[32 * g:32 * g + 32, q]).then_inc(out_done, 16)
            sp.wait_ge(out_done, 16 * GB * NQ)

        @block.tensor
        def _(pe):
            def splits(o, lhs, rhs, start, stop):
                nc.tensor.matmul(o, lhs[0], rhs[0], start=start, stop=False)
                nc.tensor.matmul(o, lhs[0], rhs[1], start=False, stop=False)
                return nc.tensor.matmul(o, lhs[1], rhs[0], start=False, stop=stop)

            def up_product(c, static, q):
                slot, par = static % RING, (q + 1) % 2
                need(pe, w1_hi, c + 1)
                need(pe, w1_lo, c + 1)
                need(pe, h_hi, c - 2)
                need(pe, h_full, c - 2)
                for k in range(KC):
                    last = splits(up[slot][:], (w1hi[:, slot, k], w1lo[:, slot, k]),
                                  (xhi[:, par, k], xlo[:, par, k]), k == 0, k == KC - 1)
                last.then_inc(up_done, 1)

            def block_ready(q):
                pe.wait_ge(xhi_ok, TB * (q + 1))
                pe.wait_ge(xlo_ok, TB * (q + 1))

            class step:
                engine = pe

                def __new__(cls, c, static=None):
                    static = c if static is None else static
                    q, n = static // CH, static % CH
                    slot = static % RING
                    ahead = static + 2
                    if isinstance(c, int) and ahead % CH == 0 and ahead < NCH:
                        block_ready(ahead // CH)
                    if not isinstance(c, int) or ahead < HOLD or c >= HOLD and ahead < NCH:
                        up_product(c + 2, ahead, ahead // CH)
                    need(pe, w2_hi, c + 1)
                    need(pe, w2_lo, c + 1)
                    need(pe, h_hi, c + 1)
                    first = isinstance(c, int) and (n == 0 or c == HOLD)
                    for t in range(TB):
                        hh = hhi[:, slot, P * t:P * t + P]
                        if first and q and n == 0:
                            pe.wait_ge(acc_free, TB * (q - 1) + t + 1)
                        nc.tensor.matmul(acc[t][:], hh, w2hi[:, slot], start=first, stop=False)
                        nc.tensor.matmul(acc[t][:], hh, w2lo[:, slot], start=False, stop=False)
                    need(pe, h_lo, c + 1)
                    for t in range(TB):
                        last = nc.tensor.matmul(acc[t][:], hlo[:, slot, P * t:P * t + P], w2hi[:, slot],
                                                start=False, stop=isinstance(c, int) and c == HOLD - 1)
                    last.then_inc(down_done, 1)
                    if isinstance(c, int) and n == CH - 1:
                        pe.wait_ge(cbt_ok, TB * (q + 1))
                        for t in range(TB):
                            last = nc.tensor.matmul(acc[t][:], cbT[:, t], bias_r[:], start=False, stop=True)
                        last.then_inc(acc_ready, 1)

            def transpose_x(t, rows, bank):
                pe.wait_ge(norm, t + 1)
                for k in range(KC):
                    last = nc.tensor.transpose(bank[:, P * k:P * k + P], rows[:, P * k:P * k + P], ident[:])
                last.then_inc(xT_ps, 1)

            def gate_product(q):
                pe.wait_ge(con.sem, con.at(0))
                block_ready(q)
                for k in range(KC):
                    nc.tensor.matmul(misc[:], gw2[:, k], xhi[:, (q + 1) % 2, k], start=k == 0, stop=False)
                    last = nc.tensor.matmul(misc[:], gw2[:, k], xlo[:, (q + 1) % 2, k], start=False, stop=k == KC - 1)
                last.then_inc(gate_ps, 1)

            def gate_transpose(q):
                pe.wait_ge(gsm.sem, gsm.at(q, "parts"))
                for tb in range(TB):
                    last = nc.tensor.matmul(misc[:, E * tb:E * tb + E], lgT[:, P * tb:P * tb + P], sel[:],
                                            start=True, stop=True)
                last.then_inc(lg_ps, 1)

            def routing_products(t):
                pe.wait_ge(rt.sem, rt.at(t, "lo"))
                nc.tensor.transpose(misc[0:BR, CBT0:CBT0 + P], cb96[:], ident[:])
                nc.tensor.matmul(misc[:, RANK0:RANK0 + E], tri[:], member[:], start=True, stop=False)
                nc.tensor.matmul(misc[:, RANK0:RANK0 + E], ones_bf[:], msum[:], start=False, stop=True)\
                    .then_inc(rank_ps, 1)

            pe.wait_ge(pcon.sem, pcon.at(0, "tri"))
            pe.wait_ge(c_in, 16 * 10)
            nc.tensor.transpose(misc[:, 0:CH], b1_rows[:], ident[0:CH, 0:CH]).then_inc(b1_ps, 1)
            pe.wait_ge(b1_ok, 1)
            for tb in range(TB):
                transpose_x(tb, xn[:, tb], acc[tb])
            block_ready(0)
            up_product(0, 0, 0)
            up_product(1, 1, 0)
            gate_product(0)
            for q in range(NQ):
                def head(j, q=q):
                    if j == 0:
                        gate_transpose(q)

                def tile(tb, j, q=q):
                    t = TB * q + tb
                    if j == 0 and q < NQ - 1:
                        pe.wait_ge(gsm.sem, gsm.at(q, "lg"))
                        pe.wait_ge(cbt_ok, t)
                        pe.wait_ge(rt.sem, t * len(rt.names))
                        transpose_x(t + TB, xt, misc)
                    if j == 1:
                        if q < NQ - 1:
                            pe.wait_ge(xhi_ok, t + TB + 1)
                            pe.wait_ge(xlo_ok, t + TB + 1)
                        else:
                            pe.wait_ge(gsm.sem, gsm.at(q, "lg"))
                            pe.wait_ge(cbt_ok, t)
                            pe.wait_ge(rt.sem, t * len(rt.names))
                        routing_products(t)

                def late(j):
                    if j == 0:
                        pe.wait_ge(rt.sem, rt.at(NT - 1))
                        pe.wait_ge(cbt_ok, NT)
                        nc.tensor.matmul(misc[:, 0:E], ones_bf[:], msum[:], start=True, stop=True)\
                            .then_inc(cnt_ps, 1)
                    if j == 2:
                        pe.wait_ge(cph.sem, cph.at(0))
                        nc.tensor.transpose(misc[:, 0:P], rv[:], ident[:]).then_inc(rv_ps, 1)

                def final(j):
                    if j == 0:
                        pe.wait_ge(tvec.sem, tvec.at(0, "idf"))
                        nc.tensor.transpose(misc[:, P:2 * P], ids_f[:], ident[:]).then_inc(ids_ps, 1)
                        nc.tensor.matmul(misc[:, 2 * P:3 * P], eb1_at[32:32 + E], ohT[32:32 + E], start=True,
                                         stop=True).then_inc(bs_ps, 1)

                schedule(q, step, head, lambda s, j: None, lambda: None, tile, late, final=final)
                if q < NQ - 1:
                    pe.wait_ge(rt.sem, rt.at(TB * (q + 1) - 1, "rank"))
                    gate_product(q + 1)

            def routed_T(s, static):
                i = static % 2
                pe.wait_ge(g_in[static % 4], 16 * ((s - static) // 4 + static // 4 + 1))
                need(pe, rxh, s - 1)
                need(pe, rxl, s - 1)
                for k in range(KC):
                    last = nc.tensor.transpose(t_bank[i][:, P * k:P * k + P], xg[:, static % 4, P * k:P * k + P],
                                               ident[:])
                last.then_inc(rT, 1)

            def routed_up(s, static):
                i = static % 2
                pe.wait_ge(rxh, s + 1)
                pe.wait_ge(rxl, s + 1)
                pe.wait_ge(r1hi, s + 1)
                pe.wait_ge(r1lo, s + 1)
                need(pe, rhh, s - 1)
                need(pe, rff, s - 1)
                for k in range(KC):
                    last = splits(r_bank[i][:, 0:P], (e1hi[:, i, k], e1lo[:, i, k]), (xghi[:, i, k], xglo[:, i, k]),
                                  k == 0, k == KC - 1)
                last.then_inc(rup, 1)

            def routed_down(s, static):
                i = static % 2
                e = pe.value_load(rvT[0:1, bass.ds(s, 1)], min_val=0, max_val=E - 1)
                pe.wait_ge(rhh, s + 1)
                pe.wait_ge(rhl, s + 1)
                need(pe, rye[i], y_taken(s, static) - 1)
                splits(y_bank[i][:], (rhi[:, i], rlo[:, i]), (e2hi[:, e], e2lo[:, e]), True, True).then_inc(ry, 1)

            pe.wait_ge(tvec.sem, tvec.at(0))
            pe.wait_ge(h_hi, HOLD)
            pe.wait_ge(h_full, HOLD)
            routed_T(0, 0)
            routed_T(1, 1)
            routed_up(0, 0)
            pe.wait_ge(r2hi, E)
            pe.wait_ge(r2lo, E)
            pe.wait_ge(acc_free, TB * NQ)
            NL = SLOT_TILES // 4 - 1
            for s in range(4):
                routed_T(s + 2, s + 2)
                routed_up(s + 1, s + 1)
                routed_down(s, s)
            with pe.Fori(1, NL) as it:
                for j in range(4):
                    s = 4 * it + j
                    routed_T(s + 2, j + 2)
                    routed_up(s + 1, j + 1)
                    routed_down(s, j)
            for s in range(4 * NL, SLOT_TILES):
                if s + 2 < SLOT_TILES:
                    routed_T(s + 2, s + 2)
                if s + 1 < SLOT_TILES:
                    routed_up(s + 1, s + 1)
                routed_down(s, s)

            up_product(HOLD, HOLD, NQ - 1)
            up_product(HOLD + 1, HOLD + 1, NQ - 1)
            pe.wait_ge(rye[0], SLOT_TILES // 2)
            pe.wait_ge(rye[1], SLOT_TILES // 2)
            last_chunks(step)

        @block.scalar
        def _(act):
            def split_w1(c, static):
                slot = static % RING
                act.wait_ge(w1_in[slot], 16 * uses(c, static))
                need(act, up_done, c - 2)
                nc.scalar.copy(w1hi[:, slot], w1_raw[:, slot]).then_inc(w1_hi, 1)

            class step:
                engine = act

                def __new__(cls, c, static=None):
                    static = c if static is None else static
                    slot, n = static % RING, static % CH
                    cc = c % CH if isinstance(c, int) else c - CH * (static // CH)
                    bias = b1_col[:, bass.ds(cc, 1)]
                    act.wait_ge(b1_ok, 1)
                    act.wait_ge(up_done, c + 1)
                    need(act, down_done, c - 2)
                    nc.scalar.activation(hhi[:, slot], up[slot][:], ACT.Gelu, bias=bias).then_inc(h_hi, 1)
                    act.wait_ge(b1_ok, 1)
                    need(act, h_lo, c - 2)
                    nc.scalar.activation(hf[:, slot], up[slot][:], ACT.Gelu, bias=bias).then_inc(h_full, 1)
                    act.wait_ge(w2_in[slot], 16 * uses(c, static))
                    nc.scalar.copy(w2hi[:, slot], w2_raw[:, slot]).then_inc(w2_hi, 1)
                    if not isinstance(c, int) or c + 3 < HOLD or c >= HOLD and c + 3 < NCH:
                        split_w1(c + 3, static + 3)

            exps = {"b": (pp[:, :, 1:], eb[:, :, 1:], -1.0, "num"), "a": (pp[:, :, 1:], ea[:, :, 1:], 1.0, "nr"),
                    "n": (qq[:, :, 1:], en[:], 1.0, None), "u": (qq[:, :, 1:], eu[:], -1.0, None)}

            def wkv_relu(r, name):
                z, buf, sign, frees = exps[name]
                if name in "ba":
                    act.wait_ge(wz.sem, wz.at(r, "z"))
                else:
                    act.wait_ge(z2_ok, r + 1)
                if not isinstance(r, int) or r:
                    if name in "ba":
                        act.wait_ge(wkv.sem, wkv.at(r - 1, frees))
                    else:
                        act.wait_ge(x2_ok, r)
                nc.scalar.activation(buf, z, ACT.Relu, scale=sign).then_inc(wrelu.sem, 1)

            def wkv_exp(r, name):
                _, buf, _, _ = exps[name]
                act.wait_ge(wrelu.sem, wrelu.at(r, name))
                nc.scalar.activation(buf, buf, ACT.Exp, scale=-1.0).then_inc(wexp.sem, 1)

            def wkv_reciprocal(r):
                act.wait_ge(wkv.sem, wkv.at(r, "den"))
                nc.scalar.activation(en[:], ea[:, :, 1:], ACT.Ln).then_inc(wexp.sem, 1)
                act.wait_ge(wexp.sem, wexp.at(r, "ln"))
                nc.scalar.activation(en[:], en[:], ACT.Exp, scale=-1.0).then_inc(wexp.sem, 1)

            def gate_exp(q):
                act.wait_ge(gsm.sem, gsm.at(q, "sub"))
                nc.scalar.activation(gates[:], gates[:], ACT.Exp).then_inc(gexp, 1)

            def x_hi(t, par, tb, bank):
                act.wait_ge(xT_ps, t + 1)
                nc.scalar.copy(xhi[:, par, :, bass.ds(P * tb, P)],
                               bank[:].rearrange("p (k n) -> p k n", k=KC)).then_inc(xhi_ok, 1)

            def split_e2(part, e):
                act.wait_ge(e2_in[part], 16 * (EH if part == 0 else EH // 2))
                nc.scalar.copy(e2hi[:, e], e2raw[:, e]).then_inc(r2hi, 1)

            def combine_T(t, tb, q):
                act.wait_ge(rank_ps, t + 1)
                need(act, acc_ready, q)
                nc.scalar.copy(cbT[:, tb], misc[0:BR, CBT0:CBT0 + P]).then_inc(cbt_ok, 1)

            nc.scalar.preload_act_table_set("natural_log_exp_and_others")
            act.wait_ge(uw_in, 16 * 2 * GB)
            nc.scalar.copy(wp[:, :, 1:], w_col[:].unsqueeze(2).broadcast_to([P, CB, T])).then_inc(w_ok, 1)
            for c in range(RING):
                split_w1(c, c)
            act.wait_ge(b1_ps, 1)
            nc.scalar.copy(b1_col[:], misc[:, 0:CH]).then_inc(b1_ok, 1)
            act.wait_ge(b1_ok, 1)
            for s in range(2):
                for name in "ba":
                    wkv_relu(s, name)
                    wkv_exp(s, name)
                for name in "nu":
                    wkv_relu(s, name)
                for name in "nu":
                    wkv_exp(s, name)
                wkv_reciprocal(s)
            for tb in range(TB):
                x_hi(tb, 1, tb, acc[tb])

            for q in range(NQ):
                def head(j, q=q):
                    if j == 1:
                        gate_exp(q)

                def half(s, j, q=q):
                    r = 2 * (q + 1) + s
                    if j == 1:
                        wkv_relu(r, "b")
                        wkv_relu(r, "a")
                    if j == 2:
                        wkv_relu(r, "n")
                        wkv_relu(r, "u")
                    if j == 3:
                        nc.scalar.preload_act_table_set("natural_log_exp_and_others")
                        for name in "banu":
                            wkv_exp(r, name)
                    if j == 6:
                        nc.scalar.preload_act_table_set("natural_log_exp_and_others")
                        wkv_reciprocal(r)

                def tile(tb, j, q=q):
                    if j == 1 and q < NQ - 1:
                        if q:
                            act.wait_ge(up_done, CH * q)
                        x_hi(TB * (q + 1) + tb, q % 2, tb, misc)
                    if j == 2:
                        combine_T(TB * q + tb, tb, q)
                    if j < 2 and q == NQ - 1:
                        split_e2(0, 2 * tb + j)

                schedule(q, step, head, half, lambda: None, tile, lambda j: None)

            for part in (1, 2):
                with act.Fori(EH * (part + 1) // 2, EH * (part + 2) // 2) as e:
                    split_e2(part, e)
            act.wait_ge(tvec.sem, tvec.at(0))
            act.wait_ge(ew_in, 16 * E)
            act.wait_ge(down_done, HOLD)
            act.wait_ge(h_lo, HOLD)
            act.wait_ge(w1_lo, HOLD)
            act.wait_ge(w2_lo, HOLD)
            act.wait_ge(w2_hi, HOLD)
            act.wait_ge(h_full, HOLD)

            def routed_w1(s, static):
                e = act.value_load(rvT[0:1, bass.ds(s, 1)], min_val=0, max_val=E - 1)
                need(act, rup, s - 1)
                nc.scalar.copy(e1hi[:, static % 2], ew1_sb[:, e]).then_inc(r1hi, 1)

            def routed_x(s, static):
                i = static % 2
                act.wait_ge(rT, s + 1)
                need(act, rup, s - 1)
                nc.scalar.copy(xghi[:, i], t_bank[i][:].rearrange("p (k n) -> p k n", k=KC)).then_inc(rxh, 1)

            def routed_h(s, static):
                i = static % 2
                b = bslot[:, bass.ds(s, 1)]
                act.wait_ge(tvec.sem, tvec.at(0))
                act.wait_ge(rup, s + 1)
                need(act, ry, s - 1)
                nc.scalar.activation(rhi[:, i], r_bank[i][:, 0:P], ACT.Gelu, bias=b).then_inc(rhh, 1)
                act.wait_ge(tvec.sem, tvec.at(0))
                need(act, rhl, s - 1)
                nc.scalar.activation(rf[:, i], r_bank[i][:, 0:P], ACT.Gelu, bias=b).then_inc(rff, 1)

            def routed_y(s, static):
                n = static % 4
                act.wait_ge(ry, s + 1)
                need(act, yst[n], 16 * ((s - static) // 4 + static // 4))
                nc.scalar.copy(ysb[:, n], y_bank[1][:]).then_inc(rye[1], 1)

            routed_rounds(act, routed_w1, routed_x, routed_h, routed_y, 1)

            act.wait_ge(ry, SLOT_TILES)
            for c in range(HOLD, HOLD + RING):
                split_w1(c, c)
            last_chunks(step)

        @block.vector
        def _(dve):
            V = nc.vector

            def f(ap):
                return ap.bitcast(f32)

            class step:
                engine = dve

                def __new__(cls, c, static=None):
                    static = c if static is None else static
                    slot = static % RING
                    dve.wait_ge(h_hi, c + 1)
                    dve.wait_ge(h_full, c + 1)
                    need(dve, down_done, c - 2)
                    V.tensor_tensor(hlo[:, slot], hf[:, slot], f(hhi[:, slot]), ALU.subtract).then_inc(h_lo, 1)
                    dve.wait_ge(w2_hi, c + 1)
                    dve.wait_ge(w2_in[slot], 16 * uses(c, static))
                    V.tensor_tensor(w2lo[:, slot], w2_raw[:, slot], f(w2hi[:, slot]), ALU.subtract).then_inc(w2_lo, 1)

            def const(ins):
                ins.then_inc(con.sem, 1)

            def after(steps, r, name):
                dve.wait_ge(steps.sem, steps.at(r, name))

            def ln1_stats(q):
                dve.wait_ge(x_in[q], 16 * GB)
                if q:
                    dve.wait_ge(norm, TB * q)
                for tb in range(TB):
                    V.bn_stats(st6[:, tb], X2[:, q, tb]).then_inc(ln1.sem, 1)
                for tb in range(TB):
                    after(ln1, q, f"s{tb}")
                    V.bn_aggr(mv[:, tb], st6[:, tb]).then_inc(ln1.sem, 1)
                after(ln1, q, "a3")
                V.tensor_scalar(veps[:], mv[:, :, 1], EPS, None, ALU.add).then_inc(ln1.sem, 1)

            def ln1_apply(q):
                dve.wait_ge(rstd1, q + 1)
                if q:
                    dve.wait_ge(xn_out, 16 * TB * q)
                    dve.wait_ge(xT_ps, TB * q)
                for tb in range(TB):
                    V.tensor_scalar(kn[:, tb], X2[:, q, tb], mv[:, tb, 0:1], rstd[:, tb:tb + 1],
                                    ALU.subtract, ALU.mult).then_inc(ln1.sem, 1)
                after(ln1, q, "n3")
                V.transpose(kp[:, :, 1:].rearrange("p c (tb t) -> p c tb t", t=TT),
                            kn[:].rearrange("p tb (c k) -> p c tb k", k=32)).then_inc(ln1.sem, 1)

            def v_transpose(q):
                dve.wait_ge(v_in, 16 * GB * (q + 1))
                if q:
                    dve.wait_ge(ev_ok, 2 * q)
                    after(wkv, 2 * q - 1, "bmul")
                V.transpose(vp[:].rearrange("p c (tb t) -> p c tb t", t=TT),
                            vin[:].rearrange("p tb (c k) -> p c tb k", k=32)).then_inc(vT, 1)

            def flat(a):
                return a.rearrange("p c t -> p (c t)")

            m_prev = mx[:, :, 0:T]

            def wkv_scan(q, s):
                cs, r = bass.ds(HC * s, HC), 2 * q + s
                after(ln1, q, "tk")
                if not isinstance(r, int) or r:
                    after(wz, r - 1, "z")
                    dve.wait_ge(z2_ok, r)
                V.tensor_tensor_scan(flat(mx[:]), flat(wp[:, cs, :]), flat(kp[:, cs, :]), 0.0,
                                     ALU.add, ALU.max).then_inc(wscan, 1)

            def wkv_z(q, s):
                cs, r = bass.ds(HC * s, HC), 2 * q + s
                dve.wait_ge(wscan, r + 1)
                if isinstance(r, int) and r == 1:
                    after(wkv, 0, "den")
                    dve.wait_ge(ev_ok, 1)
                elif not isinstance(r, int) or r:
                    dve.wait_ge(ty, r)
                V.tensor_tensor(eu[:], wp[:, cs, 1:], m_prev, ALU.add).then_inc(wz.sem, 1)
                after(wz, r, "wm")
                V.tensor_tensor(pp[:, :, 1:], kp[:, cs, 1:], eu[:], ALU.subtract).then_inc(wz.sem, 1)

            def wkv_part(q, s, part):
                r = 2 * q + s
                cs = bass.ds(HC * s, HC)
                v_h = vp[:, cs, :]
                p_prev, q_prev = pp[:, :, 0:T], qq[:, :, 0:T]

                def do(ins):
                    ins.then_inc(wkv.sem, 1)

                if part == 0:
                    wkv_scan(q, s)
                    wkv_z(q, s)
                elif part == 4:
                    dve.wait_ge(vT, q + 1)
                    if not isinstance(r, int) or r:
                        after(wkv, r - 1, "y")
                    after(wexp, r, "b")
                    do(V.tensor_tensor(bv[:, :, 1:], eb[:, :, 1:], v_h, ALU.mult))
                    after(wexp, r, "a")
                    after(wkv, r, "bmul")
                    do(V.tensor_tensor_scan(flat(pp[:]), flat(ea[:]), flat(bv[:]), 0.0, ALU.mult, ALU.add))
                    after(wrelu, r, "u")
                    do(V.tensor_tensor_scan(flat(qq[:]), flat(ea[:]), flat(eb[:]), 0.0, ALU.mult, ALU.add))
                elif part == 5:
                    after(wkv, r, "sq")
                    after(wexp, r, "n")
                    do(V.tensor_tensor(ea[:, :, 1:], en[:], q_prev, ALU.mult))
                    do(V.tensor_tensor(bv[:, :, 1:], en[:], p_prev, ALU.mult))
                    after(wexp, r, "u")
                    after(wkv, r, "ap")
                    do(V.tensor_tensor(ea[:, :, 1:], ea[:, :, 1:], eu[:], ALU.add))
                elif part == 6:
                    dve.wait_ge(ev_ok, r + 1)
                    do(V.tensor_tensor(bv[:, :, 1:], bv[:, :, 1:], eb[:, :, 1:], ALU.add))
                elif part == 7:
                    after(wexp, r, "rec")
                    do(V.tensor_tensor(ea[:, :, 1:], ea[:, :, 1:], en[:], ALU.mult))
                    after(wkv, r, "nt")
                    do(V.scalar_tensor_tensor(out=en[:], in0=ea[:, :, 1:], scalar=-2.0, in1=en[:],
                                              op0=ALU.add, op1=ALU.mult))
                    after(wkv, r, "nr")
                    do(V.scalar_tensor_tensor(out=eu[:], in0=en[:], scalar=-1.0, in1=bv[:, :, 1:],
                                              op0=ALU.mult, op1=ALU.mult))
                elif part == 8:
                    wkv_back(q, s)

            def wkv_back(q, s):
                r = 2 * q + s
                after(wkv, r, "y")
                cols = bass.ds(32 * HC * s, 32 * HC)
                V.transpose(yT.rearrange("p tb (c k) -> p tb c k", k=32),
                            eu[:].rearrange("p c (tb t) -> p tb c t", t=TT)).then_inc(ty, 1)
                dve.wait_ge(ty, r + 1)
                V.tensor_tensor(X2[:, q, :, cols], X2[:, q, :, cols], yT, ALU.add)\
                    .then_inc(x2_ok, 1)

            def ln2_quad(q):
                dve.wait_ge(x2_ok, 2 * (q + 1))
                after(ln1, q, "n3")
                for tb in range(TB):
                    V.bn_stats(st6[:, tb], X2[:, q, tb]).then_inc(ln2.sem, 1)
                for tb in range(TB):
                    after(ln2, q, f"s{tb}")
                    V.bn_aggr(mv[:, tb], st6[:, tb]).then_inc(ln2.sem, 1)
                after(ln2, q, "a3")
                V.tensor_scalar(veps[:], mv[:, :, 1], EPS, None, ALU.add).then_inc(ln2.sem, 1)

            def ln2_apply(q, tb, t, rows):
                dve.wait_ge(rstd2, q + 1)
                if q:
                    dve.wait_ge(xn_out, 16 * t)
                    dve.wait_ge(xT_ps, t)
                V.tensor_scalar(rows, X2[:, q, tb], mv[:, tb, 0:1],
                                rstd[:, bass.ds(tb, 1)], ALU.subtract, ALU.mult).then_inc(norm, 1)

            def x_lo(tb, par, t, bank):
                dve.wait_ge(xhi_ok, t + 1)
                tok = bass.ds(P * tb, P)
                V.tensor_tensor(xlo[:, par, :, tok], bank[:].rearrange("p (k n) -> p k n", k=KC),
                                f(xhi[:, par, :, tok]), ALU.subtract).then_inc(xlo_ok, 1)

            def spread(col):
                return col.unsqueeze(2).broadcast_to([P, TB, E])

            def gate_parts(q):
                dve.wait_ge(gate_ps, q + 1)
                V.tensor_copy(lgT[:], misc[0:64]).then_inc(gsm.sem, 1)

            def gates_max(q):
                dve.wait_ge(lg_ps, q + 1)
                V.tensor_tensor(logits[:], misc[:, 0:TB * E].rearrange("p (t e) -> p t e", e=E),
                                gb_b[:].unsqueeze(1).broadcast_to([P, TB, E]), ALU.add).then_inc(gsm.sem, 1)
                after(gsm, q, "lg")
                V.tensor_reduce(gmax[:], logits[:], AX.X, ALU.max).then_inc(gsm.sem, 1)
                after(gsm, q, "max")
                V.tensor_tensor(gates[:], logits[:], spread(gmax[:]), ALU.subtract).then_inc(gsm.sem, 1)

            def gates_norm(q):
                dve.wait_ge(gexp, q + 1)
                V.tensor_reduce(gsum[:], gates[:], AX.X, ALU.add).then_inc(gsm.sem, 1)
                after(gsm, q, "sum")
                V.reciprocal(grec[:], gsum[:]).then_inc(gsm.sem, 1)
                after(gsm, q, "rec")
                V.tensor_tensor(gates[:], gates[:], spread(grec[:]), ALU.mult).then_inc(gsm.sem, 1)

            def rdo(ins):
                ins.then_inc(rt.sem, 1)

            def route_pick(q, tb, t):
                after(gsm, q, "gates")
                if not isinstance(t, int) or t:
                    dve.wait_ge(rank_ps, t)
                rdo(V.tensor_copy(gt[:], gates[:, tb]))
                after(rt, t, "gt")
                apart(dve)
                rdo(V.max(top8[:], gt[:]))
                after(rt, t, "max")
                apart(dve)
                rdo(V.max_index(idx8[:], top8[:], gt[:]))
                after(rt, t, "idx")
                rdo(V.tensor_copy(idxf[:], idx8[:, 0:2]))
                rdo(V.tensor_copy(c_all[:, t] if isinstance(t, int) else c_all[:, t, :], top8[:, 0:2]))
                after(rt, t, "idxf")
                rdo(V.tensor_copy(e_all[:, t] if isinstance(t, int) else e_all[:, t, :], idxf[:]))
                for j in range(2):
                    rdo(V.tensor_scalar(oh[:, j], iota_e[:], idxf[:, j:j + 1], None, ALU.is_equal))
                after(rt, t, "o2")
                rdo(V.tensor_tensor(member[:], oh[:, 0], oh[:, 1], ALU.add))
                rdo(V.tensor_scalar(comb2[:], oh[:, 0], top8[:, 0:1], None, ALU.mult))

            def route_combine(t):
                after(rt, t, "wc")
                rdo(V.scalar_tensor_tensor(out=comb[:], in0=oh[:, 1], scalar=top8[:, 1:2], in1=comb2[:],
                                           op0=ALU.mult, op1=ALU.add))
                after(rt, t, "comb")
                rdo(V.tensor_copy(chi[:], comb[:]))
                after(rt, t, "hi")
                rdo(V.tensor_copy(cb96[:, 0:E], f(chi[:])))
                rdo(V.tensor_copy(cb96[:, 32:32 + E], f(chi[:])))
                rdo(V.tensor_tensor(cb96[:, 64:64 + E], comb[:], f(chi[:]), ALU.subtract))

            def route_place(t):
                dve.wait_ge(rank_ps, t + 1)
                dve.wait_ge(cbt_ok, t + 1)
                rdo(V.tensor_tensor(rb[:], misc[:, RANK0:RANK0 + E], ebase[:], ALU.add))
                after(rt, t, "rank")
                for j in range(2):
                    rdo(V.tensor_tensor(rsel[:, j], oh[:, j], rb[:], ALU.mult))
                after(rt, t, "m2")
                rdo(V.tensor_reduce(posf[:], rsel[:], AX.X, ALU.add))
                after(rt, t, "pos")
                need(dve, scat, 32 * t)
                rdo(V.tensor_copy(pos_stage[:], posf[:]))
                rdo(V.tensor_copy(pos_all[:, t] if isinstance(t, int) else pos_all[:, t, :], posf[:]))
                rdo(V.tensor_tensor(msum[:], msum[:], member[:], ALU.add))

            def split_e2(e):
                dve.wait_ge(r2hi, e + 1)
                V.tensor_tensor(e2lo[:, e], e2raw[:, e], f(e2hi[:, e]), ALU.subtract).then_inc(r2lo, 1)

            def take_block(q, part=False):
                if part:
                    dve.wait_ge(down_done, HOLD)
                else:
                    dve.wait_ge(acc_ready, q + 1)
                for t in range(TB):
                    V.tensor_tensor(X2[:, q, t], X2[:, q, t], acc[t][:], ALU.add).then_inc(acc_free, 1)

            const(V.memset(kp[:, :, 0:1], NEG))
            const(V.memset(wp[:, :, 0:1], NEG))
            const(V.memset(ea[:, :, 0:1], 0.0))
            const(V.memset(eb[:, :, 0:1], 0.0))
            const(V.memset(bv[:, :, 0:1], 0.0))
            const(V.memset(neg_half[:], -0.5))
            const(V.memset(bias_f[:], 0.0))
            const(V.memset(msum[:], 0.0))
            const(V.memset(ones_bf[:], 1.0))
            const(V.memset(ones16[:], 1.0))
            const(V.memset(cb96[:], 0.0))
            after(con, 0, "cb0")
            const(V.memset(cb96[:, E:E + S_EXP], 1.0))
            const(V.memset(cb96[:, 32 + E:32 + E + S_EXP], 1.0))
            const(V.memset(f(gw2[:]), 0.0))
            ln1_stats(0)
            ln1_apply(0)
            dve.wait_ge(pcon.sem, pcon.at(0))
            after(con, 0, "gz")
            dve.wait_ge(w_ok, 1)
            wkv_scan(0, 0)
            wkv_z(0, 0)
            v_transpose(0)
            wkv_scan(0, 1)
            for part in (4, 5, 6):
                wkv_part(0, 0, part)
            wkv_z(0, 1)
            after(wz, 1, "z")
            wkv_part(0, 0, 7)
            wkv_back(0, 0)
            for part in (4, 5, 6):
                wkv_part(0, 1, part)
            dve.wait_ge(c_in, 16 * 10)
            after(con, 0, "gz")
            const(V.tensor_copy(gw2[:, :, 0:E], gw_f[:]))
            after(con, 0, "ghi")
            const(V.tensor_tensor(gw2[:, :, 32:32 + E], gw_f[:], f(gw2[:, :, 0:E]), ALU.subtract))
            wkv_part(0, 1, 7)
            wkv_back(0, 1)
            ln2_quad(0)
            for tb in range(TB):
                ln2_apply(0, tb, tb, xn[:, tb])
            for tb in range(TB):
                x_lo(tb, 1, tb, acc[tb])
            const(V.tensor_copy(bias_r[0:32], bias_f[0:32]))
            const(V.tensor_copy(bias_r[64:96], bias_f[64:96]))
            const(V.tensor_copy(bias_r[32:64], bias_f[32:64]))
            after(con, 0, "blo")
            const(V.tensor_tensor(bias_r[32:64], bias_f[32:64], f(bias_r[32:64]), ALU.subtract))
            after(con, 0, None)

            for q in range(NQ):
                def head(j, q=q):
                    if j == 0:
                        gate_parts(q)
                        if q:
                            take_block(q - 1)
                        if q == 0:
                            v_transpose(1)
                            ln1_stats(1)
                    else:
                        gates_max(q)
                        if q < NQ - 1:
                            ln1_apply(q + 1)
                        else:
                            gates_norm(q)

                def mid(q=q):
                    gates_norm(q)
                    ln2_quad(q + 1)

                def half(s, j, q=q):
                    wkv_part(q + 1, s, j)

                def tile(tb, j, q=q):
                    t = TB * q + tb
                    if j == 0:
                        if q < NQ - 1:
                            ln2_apply(q + 1, tb, t + TB, xt)
                        route_pick(q, tb, t)
                    if j == 1:
                        route_combine(t)
                        if q < NQ - 1:
                            if q:
                                dve.wait_ge(up_done, CH * q)
                            x_lo(tb, q % 2, t + TB, misc)
                    if j < 2 and q == NQ - 1:
                        split_e2(2 * tb + j)
                    if j == 2:
                        route_place(t)
                    if isinstance(tb, int) and tb == TB - 1 and q + 2 < NQ:
                        if j == 1:
                            v_transpose(q + 2)
                        if j == 2:
                            ln1_stats(q + 2)

                def late(j):
                    if j == 1:
                        slots()

                def cdo(ins):
                    ins.then_inc(cph.sem, 1)

                def slots():
                    dve.wait_ge(cnt_ps, 1)
                    dve.wait_ge(cz, 2)
                    cdo(V.tensor_copy(cnt[:], misc[:, 0:E]))
                    after(cph, 0, "cnt")
                    cdo(V.tensor_tensor(cmp[:], cnt[:].unsqueeze(2).broadcast_to([P, E, TPE]),
                                        thr[:].unsqueeze(1).broadcast_to([P, E, TPE]), ALU.is_gt))
                    after(cph, 0, "cmp")
                    cdo(V.tensor_reduce(nt[:], cmp[:], AX.X, ALU.add))
                    after(cph, 0, "nt")
                    cdo(V.tensor_tensor_scan(tend[:], ones16[:], nt[:], 0.0, ALU.mult, ALU.add))
                    after(cph, 0, "tend")
                    cdo(V.tensor_scalar(fin_e[:], tend[:], iota_p[:], None, ALU.is_le))
                    cdo(V.tensor_tensor(move[:], tend[:], nt[:], ALU.subtract))
                    after(cph, 0, "etile")
                    cdo(V.scalar_tensor_tensor(out=move[:], in0=move[:], scalar=float(P), in1=ebase[:],
                                               op0=ALU.mult, op1=ALU.subtract))
                    cdo(V.tensor_reduce(e_s[:], fin_e[:], AX.X, ALU.add))
                    cdo(V.tensor_tensor(fin_n[:], fin_e[:], nt[:], ALU.mult))
                    after(cph, 0, "ctiles")
                    cdo(V.tensor_reduce(ts[:], fin_n[:], AX.X, ALU.add))
                    cdo(V.scalar_tensor_tensor(out=trow[:], in0=e_s[:], scalar=float(TPE), in1=iota_p[:],
                                               op0=ALU.mult, op1=ALU.add))
                    cdo(V.tensor_scalar(rv[:, 0:1], e_s[:], float(E - 1), None, ALU.min))
                    after(rt, NT - 1, None)
                    cdo(V.tensor_tensor(pick[:], e_all[:].rearrange("p n j -> p (n j)").unsqueeze(2)
                                        .broadcast_to([P, NT * 2, E]),
                                        iota_e[:].unsqueeze(1).broadcast_to([P, NT * 2, E]), ALU.is_equal))
                    after(cph, 0, "eq")
                    cdo(V.tensor_tensor(trow[:], trow[:], ts[:], ALU.subtract))
                    cdo(V.tensor_scalar(rv[:, 32:32 + E], iota_e[:], rv[:, 0:1], None, ALU.is_equal))
                    after(cph, 0, "trow")
                    cdo(V.tensor_copy(trow_i[:], trow[:]))
                    cdo(V.tensor_tensor(pick[:], pick[:], move[:].unsqueeze(1).broadcast_to([P, NT * 2, E]),
                                        ALU.mult))
                    after(cph, 0, "mul")
                    cdo(V.tensor_reduce(moved[:], pick[:], AX.X, ALU.add))
                    after(cph, 0, "shift")
                    cdo(V.tensor_tensor(row_all[:], pos_all[:], moved[:].rearrange("p (n j) -> p n j", j=2),
                                        ALU.add))

                def final(j):
                    if j == 0:
                        dve.wait_ge(rv_ps, 1)
                        V.tensor_copy(rvT[:], misc[0:1, 0:P]).then_inc(tvec.sem, 1)
                        V.tensor_copy(ohT[32:32 + E], misc[32:32 + E, 0:P]).then_inc(tvec.sem, 1)
                        dve.wait_ge(tab_in, 16)
                        V.tensor_copy(ids_f[0:SLOT_TILES], ids_i[0:SLOT_TILES]).then_inc(tvec.sem, 1)
                    if j == 1:
                        dve.wait_ge(ids_ps, 1)
                        dve.wait_ge(bs_ps, 1)
                        V.tensor_copy(xrow[:], misc[:, P:P + NS]).then_inc(tvec.sem, 1)
                        V.tensor_copy(bslot[:], misc[:, 2 * P:2 * P + NS]).then_inc(tvec.sem, 1)
                        after(tvec, 0, "xrow")
                        V.tensor_copy(idx[:], xrow[:, 0:4]).then_inc(idx_ok, 1)

                schedule(q, step, head, half, mid, tile, late, final)

            with dve.Fori(EH, E) as e:
                split_e2(e)
            after(tvec, 0, None)
            dve.wait_ge(ew_in, 16 * E)
            dve.wait_ge(down_done, HOLD)
            dve.wait_ge(w1_lo, HOLD)
            dve.wait_ge(w2_lo, HOLD)
            dve.wait_ge(h_lo, HOLD)


            def routed_w1(s, static):
                i = static % 2
                e = dve.value_load(rvT[0:1, bass.ds(s, 1)], min_val=0, max_val=E - 1)
                dve.wait_ge(r1hi, s + 1)
                need(dve, rup, s - 1)
                V.tensor_tensor(e1lo[:, i], ew1_sb[:, e], f(e1hi[:, i]), ALU.subtract).then_inc(r1lo, 1)

            def routed_x(s, static):
                i = static % 2
                dve.wait_ge(rxh, s + 1)
                need(dve, rup, s - 1)
                V.tensor_tensor(xglo[:, i], t_bank[i][:].rearrange("p (k n) -> p k n", k=KC), f(xghi[:, i]),
                                ALU.subtract).then_inc(rxl, 1)
                n = static % 4
                V.tensor_copy(idx[:, n:n + 1], xrow[:, bass.ds(s + 4, 1)]).then_inc(idx_ok, 1)

            def routed_h(s, static):
                i = static % 2
                dve.wait_ge(rhh, s + 1)
                dve.wait_ge(rff, s + 1)
                need(dve, ry, s - 1)
                V.tensor_tensor(rlo[:, i], rf[:, i], f(rhi[:, i]), ALU.subtract).then_inc(rhl, 1)

            def routed_y(s, static):
                n = static % 4
                dve.wait_ge(ry, s + 1)
                need(dve, yst[n], 16 * ((s - static) // 4 + static // 4))
                V.tensor_copy(ysb[:, n], y_bank[0][:]).then_inc(rye[0], 1)

            routed_rounds(dve, routed_w1, routed_x, routed_h, routed_y, 0, lambda: take_block(NQ - 1, True))

            def split_w1(c):
                slot = c % RING
                dve.wait_ge(w1_in[slot], 16 * uses(c, c))
                need(dve, up_done, c - 2)
                dve.wait_ge(w1_hi, c + 1)
                V.tensor_tensor(w1lo[:, slot], w1_raw[:, slot], f(w1hi[:, slot]), ALU.subtract).then_inc(w1_lo, 1)

            def tail(k):
                if HOLD + k + 3 < NCH:
                    split_w1(HOLD + k + 3)
                if 2 <= k < 2 + 2 * NQ:
                    q, j = divmod(k - 2, 2)
                    dve.wait_ge(yg_in[q][j], 16 * TB)
                    if j == 0 and q == NQ - 1:
                        dve.wait_ge(acc_free, TB * NQ)
                    for tb in range(TB):
                        t = TB * q + tb
                        if j:
                            dve.wait_ge(comb1, t + 1)
                        V.scalar_tensor_tensor(out=X2[:, q, tb], in0=yg[:, q, j, tb], scalar=c_all[:, t, j:j + 1],
                                               in1=X2[:, q, tb], op0=ALU.mult, op1=ALU.add)\
                            .then_inc(comb2s if j else comb1, 1)

            dve.wait_ge(ry, SLOT_TILES)
            for c in range(HOLD, HOLD + RING):
                split_w1(c)
            last_chunks(step, tail)
            dve.wait_ge(comb2s, TB * NQ)
            take_block(NQ - 1)

        @block.gpsimd
        def _(pool):
            G = nc.gpsimd

            def const(ins):
                ins.then_inc(pcon.sem, 1)

            const(G.memset(ident[:], 0.0))
            const(G.memset(tri[:], 1.0))
            const(G.memset(sel[:], 0.0))
            pool.wait_ge(pcon.sem, pcon.at(0, "sel0"))
            const(G.affine_select(out=ident[:], in_=ident[:], compare_op=ALU.not_equal, fill=1.0, base=0,
                                  pattern=[[-1, P]], channel_multiplier=1))
            const(G.affine_select(out=tri[:], in_=tri[:], compare_op=ALU.is_gt, fill=0.0, base=0,
                                  pattern=[[1, P]], channel_multiplier=-1))
            const(G.affine_select(out=sel[:], in_=sel[:], compare_op=ALU.not_equal, fill=1.0, base=0,
                                  pattern=[[-1, E]], channel_multiplier=1))
            pool.wait_ge(pcon.sem, pcon.at(0, "sela"))
            const(G.affine_select(out=sel[:], in_=sel[:], compare_op=ALU.not_equal, fill=1.0, base=-32,
                                  pattern=[[-1, E]], channel_multiplier=1))
            const(G.iota(iota_e[:], [[1, E]], base=0, channel_multiplier=0, allow_small_or_imprecise_dtypes=True))
            const(G.iota(ebase[:], [[NTOK, E]], base=0, channel_multiplier=0, allow_small_or_imprecise_dtypes=True))
            const(G.iota(thr[:], [[P, TPE]], base=0, channel_multiplier=0, allow_small_or_imprecise_dtypes=True))
            const(G.iota(iota_p[:], [[0, 1]], base=0, channel_multiplier=1, allow_small_or_imprecise_dtypes=True))
            const(G.iota(tokid[:], [[P, NT]], base=0, channel_multiplier=1))
            const(G.memset(tok_stage[:], 0))
            const(G.memset(zero_i[:], 0))
            pool.wait_ge(pcon.sem, pcon.at(0))
            pool.dma_start(table_dram.rearrange("(p n) o -> p (n o)", p=P), zero_i[:]).then_inc(tz, 16)

            def split_w1(c, static):
                slot = static % RING
                pool.wait_ge(w1_in[slot], 16 * uses(c, static))
                need(pool, up_done, c - 2)
                pool.wait_ge(w1_hi, c + 1)
                G.tensor_tensor(w1lo[:, slot], w1_raw[:, slot], w1hi[:, slot].bitcast(f32), ALU.subtract)\
                    .then_inc(w1_lo, 1)

            class step:
                engine = pool

                def __new__(cls, c, static=None):
                    static = c if static is None else static
                    if not isinstance(c, int) or c + 3 < HOLD:
                        split_w1(c + 3, static + 3)

            def rstd_quad(q):
                pool.wait_ge(ln1.sem, ln1.at(q, "veps"))
                G.tensor_tensor(rstd[:], veps[:], neg_half[:], ALU.pow).then_inc(rstd1, 1)

            def rstd_quad2(q):
                pool.wait_ge(ln2.sem, ln2.at(q, "veps"))
                G.tensor_tensor(rstd[:], veps[:], neg_half[:], ALU.pow).then_inc(rstd2, 1)

            def key_plus_bonus(q):
                pool.wait_ge(uw_in, 16 * 2 * GB)
                pool.wait_ge(ln1.sem, ln1.at(q, "tk"))
                for s in range(2):
                    cs = bass.ds(HC * s, HC)
                    G.tensor_tensor(ku_sum[:, cs, :], kp[:, cs, 1:], u_col[:, cs].unsqueeze(2).broadcast_to([P, HC, T]),
                                    ALU.add).then_inc(ku, 1)

            def wkv_z2(q, s):
                cs, r = bass.ds(HC * s, HC), 2 * q + s
                pool.wait_ge(ku, 2 * (q + 1))
                if not isinstance(r, int) or r:
                    pool.wait_ge(wkv.sem, wkv.at(r - 1, "aq"))
                pool.wait_ge(wscan, r + 1)
                G.tensor_tensor(qq[:, :, 1:], ku_sum[:, cs, :], mx[:, :, 0:T], ALU.subtract).then_inc(z2_ok, 1)

            def wkv_ev(q, s):
                cs, r = bass.ds(HC * s, HC), 2 * q + s
                pool.wait_ge(vT, q + 1)
                pool.wait_ge(wkv.sem, wkv.at(r, "sq"))
                pool.wait_ge(wexp.sem, wexp.at(r, "u"))
                G.tensor_tensor(eb[:, :, 1:], eu[:], vp[:, cs, :], ALU.mult).then_inc(ev_ok, 1)

            def store_rows(t, rows):
                pool.wait_ge(norm, t + 1)
                pool.dma_start(xn_tiles[t], rows).then_inc(xn_out, 16)

            def scatter(t):
                need(pool, scat, 32 * t)
                G.tensor_copy(tok_stage[:], tokid[:, bass.ds(t, 1)]).then_inc(pst, 1)
                pool.wait_ge(pst, t + 1)
                pool.wait_ge(rt.sem, rt.at(t, "pint"))
                apart(pool)
                pool.indirect_dma_start(out=table_dram[:, :], out_offset=bass.IndirectOffsetOnAxis(
                    ap=pos_stage[:, 0:1], axis=0), in_=tok_stage[:], in_offset=None).then_inc(scat, 16)
                pool.indirect_dma_start(out=table_dram[:, :], out_offset=bass.IndirectOffsetOnAxis(
                    ap=pos_stage[:, 1:2], axis=0), in_=tok_stage[:], in_offset=None).then_inc(scat, 16)

            pool.wait_ge(con.sem, con.at(0, "half"))
            rstd_quad(0)
            key_plus_bonus(0)
            wkv_z2(0, 0)
            for c in range(RING):
                split_w1(c, c)
            wkv_ev(0, 0)
            wkv_z2(0, 1)
            wkv_ev(0, 1)
            rstd_quad2(0)
            for tb in range(TB):
                store_rows(tb, xn[:, tb])
            pool.wait_ge(tz, 16)
            for q in range(NQ):
                def head(j, q=q):
                    if q < NQ - 1:
                        if j == 0:
                            rstd_quad(q + 1)
                        else:
                            key_plus_bonus(q + 1)
                    elif j == 0:
                        pool.wait_ge(xT_ps, NT)
                        pool.wait_ge(xn_out, 16 * NT)
                        G.memset(rv[:], 0.0).then_inc(cz, 1)
                        G.memset(ids_f[:], 0.0).then_inc(cz, 1)

                def mid(q=q):
                    rstd_quad2(q + 1)

                def tile(tb, j, q=q):
                    if j == 0 and q < NQ - 1:
                        store_rows(TB * (q + 1) + tb, xt)
                    if j == 2:
                        scatter(TB * q + tb)

                def late(j):
                    if j == 2:
                        pool.wait_ge(cph.sem, cph.at(0))
                        pool.wait_ge(scat, 32 * NT)
                        pool.indirect_dma_start(out=ids_i[0:SLOT_TILES, :], out_offset=None, in_=table_rows[:, :],
                                                in_offset=bass.IndirectOffsetOnAxis(
                                                    ap=trow_i[0:SLOT_TILES, 0:1], axis=0)).then_inc(tab_in, 16)

                def half(s, j, q=q):
                    if j == 0:
                        wkv_z2(q + 1, s)
                    if j == 5:
                        wkv_ev(q + 1, s)

                schedule(q, step, head, half, mid, tile, late)

            pool.wait_ge(tvec.sem, tvec.at(0))

            def gather(s, static):
                n = static % 4
                need(pool, rT, s - 3)
                pool.wait_ge(idx_ok, 1 if isinstance(s, int) and s < 4 else s - 2)
                apart(pool)
                pool.indirect_dma_start(out=xg[:, n], out_offset=None, in_=xn_dram[:, :],
                                        in_offset=bass.IndirectOffsetOnAxis(ap=idx[:, n:n + 1], axis=0))\
                    .then_inc(g_in[n], 16)

            for s in range(8):
                gather(s, s)
            with pool.Fori(2, SLOT_TILES // 4) as i:
                for j in range(4):
                    gather(4 * i + j, j)

            for n in range(4):
                pool.wait_ge(yst[n], 16 * (SLOT_TILES // 4))
            pool.wait_ge(ry, SLOT_TILES)

            def tail(k):
                if k < 2 * NQ:
                    q, j = divmod(k, 2)
                    for tb in range(TB):
                        pool.indirect_dma_start(out=yg[:, q, j, tb], out_offset=None, in_=y_dram[:, :],
                                                in_offset=bass.IndirectOffsetOnAxis(
                                                    ap=row_all[:, TB * q + tb, j:j + 1], axis=0))\
                            .then_inc(yg_in[q][j], 16)

            for k in range(2 * NQ):
                tail(k)


_INS = ["x", "ctx_2048", "L0_xattn_w", "L0_xattn_u", "L0_ffn_gate_w", "L0_ffn_gate_b", "L0_ffn_ew1", "L0_ffn_eb1",
        "L0_ffn_ew2", "L0_ffn_eb2", "L0_ffn_sw1", "L0_ffn_sb1", "L0_ffn_sw2", "L0_ffn_sb2"]


def kernel(**inputs):
    import numpy as np
    import concourse.bacc as bacc
    from concourse import mybir as mb
    from concourse.bass_utils import run_bass_kernel_spmd

    nc = bacc.Bacc("TRN2", target_bir_lowering=False, num_devices=1)
    arrays, args = {}, []
    for name in _INS:
        a = np.ascontiguousarray(inputs[name])
        arrays[f"in_{name}"] = a
        args.append(nc.dram_tensor(f"in_{name}", a.shape, mb.dt.from_np(a.dtype), kind="ExternalInput").ap())
    shape = arrays["in_x"].shape
    args.append(nc.dram_tensor("out_0", shape, mb.dt.float32, kind="ExternalOutput").ap())
    with nc.allow_non_contiguous_dma(reason="small per-channel vectors go to columns"):
        mixed_layer(nc, *args)
    r = run_bass_kernel_spmd(nc, [arrays], core_ids=[0])
    return r.results[0]["out_0"]
```
